# Optimizing a Trainium2 kernel written in Bass

```python
import numpy as np
import jax
import jax.numpy as jnp

def _softmax(x, axis=-1):
    return jax.nn.softmax(x, axis=axis)

def _gelu(x):
    return jax.nn.gelu(x, approximate=True)

def _silu(x):
    return jax.nn.silu(x)

def _sigmoid(x):
    return jax.nn.sigmoid(x)

def _layernorm(x, axis=-1, eps=1e-05):
    m = jnp.mean(x, axis=axis, keepdims=True)
    v = jnp.var(x, axis=axis, keepdims=True)
    return (x - m) / jnp.sqrt(v + eps)

def _scatter_add(tgt, idx, src, axis=0):
    return tgt.at[idx].add(src)

def _segment_sum(src, seg, n):
    return jax.ops.segment_sum(src, seg, n)
kernel_name = 'mk_adaln_d2_jaxref_r8_11a548'

def setup_inputs(seed: int=0):
    np.random.seed(seed)
    _w = jnp.asarray

    def _L0_attn_setup():
        import jax, jax.numpy as jnp
        import numpy as np
        B, N, D, H = (2, 256, 128, 16)
        HD = D // H
        SCALING = (D / H) ** 0.5
        EPS = 1e-05
        key = jax.random.key(seed)
        k1, k2, k3 = jax.random.split(key, 3)
        return {'z': jax.random.normal(k1, (B, N, D), dtype=jnp.float32), 'ln_scale': jnp.ones((D,), dtype=jnp.float32), 'ln_bias': jnp.zeros((D,), dtype=jnp.float32), 'w_qkv': jax.random.normal(k2, (D, 3 * D), dtype=jnp.float32) * D ** (-0.5), 'w_proj': jax.random.normal(k3, (D, D), dtype=jnp.float32) * D ** (-0.5), 'b_proj': jnp.zeros((D,), dtype=jnp.float32)}
    _L0_attn_in = _L0_attn_setup()

    def _L0_ffn_setup():
        import jax, jax.numpy as jnp
        import numpy as np
        N_HEAD, N_ACTIVE, D_MODEL, D_ATTN = (16, 4, 128, 64)
        key = jax.random.key(seed)
        ks = jax.random.split(key, 12)
        s = 0.02
        B, S = (2, 512)
        return {'x': jax.random.normal(ks[0], (B, S, D_MODEL), dtype=jnp.float32), 'Wq': jax.random.normal(ks[1], (D_MODEL, N_HEAD * D_ATTN), dtype=jnp.float32) * s, 'bq': jnp.zeros((N_HEAD * D_ATTN,), dtype=jnp.float32), 'Wk': jax.random.normal(ks[2], (D_MODEL, N_HEAD * D_ATTN), dtype=jnp.float32) * s, 'bk': jnp.zeros((N_HEAD * D_ATTN,), dtype=jnp.float32), 'Wv': jax.random.normal(ks[3], (D_MODEL, N_HEAD * D_ATTN), dtype=jnp.float32) * s, 'bv': jnp.zeros((N_HEAD * D_ATTN,), dtype=jnp.float32), 'Wr': jax.random.normal(ks[4], (D_MODEL, N_HEAD), dtype=jnp.float32) * s, 'br': jnp.zeros((N_HEAD,), dtype=jnp.float32), 'Wo': jax.random.normal(ks[5], (N_ACTIVE * D_ATTN, D_MODEL), dtype=jnp.float32) * s, 'bo': jnp.zeros((D_MODEL,), dtype=jnp.float32)}
    _L0_ffn_in = _L0_ffn_setup()
    _L0_c = _w((lambda *s: np.random.randn(*s).astype(np.float32) * 0.05)(16, 128))
    _L0_wmod = _w((lambda *s: np.random.randn(*s).astype(np.float32) * 0.05)(128, 6 * 128) * 128 ** (-0.5))

    def _L1_attn_setup():
        import jax, jax.numpy as jnp
        import numpy as np
        D_MODEL = 128
        N_HEADS = 16
        D_HEAD = D_MODEL // N_HEADS
        EPS = 1e-06
        B, N = (1, 256)

        def _phi(x):
            return jax.nn.elu(x) + 1.0

        def _split_heads(y, b, n):
            return y.reshape(b, n, N_HEADS, D_HEAD).transpose(0, 2, 1, 3)
        key = jax.random.key(seed)
        ks = jax.random.split(key, 10)
        s = 1.0 / np.sqrt(D_MODEL)
        return {'x': jax.random.normal(ks[0], (B, N, D_MODEL), dtype=jnp.float32), 'mask': jnp.tril(jnp.ones((N, N), dtype=bool)), 'Wq': jax.random.normal(ks[1], (D_MODEL, D_MODEL), dtype=jnp.float32) * s, 'bq': jax.random.normal(ks[2], (D_MODEL,), dtype=jnp.float32) * s, 'Wk': jax.random.normal(ks[3], (D_MODEL, D_MODEL), dtype=jnp.float32) * s, 'bk': jax.random.normal(ks[4], (D_MODEL,), dtype=jnp.float32) * s, 'Wv': jax.random.normal(ks[5], (D_MODEL, D_MODEL), dtype=jnp.float32) * s, 'bv': jax.random.normal(ks[6], (D_MODEL,), dtype=jnp.float32) * s, 'Wo': jax.random.normal(ks[7], (D_MODEL, D_MODEL), dtype=jnp.float32) * s, 'bo': jax.random.normal(ks[8], (D_MODEL,), dtype=jnp.float32) * s}
    _L1_attn_in = _L1_attn_setup()

    def _L1_ffn_setup():
        import jax, jax.numpy as jnp
        import numpy as np
        DIM = 128
        DEPTH = 2
        HEADS = 8
        DIM_HEAD = 64
        WINDOW = 64
        INNER = HEADS * DIM_HEAD
        HID = int(DIM * 4 * 2 / 3)
        B, N = (2, 1024)
        QK_SCALE = 8.0

        def shift_token(t):
            t1, t2 = jnp.split(t, 2, axis=-1)
            t2 = jnp.pad(t2, ((0, 0), (1, 0), (0, 0)))[:, :-1]
            return jnp.concatenate([t1, t2], axis=-1)

        def l2norm(t):
            return t / jnp.clip(jnp.linalg.norm(t, axis=-1, keepdims=True), 1e-12)

        def rotate_half(x):
            x1, x2 = jnp.split(x, 2, axis=-1)
            return jnp.concatenate([-x2, x1], axis=-1)

        def rotary_xpos(q, k):
            n = q.shape[-2]
            half_idx = jnp.arange(0, DIM_HEAD, 2, dtype=jnp.float32)
            inv_freq = 1.0 / 10000.0 ** (half_idx / DIM_HEAD)
            t = jnp.arange(n, dtype=jnp.float32)
            freqs = t[:, None] * inv_freq[None, :]
            freqs = jnp.concatenate([freqs, freqs], axis=-1)
            base = (half_idx + 0.4 * DIM_HEAD) / (1.4 * DIM_HEAD)
            power = (t - n // 2) / float(WINDOW // 2)
            scale = base[None, :] ** power[:, None]
            scale = jnp.concatenate([scale, scale], axis=-1)
            cos, sin = (jnp.cos(freqs), jnp.sin(freqs))
            q = q * cos * scale + rotate_half(q) * sin * scale
            k = k * cos / scale + rotate_half(k) * sin / scale
            return (q, k)

        def local_attention(q, k, v):
            b, h, n, d = q.shape
            w = n // WINDOW
            bq = q.reshape(b, h, w, WINDOW, d) * QK_SCALE
            bk = k.reshape(b, h, w, WINDOW, d)
            bv = v.reshape(b, h, w, WINDOW, d)

            def look_around(t):
                p = jnp.pad(t, ((0, 0), (0, 0), (1, 0), (0, 0), (0, 0)))
                return jnp.concatenate([p[:, :, :w], p[:, :, 1:]], axis=3)
            bk, bv = (look_around(bk), look_around(bv))
            bt = jnp.arange(n).reshape(w, WINDOW)
            btp = jnp.pad(bt, ((1, 0), (0, 0)), constant_values=-1)
            btk = jnp.concatenate([btp[:w], btp[1:]], axis=1)
            sim = jnp.einsum('bhwid,bhwjd->bhwij', bq, bk)
            i = bt[:, :, None]
            j = btk[:, None, :]
            mask = (i < j) | (i > j + WINDOW) | (j == -1)
            sim = jnp.where(mask, -jnp.finfo(sim.dtype).max, sim)
            attn = jax.nn.softmax(sim, axis=-1)
            out = jnp.einsum('bhwij,bhwjd->bhwid', attn, bv)
            return out.reshape(b, h, n, d)

        def _layer(x, wqkv, qs, ksc, wo, lg, lb, w1, b1, w2, b2):
            b, n, _ = x.shape
            h = shift_token(x)
            qkv = h @ wqkv
            q, k, v = jnp.split(qkv, 3, axis=-1)
            to_heads = lambda t: t.reshape(b, n, HEADS, DIM_HEAD).transpose(0, 2, 1, 3)
            q, k, v = (to_heads(q), to_heads(k), to_heads(v))
            q = l2norm(q) * qs
            k = l2norm(k) * ksc
            q, k = rotary_xpos(q, k)
            o = local_attention(q, k, v)
            o = o.transpose(0, 2, 1, 3).reshape(b, n, INNER)
            x = x + o @ wo
            h = shift_token(x)
            mu = h.mean(-1, keepdims=True)
            var = h.var(-1, keepdims=True)
            h = (h - mu) / jnp.sqrt(var + 1e-05) * lg + lb
            h = h @ w1 + b1
            a, g = jnp.split(h, 2, axis=-1)
            h = a * jax.nn.gelu(g, approximate=False)
            x = x + h @ w2 + b2
            return x
        key = jax.random.key(seed)
        ks = jax.random.split(key, 6)
        return {'x': jax.random.normal(ks[0], (B, N, DIM), jnp.float32), 'wqkv': jax.random.normal(ks[1], (DEPTH, DIM, 3 * INNER), jnp.float32) * 0.02, 'q_scale': jnp.ones((DEPTH, DIM_HEAD), jnp.float32), 'k_scale': jnp.ones((DEPTH, DIM_HEAD), jnp.float32), 'wo': jax.random.normal(ks[2], (DEPTH, INNER, DIM), jnp.float32) * 0.02, 'ln_g': jnp.ones((DEPTH, DIM), jnp.float32), 'ln_b': jnp.zeros((DEPTH, DIM), jnp.float32), 'w1': jax.random.normal(ks[3], (DEPTH, DIM, 2 * HID), jnp.float32) * 0.02, 'b1': jnp.zeros((DEPTH, 2 * HID), jnp.float32), 'w2': jax.random.normal(ks[4], (DEPTH, HID, DIM), jnp.float32) * 0.02, 'b2': jnp.zeros((DEPTH, DIM), jnp.float32)}
    _L1_ffn_in = _L1_ffn_setup()
    _L1_c = _w((lambda *s: np.random.randn(*s).astype(np.float32) * 0.05)(16, 128))
    _L1_wmod = _w((lambda *s: np.random.randn(*s).astype(np.float32) * 0.05)(128, 6 * 128) * 128 ** (-0.5))
    _d = {'L0_attn_z': _L0_attn_in['z'], 'L0_attn_ln_scale': _L0_attn_in['ln_scale'], 'L0_attn_ln_bias': _L0_attn_in['ln_bias'], 'L0_attn_w_qkv': _L0_attn_in['w_qkv'], 'L0_attn_w_proj': _L0_attn_in['w_proj'], 'L0_attn_b_proj': _L0_attn_in['b_proj'], 'L0_ffn_Wq': _L0_ffn_in['Wq'], 'L0_ffn_bq': _L0_ffn_in['bq'], 'L0_ffn_Wk': _L0_ffn_in['Wk'], 'L0_ffn_bk': _L0_ffn_in['bk'], 'L0_ffn_Wv': _L0_ffn_in['Wv'], 'L0_ffn_bv': _L0_ffn_in['bv'], 'L0_ffn_Wr': _L0_ffn_in['Wr'], 'L0_ffn_br': _L0_ffn_in['br'], 'L0_ffn_Wo': _L0_ffn_in['Wo'], 'L0_ffn_bo': _L0_ffn_in['bo'], 'L0_c': _L0_c, 'L0_wmod': _L0_wmod, 'L1_attn_mask': _L1_attn_in['mask'], 'L1_attn_Wq': _L1_attn_in['Wq'], 'L1_attn_bq': _L1_attn_in['bq'], 'L1_attn_Wk': _L1_attn_in['Wk'], 'L1_attn_bk': _L1_attn_in['bk'], 'L1_attn_Wv': _L1_attn_in['Wv'], 'L1_attn_bv': _L1_attn_in['bv'], 'L1_attn_Wo': _L1_attn_in['Wo'], 'L1_attn_bo': _L1_attn_in['bo'], 'L1_ffn_wqkv': _L1_ffn_in['wqkv'], 'L1_ffn_q_scale': _L1_ffn_in['q_scale'], 'L1_ffn_k_scale': _L1_ffn_in['k_scale'], 'L1_ffn_wo': _L1_ffn_in['wo'], 'L1_ffn_ln_g': _L1_ffn_in['ln_g'], 'L1_ffn_ln_b': _L1_ffn_in['ln_b'], 'L1_ffn_w1': _L1_ffn_in['w1'], 'L1_ffn_b1': _L1_ffn_in['b1'], 'L1_ffn_w2': _L1_ffn_in['w2'], 'L1_ffn_b2': _L1_ffn_in['b2'], 'L1_c': _L1_c, 'L1_wmod': _L1_wmod}
    _x0 = _d['L0_attn_z']
    _d['L0_attn_z'] = jax.random.normal(jax.random.fold_in(jax.random.key(seed), 1), (16, 256, 128), dtype=_x0.dtype)
    del _x0
    return _d

def reference(L0_attn_z, L0_attn_ln_scale, L0_attn_ln_bias, L0_attn_w_qkv, L0_attn_w_proj, L0_attn_b_proj, L0_ffn_Wq, L0_ffn_bq, L0_ffn_Wk, L0_ffn_bk, L0_ffn_Wv, L0_ffn_bv, L0_ffn_Wr, L0_ffn_br, L0_ffn_Wo, L0_ffn_bo, L0_c, L0_wmod, L1_attn_mask, L1_attn_Wq, L1_attn_bq, L1_attn_Wk, L1_attn_bk, L1_attn_Wv, L1_attn_bv, L1_attn_Wo, L1_attn_bo, L1_ffn_wqkv, L1_ffn_q_scale, L1_ffn_k_scale, L1_ffn_wo, L1_ffn_ln_g, L1_ffn_ln_b, L1_ffn_w1, L1_ffn_b1, L1_ffn_w2, L1_ffn_b2, L1_c, L1_wmod):

    def _L0_attn_ref(z, ln_scale, ln_bias, w_qkv, w_proj, b_proj):
        import jax, jax.numpy as jnp
        import numpy as np
        B, N, D, H = (2, 256, 128, 16)
        HD = D // H
        SCALING = (D / H) ** 0.5
        EPS = 1e-05
        b, n, d = z.shape
        mu = jnp.mean(z, axis=-1, keepdims=True)
        var = jnp.mean(jnp.square(z - mu), axis=-1, keepdims=True)
        zn = (z - mu) / jnp.sqrt(var + EPS) * ln_scale + ln_bias
        qkv = zn @ w_qkv
        qkv5 = qkv.reshape(b, n, H, HD, 3)
        q = jnp.transpose(qkv5[..., 0], (0, 2, 1, 3))
        k = jnp.transpose(qkv5[..., 1], (0, 2, 1, 3))
        v = jnp.transpose(qkv5[..., 2], (0, 2, 1, 3))
        scores = jnp.einsum('bhqd,bhkd->bhqk', q, k) / SCALING
        att = jax.nn.softmax(scores, axis=-1)
        out = jnp.einsum('bhal,bhlv->bhav', att, v)
        out = jnp.transpose(out, (0, 2, 1, 3)).reshape(b, n, d)
        out = out @ w_proj + b_proj
        return z + out

    def _L0_ffn_ref(x, Wq, bq, Wk, bk, Wv, bv, Wr, br, Wo, bo):
        import jax, jax.numpy as jnp
        import numpy as np
        N_HEAD, N_ACTIVE, D_MODEL, D_ATTN = (16, 4, 128, 64)
        B, S, D = x.shape
        H, K, dh = (N_HEAD, N_ACTIVE, D_ATTN)
        dist = jax.nn.softmax(jnp.mean(x @ Wr + br, axis=1), axis=-1)
        top_vals, top_idx = jax.lax.top_k(dist, K)
        sparse = jnp.zeros_like(dist).at[jnp.arange(B)[:, None], top_idx].set(top_vals)
        gates_all = jax.nn.softmax(sparse, axis=1)
        g = jnp.take_along_axis(gates_all, top_idx, axis=1)[:, :, None, None]

        def proj(W, b):
            return (x @ W + b).reshape(B, S, H, dh).transpose(0, 2, 1, 3)
        Q, Kt, V = (proj(Wq, bq), proj(Wk, bk), proj(Wv, bv))
        idx = top_idx[:, :, None, None]
        Qk = jnp.take_along_axis(Q, idx, axis=1) * g
        Kk = jnp.take_along_axis(Kt, idx, axis=1) * g
        Vk = jnp.take_along_axis(V, idx, axis=1) * g
        scores = jnp.einsum('bksd,bktd->bkst', Qk, Kk) / jnp.sqrt(jnp.float32(dh))
        attn = jax.nn.softmax(scores, axis=-1)
        out = jnp.einsum('bkst,bktd->bksd', attn, Vk)
        out = out.transpose(0, 2, 1, 3).reshape(B, S, K * dh)
        return out @ Wo + bo

    def _L1_attn_ref(x, mask, Wq, bq, Wk, bk, Wv, bv, Wo, bo):
        import jax, jax.numpy as jnp
        import numpy as np
        D_MODEL = 128
        N_HEADS = 16
        D_HEAD = D_MODEL // N_HEADS
        EPS = 1e-06
        B, N = (1, 256)

        def _phi(x):
            return jax.nn.elu(x) + 1.0

        def _split_heads(y, b, n):
            return y.reshape(b, n, N_HEADS, D_HEAD).transpose(0, 2, 1, 3)
        b, n, _ = x.shape
        q = _phi(_split_heads(x @ Wq.T + bq, b, n))
        k = _phi(_split_heads(x @ Wk.T + bk, b, n))
        v = _split_heads(x @ Wv.T + bv, b, n)
        kv = jnp.einsum('bhnd,bhne->bhnde', k, v)
        kv_prefix = jnp.cumsum(kv, axis=2)
        k_prefix = jnp.cumsum(k, axis=2)
        numer = jnp.einsum('bhnd,bhnde->bhne', q, kv_prefix)
        denom = jnp.einsum('bhnd,bhnd->bhn', q, k_prefix)[..., None]
        out_heads = numer / (denom + EPS)
        merged = out_heads.transpose(0, 2, 1, 3).reshape(b, n, D_MODEL)
        return merged @ Wo.T + bo

    def _L1_ffn_ref(x, wqkv, q_scale, k_scale, wo, ln_g, ln_b, w1, b1, w2, b2):
        import jax, jax.numpy as jnp
        import numpy as np
        DIM = 128
        DEPTH = 2
        HEADS = 8
        DIM_HEAD = 64
        WINDOW = 64
        INNER = HEADS * DIM_HEAD
        HID = int(DIM * 4 * 2 / 3)
        B, N = (2, 1024)
        QK_SCALE = 8.0

        def shift_token(t):
            t1, t2 = jnp.split(t, 2, axis=-1)
            t2 = jnp.pad(t2, ((0, 0), (1, 0), (0, 0)))[:, :-1]
            return jnp.concatenate([t1, t2], axis=-1)

        def l2norm(t):
            return t / jnp.clip(jnp.linalg.norm(t, axis=-1, keepdims=True), 1e-12)

        def rotate_half(x):
            x1, x2 = jnp.split(x, 2, axis=-1)
            return jnp.concatenate([-x2, x1], axis=-1)

        def rotary_xpos(q, k):
            n = q.shape[-2]
            half_idx = jnp.arange(0, DIM_HEAD, 2, dtype=jnp.float32)
            inv_freq = 1.0 / 10000.0 ** (half_idx / DIM_HEAD)
            t = jnp.arange(n, dtype=jnp.float32)
            freqs = t[:, None] * inv_freq[None, :]
            freqs = jnp.concatenate([freqs, freqs], axis=-1)
            base = (half_idx + 0.4 * DIM_HEAD) / (1.4 * DIM_HEAD)
            power = (t - n // 2) / float(WINDOW // 2)
            scale = base[None, :] ** power[:, None]
            scale = jnp.concatenate([scale, scale], axis=-1)
            cos, sin = (jnp.cos(freqs), jnp.sin(freqs))
            q = q * cos * scale + rotate_half(q) * sin * scale
            k = k * cos / scale + rotate_half(k) * sin / scale
            return (q, k)

        def local_attention(q, k, v):
            b, h, n, d = q.shape
            w = n // WINDOW
            bq = q.reshape(b, h, w, WINDOW, d) * QK_SCALE
            bk = k.reshape(b, h, w, WINDOW, d)
            bv = v.reshape(b, h, w, WINDOW, d)

            def look_around(t):
                p = jnp.pad(t, ((0, 0), (0, 0), (1, 0), (0, 0), (0, 0)))
                return jnp.concatenate([p[:, :, :w], p[:, :, 1:]], axis=3)
            bk, bv = (look_around(bk), look_around(bv))
            bt = jnp.arange(n).reshape(w, WINDOW)
            btp = jnp.pad(bt, ((1, 0), (0, 0)), constant_values=-1)
            btk = jnp.concatenate([btp[:w], btp[1:]], axis=1)
            sim = jnp.einsum('bhwid,bhwjd->bhwij', bq, bk)
            i = bt[:, :, None]
            j = btk[:, None, :]
            mask = (i < j) | (i > j + WINDOW) | (j == -1)
            sim = jnp.where(mask, -jnp.finfo(sim.dtype).max, sim)
            attn = jax.nn.softmax(sim, axis=-1)
            out = jnp.einsum('bhwij,bhwjd->bhwid', attn, bv)
            return out.reshape(b, h, n, d)

        def _layer(x, wqkv, qs, ksc, wo, lg, lb, w1, b1, w2, b2):
            b, n, _ = x.shape
            h = shift_token(x)
            qkv = h @ wqkv
            q, k, v = jnp.split(qkv, 3, axis=-1)
            to_heads = lambda t: t.reshape(b, n, HEADS, DIM_HEAD).transpose(0, 2, 1, 3)
            q, k, v = (to_heads(q), to_heads(k), to_heads(v))
            q = l2norm(q) * qs
            k = l2norm(k) * ksc
            q, k = rotary_xpos(q, k)
            o = local_attention(q, k, v)
            o = o.transpose(0, 2, 1, 3).reshape(b, n, INNER)
            x = x + o @ wo
            h = shift_token(x)
            mu = h.mean(-1, keepdims=True)
            var = h.var(-1, keepdims=True)
            h = (h - mu) / jnp.sqrt(var + 1e-05) * lg + lb
            h = h @ w1 + b1
            a, g = jnp.split(h, 2, axis=-1)
            h = a * jax.nn.gelu(g, approximate=False)
            x = x + h @ w2 + b2
            return x
        for l in range(DEPTH):
            x = _layer(x, wqkv[l], q_scale[l], k_scale[l], wo[l], ln_g[l], ln_b[l], w1[l], b1[l], w2[l], b2[l])
        return x
    x = L0_attn_z
    mod = (_silu(L0_c) @ L0_wmod).reshape(L0_c.shape[0], 6, 1, -1)
    sa, ca, ga, sb, cb, gb = (mod[:, 0], mod[:, 1], mod[:, 2], mod[:, 3], mod[:, 4], mod[:, 5])
    ga = (2 * (ga >= 0) - 1) * jnp.maximum(jnp.abs(ga), 0.25)
    gb = (2 * (gb >= 0) - 1) * jnp.maximum(jnp.abs(gb), 0.25)
    h = _layernorm(x, axis=-1) * (1 + ca) + sa
    x = x + ga * _L0_attn_ref(h, L0_attn_ln_scale, L0_attn_ln_bias, L0_attn_w_qkv, L0_attn_w_proj, L0_attn_b_proj)
    h = _layernorm(x, axis=-1) * (1 + cb) + sb
    x = x + gb * _L0_ffn_ref(h, L0_ffn_Wq, L0_ffn_bq, L0_ffn_Wk, L0_ffn_bk, L0_ffn_Wv, L0_ffn_bv, L0_ffn_Wr, L0_ffn_br, L0_ffn_Wo, L0_ffn_bo)
    mod = (_silu(L1_c) @ L1_wmod).reshape(L1_c.shape[0], 6, 1, -1)
    sa, ca, ga, sb, cb, gb = (mod[:, 0], mod[:, 1], mod[:, 2], mod[:, 3], mod[:, 4], mod[:, 5])
    ga = (2 * (ga >= 0) - 1) * jnp.maximum(jnp.abs(ga), 0.25)
    gb = (2 * (gb >= 0) - 1) * jnp.maximum(jnp.abs(gb), 0.25)
    h = _layernorm(x, axis=-1) * (1 + ca) + sa
    x = x + ga * _L1_attn_ref(h, L1_attn_mask, L1_attn_Wq, L1_attn_bq, L1_attn_Wk, L1_attn_bk, L1_attn_Wv, L1_attn_bv, L1_attn_Wo, L1_attn_bo)
    h = _layernorm(x, axis=-1) * (1 + cb) + sb
    x = x + gb * _L1_ffn_ref(h, L1_ffn_wqkv, L1_ffn_q_scale, L1_ffn_k_scale, L1_ffn_wo, L1_ffn_ln_g, L1_ffn_ln_b, L1_ffn_w1, L1_ffn_b1, L1_ffn_w2, L1_ffn_b2)
    return x

_drawn_inputs = setup_inputs


def setup_inputs(seed=0):
    import zlib

    import numpy as np

    out = dict(_drawn_inputs(seed))
    spreads = {'L0_attn_ln_scale': (1.0, 0.6),
     'L0_attn_ln_bias': (0.0, 0.28),
     'L0_attn_b_proj': (0.0, 0.313),
     'L0_ffn_bq': (0.0, 2.0),
     'L0_ffn_bk': (0.0, 2.0),
     'L0_ffn_bv': (0.0, 0.8),
     'L0_ffn_br': (0.0, 0.8),
     'L0_ffn_bo': (0.0, 0.315),
     'L1_ffn_q_scale': (1.0, 0.6),
     'L1_ffn_k_scale': (1.0, 0.6),
     'L1_ffn_ln_g': (1.0, 0.6),
     'L1_ffn_ln_b': (0.0, 0.8),
     'L1_ffn_b1': (0.0, 0.8),
     'L1_ffn_b2': (0.0, 0.8)}
    factors = {'L0_ffn_Wq': 64.0,
     'L0_ffn_Wk': 64.0,
     'L0_ffn_Wv': 8.0,
     'L0_ffn_Wr': 8.0,
     'L0_ffn_Wo': 8.0,
     'L1_attn_Wq': 8.0,
     'L1_attn_bq': 45.301,
     'L1_attn_Wk': 4.974,
     'L1_attn_bk': 45.288,
     'L1_ffn_wqkv': 6.738,
     'L1_ffn_wo': 6.829,
     'L1_ffn_w1': 8.0,
     'L1_ffn_w2': 8.0}
    for name, (base, spread) in spreads.items():
        noise = np.random.default_rng([zlib.crc32(name.encode()), seed]).standard_normal(out[name].shape)
        drawn = base * np.exp(spread * noise) if base else spread * noise
        out[name] = jnp.asarray(drawn.astype(out[name].dtype))
    for name, factor in factors.items():
        out[name] = (out[name] * factor).astype(out[name].dtype)
    return out
```

```python
from contextlib import ExitStack

import concourse.bass as bass
from concourse import mybir

F32 = mybir.dt.float32
BF16 = mybir.dt.bfloat16
U32 = mybir.dt.uint32
ACT = mybir.ActivationFunctionType
ALU = mybir.AluOpType
AX = mybir.AxisListType

P = 128
NB = 16
T = 256
NT = T // P
H0 = 16
HD = P // H0
TERMS = ((0, 0), (1, 1), (0, 1), (1, 0), (0, 2), (2, 0))
KS = HD * len(TERMS)
NH = 16
NA = 4
DA = 64
WC = 3 * DA + 3
DEPTH = 2
LH = 8
LD = 64
INNER = LH * LD
WINDOW = 64
HID = 341
HT = (128, 128, 85)
SW = P + P + WINDOW
PW = P + 2 * P
NEG = -3.0e38
LN_EPS = 1e-5
RSTD_SHIFT = 16

VEC = {n: i for i, n in enumerate(
    ["ln_scale", "ln_bias", "b_proj", "bo0", "bq1", "bk1", "bo1"]
    + [f"{n}{l}" for l in range(DEPTH) for n in
       ("ln_g", "ln_b", "b2_", "b1a0_", "b1a1_", "b1a2_", "b1g0_", "b1g1_", "b1g2_")])}
NV = len(VEC)
ROWS = 16 + P + DEPTH * 4 * LD


def program(nc, z, cT, wmod, w0qkv, w0proj, wr, wpack, wo0, w1qkv, w1o, wqkv, wo, w1, w2,
            vecs, rows, ident_in, tri_in, diag_in, sel_in, band_in, rot_in, out):
    with ExitStack() as ctx:
        def sb(name, shape, dt=F32):
            return ctx.enter_context(nc.sbuf_tensor(name, shape, dt))

        def sem(name):
            return ctx.enter_context(nc.semaphore(name))

        c_sb = sb("c_sb", [P, 2, NB])
        w0qkv_sb = sb("w0qkv_sb", [P, 3 * P])
        w0proj_sb = sb("w0proj_sb", [P, P])
        wr_sb = sb("wr_sb", [P, NH])
        wo0_sb = sb("wo0_sb", [P, 2, P])
        w1qkv_sb = sb("w1qkv_sb", [P, 3 * P])
        w1o_sb = sb("w1o_sb", [P, P])
        wqkv_sb = sb("wqkv_sb", [P, DEPTH, 3 * INNER])
        wo_sb = sb("wo_sb", [P, DEPTH, 4, P])
        w1_sb = sb("w1_sb", [P, DEPTH, 2 * HID])
        w2_sb = sb("w2_sb", [P, DEPTH, 3, P])
        vec = sb("vec", [P, NV])
        row = sb("row", [P, ROWS])
        ident = sb("ident", [P, P])
        tri = sb("tri", [P, P])
        diag = sb("diag", [P, H0 * (HD + 1)])
        bandf = sb("bandf", [P, SW])
        rot = sb("rot", [P, 4, NT, LD])
        identb = sb("identb", [P, P], BF16)
        sel = sb("sel", [2 * H0, H0, P], BF16)
        band = sb("band", [P, SW], BF16)
        ones = sb("ones", [P, P])
        eps = sb("eps", [P, 1])
        shift = sb("shift", [P, 1])
        wave = sb("wave", [P, DEPTH, 4, NT, LD])
        silu = sb("silu", [P, 2, NB])
        stmp = sb("stmp", [P, 2, NB])
        mod = sb("mod", [P, 12, NB])
        sgn = sb("sgn", [P, NB])
        mag = sb("mag", [P, NB])

        m = sb("m", [P, 12])
        x = sb("x", [P, T])
        h = sb("h", [P, T])
        zn = sb("zn", [P, T])
        xn = sb("xn", [P, NT, P])
        stats = sb("stats", [P, NT, 6])
        mv = sb("mv", [P, NT, 2])
        lnv = sb("lnv", [P, NT])
        rstd = sb("rstd", [P, NT])
        res = sb("res", [P, T])
        part = sb("part", [P, 6, T], BF16)
        rem = sb("rem", [P, 2, T])
        phi = sb("phi", [P, 2, T])
        phe = sb("phe", [P, 2, T])
        stack = sb("stack", [KS, H0, 2, T], BF16)
        vaug = sb("vaug", [P, NT, H0, HD + 1])
        nmax = sb("nmax", [P, 2, H0, NT])
        nmf = sb("nmf", [P, NT, 2, H0])
        nmb = sb("nmb", [P, NT, 2, H0], BF16)
        nmT = sb("nmT", [2 * H0, T], BF16)
        pT = sb("pT", [P, 2, 2, NT, T])
        rsum = sb("rsum", [P, NT, H0])
        den = sb("den", [P, NT, H0])
        att = sb("att", [P, NT, P])
        attT = sb("attT", [P, T])
        knat = sb("knat", [P, P])
        inter = sb("inter", [P, H0 * (HD + 1)])
        state = sb("state", [P, H0 * (HD + 1)])
        masked = sb("masked", [P, 2, 4, NT, P])

        hsum = sb("hsum", [P, 1])
        hmean = sb("hmean", [P, P])
        logit = sb("logit", [P, NH])
        lmax = sb("lmax", [P, 1])
        dist = sb("dist", [P, NH])
        dsum = sb("dsum", [P, 1])
        drec = sb("drec", [P, 1])
        top = sb("top", [P, 8])
        tidx = sb("tidx", [P, 8], U32)
        ntop = sb("ntop", [P, 1])
        ge = sb("ge", [P, NA + 1])
        gsum = sb("gsum", [P, 1])
        grec = sb("grec", [P, 1])
        g = sb("g", [P, NA])
        wsel = sb("wsel", [P, NA, WC])
        gp = sb("gp", [P, 2])
        gq = sb("gq", [P, 2])
        bp = sb("bp", [P, 2, 3])
        bvg = sb("bvg", [P, 2])
        fq = sb("fq", [P, 2, T])
        fk = sb("fk", [P, 2, T])
        fv = sb("fv", [P, NT, NA, DA])
        fnm = sb("fnm", [P, NA, NT])
        fs = sb("fs", [P, NA, NT])
        fr = sb("fr", [P, NA, NT])
        fp = sb("fp", [P, NA, NT, T])
        fo = sb("fo", [P, NT, NA, DA])
        foT = sb("foT", [P, 2, T])

        y = sb("y", [P, T])
        ysh = sb("ysh", [P, T])
        qk = sb("qk", [P, 2, NT, LH, LD])
        sq = sb("sq", [P, 2, NT, LH, LD])
        ss = sb("ss", [P, 2, NT, LH])
        lss = sb("lss", [P, 2, NT, LH])
        rn = sb("rn", [P, 2, NT, LH])
        r1 = sb("r1", [P, 2, NT, LH, LD])
        r2 = sb("r2", [P, 2, NT, LH, LD])
        qkT = sb("qkT", [P, 2, 4, T])
        lv = sb("lv", [P, NT, INNER])
        lnm = sb("lnm", [P, LH, NT])
        ls = sb("ls", [P, LH, NT])
        lr = sb("lr", [P, LH, NT])
        lp = sb("lp", [P, LH, PW])
        lpT = sb("lpT", [P, LH, PW])
        lo = sb("lo", [P, NT, INNER])
        loT = sb("loT", [P, 4, T])
        gel = sb("gel", [P, 3, T])
        ug = sb("ug", [P, 3, T])

        ps = ctx.enter_context(nc.psum_tensor("ps", [P, 8, 512], F32))
        psb = ps[:, 1, :].bitcast(BF16)

        wmod_sb = qk[:, :, :, :, :].rearrange("p i t h d -> p (i t h d)")[:, 0:12 * P].rearrange("p (l n) -> p l n", l=2)
        self32 = lpT[0:2 * H0, :, :].rearrange("p h c -> p (h c)")[:, 0:H0 * P]
        fpT = lpT[:, :, :].rearrange("p h c -> p (h c)")[:, 0:NA * NT * NT * P]\
            .rearrange("p (k t c q) -> p k t c q", k=NA, t=NT, c=NT)

        loaded = sem("loaded")
        pool_ready = sem("pool_ready")
        silu_e = sem("silu_e")
        silu_done = sem("silu_done")
        mod_mm = sem("mod_mm")
        set_chain = sem("set_chain")
        names = """x_in dve_chain act_chain m_ready
            ln_src ln_tok ln_stat ln_rstd ln_norm ln_feat ln_out
            qkv_mm part0 part1_r part1 part2 v_ready stacked
            sc_mm sc_max nm_ready nm_T nm_sb st_mm st_exp pv_mm
            att_ready att_T attT_sb proj_mm
            phi_min phi_exp phi_ready kT_ps knat_sb state_mm state_sb inter_mm inter_sb lin_mm lin_masked
            hmean_ready route_mm lmax_ready dexp top_ready gexp g_ready wsel_in fqkv_mm f_qk f_v
            fs_mm f_max f_exp f_T f_Tsb fo_mm fo_ready fo_T foT_sb fproj_mm
            y_ready lqkv_mm l_copied l_sq l_ss l_rn l_r2 l_rot l_T l_Tsb l_v ls_mm l_max l_exp l_pT l_pTsb
            lo_mm lo_ready lo_T loT_sb lproj_mm up_mm gelu_done ug_ready down_mm x_done out_done""".split()
        s = {n: sem(n) for n in names}
        loop_sems = range(s[names[0]].num, s[names[-1]].num + 1)
        assert [s[n].num for n in names] == list(loop_sems)

        LOADS = ((c_sb[:, :, :], cT), (wmod_sb, wmod), (w0qkv_sb[:, :], w0qkv), (w0proj_sb[:, :], w0proj),
                 (wr_sb[:, :], wr), (wo0_sb[:, :, :], wo0.rearrange("(j p) n -> p j n", p=P)),
                 (w1qkv_sb[:, :], w1qkv), (w1o_sb[:, :], w1o),
                 (wqkv_sb[:, :, :], wqkv.rearrange("l p n -> p l n")),
                 (wo_sb[:, 0, :, :], wo[0].rearrange("(j p) n -> p j n", p=P)),
                 (wo_sb[:, 1, :, :], wo[1].rearrange("(j p) n -> p j n", p=P)),
                 (w1_sb[:, :, :], w1.rearrange("l p n -> p l n")),
                 (w2_sb[:, :, 0, :], w2[:, 0:P, :].rearrange("l p n -> p l n")),
                 (w2_sb[:, :, 1, :], w2[:, P:2 * P, :].rearrange("l p n -> p l n")),
                 (w2_sb[0:HT[2], :, 2, :], w2[:, 2 * P:HID, :].rearrange("l p n -> p l n")),
                 (vec[:, :], vecs), (row[:, :], rows), (ident[:, :], ident_in), (tri[:, :], tri_in),
                 (diag[:, :], diag_in), (self32, sel_in), (bandf[:, :], band_in), (rot[:, :, :, :], rot_in))

        def V(name, l=""):
            i = VEC[f"{name}{l}"]
            return vec[:, i:i + 1]

        with nc.Block() as block:
            @block.sync
            def _(sp):
                for dst, src in LOADS:
                    sp.dma_start(dst, src).then_inc(loaded, 16)

            @block.gpsimd
            def _(pool):
                pool.memset(vaug[:, :, :, :], 1.0).then_inc(pool_ready, 1)
                pool.memset(lp[:, :, :], 0.0).then_inc(pool_ready, 1)
                pool.memset(ones[:, :], 1.0).then_inc(pool_ready, 1)
                pool.memset(eps[:, :], LN_EPS).then_inc(pool_ready, 1)
                pool.memset(shift[:, :], 0.5 * RSTD_SHIFT * 0.6931471805599453).then_inc(pool_ready, 1)

            @block.scalar
            def _(act):
                act.wait_ge(loaded, 16 * len(LOADS))
                act.activation(stmp[:, :, :], c_sb[:, :, :], ACT.Exp, scale=-1.0).then_inc(silu_e, 1)

            @block.tensor
            def _(pe):
                pe.wait_ge(silu_done, 1)
                for l in range(2):
                    for j in range(6):
                        mm = pe.matmul(ps[:, l, j * NB:(j + 1) * NB], wmod_sb[:, l, j * P:(j + 1) * P],
                                       silu[:, l, :], start=True, stop=True)
                mm.then_inc(mod_mm, 1)

            @block.vector
            def _(dve):
                n = [0]

                def link(ins):
                    n[0] += 1
                    ins.then_inc(set_chain, 1)
                    dve.wait_ge(set_chain, n[0])

                dve.wait_ge(loaded, 16 * len(LOADS))
                dve.tensor_copy(identb[:, :], ident[:, :])
                dve.tensor_copy(sel[:, :, :].rearrange("p a b -> p (a b)"), self32)
                dve.tensor_copy(band[:, :], bandf[:, :])
                dve.tensor_scalar(w0qkv_sb[:, 0:P], w0qkv_sb[:, 0:P], float(HD) ** -0.5, None, ALU.mult)
                for l in range(DEPTH):
                    for i in range(4):
                        at = NH + P + (l * 4 + i) * LD
                        ins = dve.tensor_tensor(wave[:, l, i, :, :], rot[:, i, :, :],
                                                row[:, None, at:at + LD].broadcast_to([P, NT, LD]), ALU.mult)
                link(ins)
                dve.tensor_scalar(wave[:, :, 0:2, :, :].rearrange("p l i t d -> p l (i t d)"),
                                  wave[:, :, 0:2, :, :].rearrange("p l i t d -> p l (i t d)"), 8.0, None, ALU.mult)
                dve.wait_ge(silu_e, 1)
                link(dve.tensor_scalar(stmp[:, :, :], stmp[:, :, :], 1.0, None, ALU.add))
                link(dve.reciprocal(stmp[:, :, :], stmp[:, :, :]))
                dve.tensor_tensor(silu[:, :, :], c_sb[:, :, :], stmp[:, :, :], ALU.mult).then_inc(silu_done, 1)
                dve.wait_ge(mod_mm, 1)
                for l in range(2):
                    for j in range(6):
                        src = ps[:, l, j * NB:(j + 1) * NB]
                        dst = mod[:, 6 * l + j, :]
                        if j % 3 == 0:
                            dve.tensor_copy(dst, src)
                        elif j % 3 == 1:
                            dve.tensor_scalar(dst, src, 1.0, None, ALU.add)
                        else:
                            link(dve.tensor_scalar(sgn[:, :], src, 0.0, 2.0, ALU.is_ge, ALU.mult))
                            link(dve.tensor_scalar(sgn[:, :], sgn[:, :], 1.0, None, ALU.subtract))
                            link(dve.tensor_tensor(mag[:, :], src, sgn[:, :], ALU.mult))
                            link(dve.scalar_tensor_tensor(dst, mag[:, :], 0.25, sgn[:, :], ALU.max, ALU.mult))
                dve.wait_ge(pool_ready, 5)

        with nc.Fori(0, NB) as b:
            with nc.Block() as block:

                @block.sync
                def _(sp):
                    sp.dma_start(x[:, :], z[bass.ds(b, 1)].rearrange("b p t -> p (b t)")).then_inc(s["x_in"], 16)
                    for use in range(2):
                        sp.wait_ge(s["part2"], use + 1)
                        if use == 1:
                            sp.wait_ge(s["pv_mm"], 1)
                        for t, (i, j) in enumerate(TERMS):
                            sp.dma_start(stack[HD * t:HD * t + HD, :, :, :],
                                         part[:, i:3 + j + 1:3 + j - i, :]).then_inc(s["stacked"], 16)
                        if use == 0:
                            sp.wait_ge(s["top_ready"], 1)
                            for k in range(NA):
                                head = sp.value_load(tidx[0:1, k:k + 1], min_val=0, max_val=NH - 1)
                                sp.dma_start(wsel[:, k, :], wpack[bass.ds(head, 1)].rearrange("b p n -> p (b n)"))\
                                    .then_inc(s["wsel_in"], 16)
                    sp.wait_ge(s["x_done"], 1)
                    sp.dma_start(out[bass.ds(b, 1)].rearrange("b p t -> p (b t)"), x[:, :]).then_inc(s["out_done"], 16)
                    sp.wait_ge(s["out_done"], 16)

                @block.gpsimd
                def _(pool):
                    for use in range(2):
                        pool.wait_ge(s["part1_r"], use + 1)
                        pool.tensor_copy(part[:, 1:5:3, :], rem[:, :, :]).then_inc(s["part1"], 1)
                    for l in range(DEPTH):
                        for i in range(2):
                            for t in range(NT):
                                pool.wait_ge(s["l_copied"], 4 * l + 2 * t + i + 1)
                                for a in range(2):
                                    d0, d1 = a * LD // 2, (1 - a) * LD // 2
                                    ins = pool.tensor_tensor(
                                        r2[:, i, t, :, d0:d0 + LD // 2], qk[:, i, t, :, d1:d1 + LD // 2],
                                        wave[:, l, 2 * i + 1, t, None, d0:d0 + LD // 2].broadcast_to([P, LH, LD // 2]),
                                        ALU.mult)
                        ins.then_inc(s["l_r2"], 1)

                @block.tensor
                def _(pe):
                    def layer_norm(u):
                        src = (x, h, x, x, x, ysh, ysh)[u]
                        if u == 0:
                            pe.wait_ge(s["x_in"], 16)
                        elif u == 1:
                            pe.wait_ge(s["ln_out"], 1)
                        else:
                            pe.wait_ge(s["ln_src"], u - 1)
                        for t in range(NT):
                            mm = pe.transpose(ps[:, 0, t * P:(t + 1) * P], src[:, t * P:(t + 1) * P], ident[:, :])
                        mm.then_inc(s["ln_tok"], 1)
                        pe.wait_ge(s["ln_norm"], u + 1)
                        for t in range(NT):
                            mm = pe.transpose(ps[:, 0, 256 + t * P:256 + (t + 1) * P], xn[:, t, :], ident[:, :])
                        mm.then_inc(s["ln_feat"], 1)

                    def narrow_qkv(use, w, src):
                        for i in range(2):
                            pe.matmul(ps[:, 2, i * T:(i + 1) * T], w[:, i * P:(i + 1) * P], src[:, :],
                                      start=True, stop=True)
                        for t in range(NT):
                            mm = pe.matmul(ps[:, 3, t * P:(t + 1) * P], src[:, t * P:(t + 1) * P], w[:, 2 * P:3 * P],
                                           start=True, stop=True)
                        mm.then_inc(s["qkv_mm"], 1)

                    def project(use, w):
                        pe.wait_ge(s["att_ready"], use + 1)
                        for t in range(NT):
                            mm = pe.transpose(ps[:, 2, t * P:(t + 1) * P], att[:, t, :], ident[:, :])
                        mm.then_inc(s["att_T"], 1)
                        pe.wait_ge(s["attT_sb"], use + 1)
                        pe.matmul(ps[:, 3, 0:T], w[:, :], attT[:, :], start=True, stop=True).then_inc(s["proj_mm"], 1)

                    layer_norm(0)
                    layer_norm(1)
                    pe.wait_ge(s["ln_out"], 2)
                    narrow_qkv(0, w0qkv_sb, zn)
                    pe.wait_ge(s["stacked"], 16 * len(TERMS))
                    for n in range(H0 // 2):
                        if n >= 2:
                            pe.wait_ge(s["sc_max"], n - 1)
                        for e in range(2):
                            for t in range(NT):
                                mm = pe.matmul(ps[:, 4 + 2 * (n % 2) + e, t * T:(t + 1) * T],
                                               stack[:, 2 * n + e, 0, t * P:(t + 1) * P], stack[:, 2 * n + e, 1, :],
                                               start=True, stop=True)
                        mm.then_inc(s["sc_mm"], 1)
                    pe.wait_ge(s["nm_ready"], 1)
                    for t in range(NT):
                        mm = pe.transpose(psb[0:2 * H0, t * P:(t + 1) * P],
                                          nmb[:, t, :, :].rearrange("p a h -> p (a h)"), identb[:, :])
                    mm.then_inc(s["nm_T"], 1)
                    pe.wait_ge(s["nm_sb"], 1)

                    def pv(n):
                        pe.wait_ge(s["st_exp"], n + 1)
                        for e in range(2):
                            for t in range(NT):
                                at = (t * H0 + 2 * n + e) * (HD + 1)
                                for k in range(NT):
                                    mm = pe.matmul(ps[:, 1, at:at + HD + 1], pT[:, n % 2, e, k, t * P:(t + 1) * P],
                                                   vaug[:, k, 2 * n + e, :], start=(k == 0), stop=(k == 1))
                        mm.then_inc(s["st_mm"], 1)

                    for n in range(H0 // 2):
                        if n < 2:
                            pe.wait_ge(s["sc_max"], 7 + n)
                        for e in range(2):
                            for k in range(NT):
                                o = ps[:, 4 + 2 * (n % 2) + e, k * T:(k + 1) * T]
                                pe.matmul(o, stack[:, 2 * n + e, 1, k * P:(k + 1) * P], stack[:, 2 * n + e, 0, :],
                                          start=True, stop=False)
                                mm = pe.matmul(o, sel[:, 2 * n + e, :], nmT[:, :], start=False, stop=True)
                        mm.then_inc(s["st_mm"], 1)
                        if n >= 1:
                            pv(n - 1)
                    pv(H0 // 2 - 1)
                    pe.matmul(ps[0:1, 2, 0:1], ident[:, 0:1], ident[:, 0:1], start=True, stop=True)\
                        .then_inc(s["pv_mm"], 1)
                    project(0, w0proj_sb)

                    layer_norm(2)
                    pe.wait_ge(s["hmean_ready"], 1)
                    pe.matmul(ps[:, 1, 0:NH], hmean[:, :], wr_sb[:, :], start=True, stop=True).then_inc(s["route_mm"], 1)
                    pe.wait_ge(s["wsel_in"], 16 * NA)
                    for j in range(2):
                        for i in range(2):
                            for e in range(2):
                                pe.matmul(ps[64 * e:64 * e + 64, 2 + i, j * T:(j + 1) * T],
                                          wsel[:, 2 * j + e, i * DA:(i + 1) * DA], h[:, :], start=True, stop=True)
                    for t in range(NT):
                        mm = pe.matmul(ps[:, 4, t * NA * DA:(t + 1) * NA * DA], h[:, t * P:(t + 1) * P],
                                       wsel[:, :, 2 * DA:3 * DA], start=True, stop=True)
                    mm.then_inc(s["fqkv_mm"], 1)
                    pe.wait_ge(s["f_qk"], 1)
                    pe.wait_ge(s["f_v"], 1)
                    for k in range(NA):
                        r = slice(64 * (k % 2), 64 * (k % 2) + 64)
                        for t in range(NT):
                            mm = pe.matmul(ps[:, 4 + k, t * T:(t + 1) * T], fq[r, k // 2, t * P:(t + 1) * P],
                                           fk[r, k // 2, :], start=True, stop=True)
                        mm.then_inc(s["fs_mm"], 1)
                    for k in range(NA):
                        pe.wait_ge(s["f_exp"], k + 1)
                        if k >= 2:
                            pe.wait_ge(s["f_Tsb"], k - 1)
                        for t in range(NT):
                            for c in range(NT):
                                mm = pe.transpose(ps[:, 2 + k % 2, (t * NT + c) * P:(t * NT + c + 1) * P],
                                                  fp[:, k, t, c * P:(c + 1) * P], ident[:, :])
                        mm.then_inc(s["f_T"], 1)
                    for k in range(NA):
                        pe.wait_ge(s["f_Tsb"], k + 1)
                        for t in range(NT):
                            for c in range(NT):
                                mm = pe.matmul(ps[:, 1, (t * NA + k) * DA:(t * NA + k + 1) * DA], fpT[:, k, t, c, :],
                                               fv[:, c, k, :], start=(c == 0), stop=(c == 1))
                    mm.then_inc(s["fo_mm"], 1)
                    pe.wait_ge(s["fo_ready"], 1)
                    for j in range(2):
                        for t in range(NT):
                            mm = pe.transpose(ps[:, 2, j * T + t * P:j * T + (t + 1) * P],
                                              fo[:, t, 2 * j:2 * j + 2, :].rearrange("p a d -> p (a d)"), ident[:, :])
                    mm.then_inc(s["fo_T"], 1)
                    pe.wait_ge(s["foT_sb"], 1)
                    for j in range(2):
                        mm = pe.matmul(ps[:, 3, 0:T], wo0_sb[:, j, :], foT[:, j, :], start=(j == 0), stop=(j == 1))
                    mm.then_inc(s["fproj_mm"], 1)

                    layer_norm(3)
                    pe.wait_ge(s["ln_out"], 4)
                    narrow_qkv(1, w1qkv_sb, h)
                    pe.wait_ge(s["phi_ready"], 1)
                    pe.transpose(ps[:, 1, 0:P], phi[:, 1, 0:P], ident[:, :]).then_inc(s["kT_ps"], 1)
                    pe.wait_ge(s["knat_sb"], 1)
                    pe.wait_ge(s["v_ready"], 2)
                    pe.matmul(ps[:, 3, 0:H0 * (HD + 1)], knat[:, :], vaug[:, 0, :, :].rearrange("p h d -> p (h d)"),
                              start=True, stop=True).then_inc(s["state_mm"], 1)
                    pe.wait_ge(s["state_sb"], 1)
                    pe.matmul(ps[:, 3, T:T + H0 * (HD + 1)], phi[:, 0, P:T], state[:, :], start=True, stop=True)\
                        .then_inc(s["inter_mm"], 1)
                    pe.wait_ge(s["stacked"], 2 * 16 * len(TERMS))

                    def lin_pv(n):
                        pe.wait_ge(s["lin_masked"], n + 1)
                        for e in range(4):
                            for t in range(NT):
                                at = (t * H0 + 4 * n + e) * (HD + 1)
                                mm = pe.matmul(ps[:, 1, at:at + HD + 1], masked[:, n % 2, e, t, :],
                                               vaug[:, t, 4 * n + e, :], start=True, stop=True)
                        mm.then_inc(s["lin_mm"], 1)

                    for n in range(H0 // 4):
                        if n >= 2:
                            pe.wait_ge(s["lin_masked"], n - 1)
                        for e in range(4):
                            for t in range(NT):
                                mm = pe.matmul(ps[:, 4 + 2 * (n % 2) + e // 2, (e % 2) * T + t * P:(e % 2) * T + (t + 1) * P],
                                               stack[:, 4 * n + e, 1, t * P:(t + 1) * P],
                                               stack[:, 4 * n + e, 0, t * P:(t + 1) * P], start=True, stop=True)
                        mm.then_inc(s["lin_mm"], 1)
                        if n >= 1:
                            lin_pv(n - 1)
                    lin_pv(3)
                    project(1, w1o_sb)

                    layer_norm(4)
                    for l in range(DEPTH):
                        pe.wait_ge(s["y_ready"], l + 1)
                        for t in range(NT):
                            for i in range(3):
                                pe.matmul(ps[:, 2 + 3 * t + i, :], ysh[:, t * P:(t + 1) * P],
                                          wqkv_sb[:, l, i * INNER:(i + 1) * INNER], start=True, stop=True)\
                                    .then_inc(s["lqkv_mm"], 1)
                        for n in range(4):
                            i, half = n // 2, n % 2
                            pe.wait_ge(s["l_rot"], 2 * l + i + 1)
                            if n == 0:
                                pe.wait_ge(s["l_v"], 2 * (l + 1))
                                pe.wait_ge(s["l_sq"], 4 * (l + 1))
                            for j in range(2):
                                for t in range(NT):
                                    c = (2 * half + j) * 2
                                    mm = pe.transpose(ps[:, 2 + n, j * T + t * P:j * T + (t + 1) * P],
                                                      r1[:, i, t, c:c + 2, :].rearrange("p a d -> p (a d)"),
                                                      ident[:, :])
                            mm.then_inc(s["l_T"], 1)
                        for e in range(LH):
                            if e == 0:
                                pe.wait_ge(s["l_Tsb"], 4 * (l + 1))
                            if e >= 4:
                                pe.wait_ge(s["l_exp"], LH * l + e - 3)
                            o = ps[:, 4 + e % 4, 0:SW]
                            r = slice(64 * (e % 2), 64 * (e % 2) + 64)
                            pe.matmul(o[:, 0:P], identb[:, :], band[:, 0:P], start=True, stop=False)
                            pe.matmul(o[:, 0:P], qkT[r, 0, e // 2, 0:P], qkT[r, 1, e // 2, 0:P],
                                      start=False, stop=True)
                            pe.matmul(o[:, P:SW], identb[:, :], band[:, P:SW], start=True, stop=False)
                            pe.matmul(o[:, P:SW], qkT[r, 0, e // 2, P:T], qkT[r, 1, e // 2, P - WINDOW:T],
                                      start=False, stop=True).then_inc(s["ls_mm"], 1)
                        for e in range(LH):
                            pe.wait_ge(s["l_exp"], LH * l + e + 1)
                            if e >= 2:
                                pe.wait_ge(s["l_pTsb"], LH * l + e - 1)
                            for c in range(3):
                                mm = pe.transpose(ps[:, 2 + e % 2, c * P:(c + 1) * P], lp[:, e, c * P:(c + 1) * P],
                                                  ident[:, :])
                            mm.then_inc(s["l_pT"], 1)
                        for e in range(LH):
                            pe.wait_ge(s["l_pTsb"], LH * l + e + 1)
                            d = slice(e * LD, (e + 1) * LD)
                            pe.matmul(ps[:, 4, d], lpT[:, e, 0:P], lv[:, 0, d], start=True, stop=True)
                            pe.matmul(ps[:, 5, d], lpT[:, e, P:2 * P], lv[:, 0, d], start=True, stop=False)
                            mm = pe.matmul(ps[:, 5, d], lpT[:, e, 2 * P:3 * P], lv[:, 1, d], start=False, stop=True)
                        mm.then_inc(s["lo_mm"], 1)
                        pe.wait_ge(s["lo_ready"], l + 1)
                        for j in range(4):
                            for t in range(NT):
                                mm = pe.transpose(ps[:, 6 + j // 2, (j % 2) * T + t * P:(j % 2) * T + (t + 1) * P],
                                                  lo[:, t, j * P:(j + 1) * P], ident[:, :])
                        mm.then_inc(s["lo_T"], 1)
                        pe.wait_ge(s["loT_sb"], l + 1)
                        for j in range(4):
                            mm = pe.matmul(ps[:, 2, 0:T], wo_sb[:, l, j, :], loT[:, j, :], start=(j == 0), stop=(j == 3))
                        mm.then_inc(s["lproj_mm"], 1)
                        layer_norm(5 + l)
                        pe.wait_ge(s["ln_out"], 6 + l)
                        for j in range(3):
                            for i in range(2):
                                at = i * HID + j * P
                                mm = pe.matmul(ps[0:HT[j], 3 + j, i * T:(i + 1) * T], w1_sb[:, l, at:at + HT[j]],
                                               h[:, :], start=True, stop=True)
                            mm.then_inc(s["up_mm"], 1)
                        pe.wait_ge(s["ug_ready"], 3 * (l + 1))
                        for j in range(3):
                            mm = pe.matmul(ps[:, 6, 0:T], w2_sb[0:HT[j], l, j, :], ug[0:HT[j], j, :],
                                           start=(j == 0), stop=(j == 2))
                        mm.then_inc(s["down_mm"], 1)

                @block.scalar
                def _(act):
                    n = [0]

                    def link(ins):
                        n[0] += 1
                        ins.then_inc(s["act_chain"], 1)
                        act.wait_ge(s["act_chain"], n[0])

                    def layer_norm(u):
                        act.wait_ge(s["ln_stat"], u + 1)
                        link(act.activation(lnv[:, :], mv[:, :, 1], ACT.Ln, bias=eps[:, :]))
                        act.activation(rstd[:, :], lnv[:, :], ACT.Exp, scale=-0.5).then_inc(s["ln_rstd"], 1)

                    def project(use):
                        act.wait_ge(s["att_T"], use + 1)
                        act.activation(attT[:, :], ps[:, 2, 0:T], ACT.Copy).then_inc(s["attT_sb"], 1)

                    layer_norm(0)
                    layer_norm(1)
                    act.wait_ge(s["qkv_mm"], 1)
                    act.activation(part[:, 0:4:3, :], ps[:, 2, :].rearrange("p (i t) -> p i t", i=2), ACT.Copy)\
                        .then_inc(s["part0"], 1)
                    act.wait_ge(s["nm_T"], 1)
                    act.activation(nmT[:, :], psb[0:2 * H0, 0:T], ACT.Copy).then_inc(s["nm_sb"], 1)
                    for k in range(H0 // 2):
                        act.wait_ge(s["st_mm"], 1 if k == 0 else 2 * k)
                        if k >= 2:
                            act.wait_ge(s["st_mm"], 2 * k - 1)
                        act.activation(pT[:, k % 2, :, :, :].rearrange("p e k t -> p (e k t)"),
                                       ps[:, 4 + 2 * (k % 2):6 + 2 * (k % 2), :].rearrange("p a b -> p (a b)"),
                                       ACT.Exp).then_inc(s["st_exp"], 1)
                    project(0)

                    layer_norm(2)
                    act.wait_ge(s["lmax_ready"], 1)
                    act.activation(dist[:, :], logit[:, :], ACT.Exp, bias=lmax[:, :]).then_inc(s["dexp"], 1)
                    act.wait_ge(s["top_ready"], 2)
                    act.activation(ge[:, 0:NA], top[:, 0:NA], ACT.Exp, bias=ntop[:, :]).then_inc(s["gexp"], 1)
                    act.activation(ge[:, NA:NA + 1], ntop[:, :], ACT.Exp).then_inc(s["gexp"], 1)
                    act.wait_ge(s["fqkv_mm"], 1)
                    act.activation(fv[:, :, :, :].rearrange("p t k d -> p (t k d)"), ps[:, 4, :], ACT.Copy)\
                        .then_inc(s["f_v"], 1)
                    for k in range(NA):
                        act.wait_ge(s["f_max"], k + 1)
                        for t in range(NT):
                            ins = act.activation(fp[:, k, t, :], ps[:, 4 + k, t * T:(t + 1) * T], ACT.Exp,
                                                 bias=fnm[:, k, t:t + 1], accum_out=fs[:, k, t:t + 1])
                        ins.then_inc(s["f_exp"], 1)

                    layer_norm(3)
                    act.wait_ge(s["phi_min"], 1)
                    act.activation(phe[:, :, :], phe[:, :, :], ACT.Exp).then_inc(s["phi_exp"], 1)
                    act.wait_ge(s["kT_ps"], 1)
                    act.activation(knat[:, :], ps[:, 1, 0:P], ACT.Copy).then_inc(s["knat_sb"], 1)
                    act.wait_ge(s["phi_ready"], 1)
                    act.activation(part[:, 0:4:3, :], phi[:, :, :], ACT.Copy).then_inc(s["part0"], 1)
                    act.wait_ge(s["inter_mm"], 1)
                    act.activation(inter[:, :], ps[:, 3, T:T + H0 * (HD + 1)], ACT.Copy).then_inc(s["inter_sb"], 1)
                    project(1)

                    layer_norm(4)
                    for l in range(DEPTH):
                        for t in range(NT):
                            for i in range(2):
                                act.wait_ge(s["lqkv_mm"], 6 * l + 3 * t + i + 1)
                                src = ps[:, 2 + 3 * t + i, :]
                                act.activation(qk[:, i, t, :, :].rearrange("p h d -> p (h d)"), src, ACT.Copy)\
                                    .then_inc(s["l_copied"], 1)
                                act.activation(sq[:, i, t, :, :].rearrange("p h d -> p (h d)"), src, ACT.Square)\
                                    .then_inc(s["l_sq"], 1)
                            act.wait_ge(s["lqkv_mm"], 6 * l + 3 * t + 3)
                            act.activation(lv[:, t, :], ps[:, 4 + 3 * t, :], ACT.Copy).then_inc(s["l_v"], 1)
                        act.wait_ge(s["l_ss"], l + 1)
                        link(act.activation(lss[:, :, :, :], ss[:, :, :, :], ACT.Ln, scale=float(2 ** RSTD_SHIFT)))
                        act.activation(rn[:, :, :, :], lss[:, :, :, :], ACT.Exp, scale=-0.5, bias=shift[:, :])\
                            .then_inc(s["l_rn"], 1)
                        for k in range(4):
                            act.wait_ge(s["l_T"], 4 * l + k + 1)
                            act.activation(qkT[:, k // 2, 2 * (k % 2):2 * (k % 2) + 2, :].rearrange("p j t -> p (j t)"),
                                           ps[:, 2 + k, :], ACT.Copy).then_inc(s["l_Tsb"], 1)
                        for e in range(LH):
                            act.wait_ge(s["l_max"], LH * l + e + 1)
                            act.activation(lp[:, e, 0:P], ps[:, 4 + e % 4, 0:P], ACT.Exp, bias=lnm[:, e, 0:1],
                                           accum_out=ls[:, e, 0:1])
                            act.activation(lp[:, e, P + P - WINDOW:PW], ps[:, 4 + e % 4, P:SW], ACT.Exp,
                                           bias=lnm[:, e, 1:2], accum_out=ls[:, e, 1:2]).then_inc(s["l_exp"], 1)
                        act.wait_ge(s["lo_T"], l + 1)
                        act.activation(loT[:, :, :].rearrange("p j t -> p (j t)"),
                                       ps[:, 6:8, :].rearrange("p a b -> p (a b)"), ACT.Copy).then_inc(s["loT_sb"], 1)
                        layer_norm(5 + l)
                        for j in range(3):
                            act.wait_ge(s["up_mm"], 3 * l + j + 1)
                            act.activation(gel[0:HT[j], j, :], ps[0:HT[j], 3 + j, T:2 * T], ACT.Gelu,
                                           bias=V(f"b1g{j}_", l)[0:HT[j], :]).then_inc(s["gelu_done"], 1)

                @block.vector
                def _(dve):
                    n = [0]

                    def link(ins):
                        n[0] += 1
                        ins.then_inc(s["dve_chain"], 1)
                        dve.wait_ge(s["dve_chain"], n[0])

                    def layer_norm(u, dst, scale, bias):
                        dve.wait_ge(s["ln_tok"], u + 1)
                        for t in range(NT):
                            ins = dve.bn_stats(stats[:, t, :], ps[:, 0, t * P:(t + 1) * P])
                        link(ins)
                        for t in range(NT):
                            ins = dve.bn_aggr(mv[:, t, :], stats[:, t, :])
                        ins.then_inc(s["ln_stat"], 1)
                        dve.wait_ge(s["ln_rstd"], u + 1)
                        for t in range(NT):
                            ins = dve.tensor_scalar(xn[:, t, :], ps[:, 0, t * P:(t + 1) * P], mv[:, t, 0:1],
                                                    rstd[:, t:t + 1], ALU.subtract, ALU.mult)
                        ins.then_inc(s["ln_norm"], 1)
                        dve.wait_ge(s["ln_feat"], u + 1)
                        dve.tensor_scalar(dst, ps[:, 0, 256:512], scale, bias, ALU.mult, ALU.add)\
                            .then_inc(s["ln_out"], 1)
                        dve.wait_ge(s["ln_out"], u + 1)

                    def split(use, src):
                        dve.wait_ge(s["part0"], use + 1)
                        dve.tensor_tensor(rem[:, :, :], src, part[:, 0:4:3, :], ALU.subtract).then_inc(s["part1_r"], 1)
                        dve.wait_ge(s["part1"], use + 1)
                        dve.tensor_tensor(part[:, 2:6:3, :], rem[:, :, :], part[:, 1:5:3, :], ALU.subtract)\
                            .then_inc(s["part2"], 1)

                    dve.tensor_copy(m[:, :], mod[:, :, bass.ds(b, 1)].rearrange("p a b -> p (a b)"))\
                        .then_inc(s["m_ready"], 1)
                    dve.wait_ge(s["m_ready"], 1)
                    dve.wait_ge(s["x_in"], 16)
                    layer_norm(0, h[:, :], m[:, 1:2], m[:, 0:1])
                    layer_norm(1, zn[:, :], V("ln_scale"), V("ln_bias"))
                    dve.wait_ge(s["qkv_mm"], 1)
                    split(0, ps[:, 2, :].rearrange("p (i t) -> p i t", i=2))
                    dve.tensor_copy(vaug[:, :, :, 0:HD],
                                    ps[:, 3, 0:T].rearrange("p (t h d) -> p t h d", t=NT, h=H0)).then_inc(s["v_ready"], 1)
                    for k in range(H0 // 2):
                        dve.wait_ge(s["sc_mm"], k + 1)
                        dve.tensor_reduce(nmax[:, 0, 2 * k:2 * k + 2, :],
                                          ps[:, 4 + 2 * (k % 2):6 + 2 * (k % 2), :].rearrange("p a (t j) -> p a t j", t=NT),
                                          AX.X, ALU.max, negate=True).then_inc(s["sc_max"], 1)
                    dve.wait_ge(s["sc_max"], 8)
                    neg = nmax[:, 0, :, :].rearrange("p h t -> p t h")
                    link(dve.tensor_copy(nmb[:, :, 0, :], neg))
                    dve.tensor_tensor(nmb[:, :, 1, :], neg, nmb[:, :, 0, :], ALU.subtract).then_inc(s["nm_ready"], 1)

                    def narrow_out(use):
                        o = ps[:, 1, 0:NT * H0 * (HD + 1)].rearrange("p (t h d) -> p t h d", t=NT, h=H0)
                        if use == 0:
                            link(dve.reciprocal(rsum[:, :, :], o[:, :, :, HD]))
                        else:
                            later = ps[:, 1, H0 * (HD + 1):2 * H0 * (HD + 1)]
                            link(dve.tensor_tensor(later, later, inter[:, :], ALU.add))
                            link(dve.tensor_scalar(den[:, :, :], o[:, :, :, HD], 1e-6, None, ALU.add))
                            link(dve.reciprocal(rsum[:, :, :], den[:, :, :]))
                        dve.tensor_tensor(att[:, :, :].rearrange("p t (h d) -> p t h d", h=H0), o[:, :, :, 0:HD],
                                          rsum[:, :, :, None].broadcast_to([P, NT, H0, HD]), ALU.mult)\
                            .then_inc(s["att_ready"], 1)

                    dve.wait_ge(s["st_mm"], H0)
                    narrow_out(0)
                    dve.wait_ge(s["proj_mm"], 1)
                    link(dve.scalar_tensor_tensor(res[:, :], ps[:, 3, 0:T], V("b_proj"), h[:, :], ALU.add, ALU.add))
                    dve.scalar_tensor_tensor(x[:, :], res[:, :], m[:, 2:3], x[:, :], ALU.mult, ALU.add)\
                        .then_inc(s["ln_src"], 1)

                    layer_norm(2, h[:, :], m[:, 4:5], m[:, 3:4])
                    link(dve.reduce_sum(hsum[:, :], h[:, :], AX.X))
                    dve.tensor_scalar(hmean[:, :], ones[:, :], hsum[:, :], 1.0 / T, ALU.mult, ALU.mult)\
                        .then_inc(s["hmean_ready"], 1)
                    dve.wait_ge(s["route_mm"], 1)
                    link(dve.tensor_tensor(logit[:, :], ps[:, 1, 0:NH], row[:, 0:NH], ALU.add))
                    dve.tensor_reduce(lmax[:, :], logit[:, :], AX.X, ALU.max, negate=True).then_inc(s["lmax_ready"], 1)
                    dve.wait_ge(s["dexp"], 1)
                    link(dve.reduce_sum(dsum[:, :], dist[:, :], AX.X))
                    link(dve.reciprocal(drec[:, :], dsum[:, :]))
                    link(dve.tensor_scalar(dist[:, :], dist[:, :], drec[:, :], None, ALU.mult))
                    link(dve.max(top[:, :], dist[:, :]))
                    dve.max_index(tidx[:, :], top[:, :], dist[:, :]).then_inc(s["top_ready"], 1)
                    dve.tensor_scalar(ntop[:, :], top[:, 0:1], -1.0, None, ALU.mult).then_inc(s["top_ready"], 1)
                    dve.wait_ge(s["gexp"], 2)
                    link(dve.reduce_sum(gsum[:, :], ge[:, 0:NA], AX.X))
                    link(dve.scalar_tensor_tensor(gsum[:, :], ge[:, NA:NA + 1], float(NH - NA), gsum[:, :],
                                                  ALU.mult, ALU.add))
                    link(dve.reciprocal(grec[:, :], gsum[:, :]))
                    link(dve.tensor_scalar(g[:, :], ge[:, 0:NA], grec[:, :], None, ALU.mult))
                    dve.wait_ge(s["wsel_in"], 16 * NA)
                    for k in range(NA):
                        r = slice(64 * (k % 2), 64 * (k % 2) + 64)
                        dve.tensor_copy(gp[r, k // 2:k // 2 + 1], g[r, k:k + 1])
                        ins = dve.tensor_copy(bp[r, k // 2, :], wsel[r, k, 3 * DA:WC])
                    link(ins)
                    dve.tensor_scalar(gq[:, :], gp[:, :], float(DA) ** -0.5, None, ALU.mult)
                    link(dve.tensor_tensor(bvg[:, :], bp[:, :, 2], gp[:, :], ALU.mult))
                    dve.wait_ge(s["fqkv_mm"], 1)
                    for j in range(2):
                        dve.tensor_scalar(fq[:, j, :], ps[:, 2, j * T:(j + 1) * T], bp[:, j, 0:1], gq[:, j:j + 1],
                                          ALU.add, ALU.mult)
                        ins = dve.tensor_scalar(fk[:, j, :], ps[:, 3, j * T:(j + 1) * T], bp[:, j, 1:2], gp[:, j:j + 1],
                                                ALU.add, ALU.mult)
                    ins.then_inc(s["f_qk"], 1)
                    for k in range(NA):
                        dve.wait_ge(s["fs_mm"], k + 1)
                        dve.tensor_reduce(fnm[:, k, :], ps[:, 4 + k, :].rearrange("p (t j) -> p t j", t=NT),
                                          AX.X, ALU.max, negate=True).then_inc(s["f_max"], 1)
                    for k in range(NA):
                        dve.wait_ge(s["f_T"], k + 1)
                        dve.tensor_copy(fpT[:, k, :, :, :].rearrange("p t c q -> p (t c q)"), ps[:, 2 + k % 2, :])\
                            .then_inc(s["f_Tsb"], 1)
                    link(dve.reciprocal(fr[:, :, :], fs[:, :, :]))
                    link(dve.tensor_tensor(fr[:, :, :], fr[:, :, :], g[:, :, None].broadcast_to([P, NA, NT]), ALU.mult))
                    dve.wait_ge(s["fo_mm"], 1)
                    dve.tensor_tensor(fo[:, :, :, :], ps[:, 1, :].rearrange("p (t k d) -> p t k d", t=NT, k=NA),
                                      fr[:, :, :, None].rearrange("p k t o -> p t k o").broadcast_to([P, NT, NA, DA]),
                                      ALU.mult).then_inc(s["fo_ready"], 1)
                    dve.wait_ge(s["fo_T"], 1)
                    for j in range(2):
                        ins = dve.tensor_scalar(foT[:, j, :], ps[:, 2, j * T:(j + 1) * T], bvg[:, j:j + 1], None, ALU.add)
                    ins.then_inc(s["foT_sb"], 1)
                    dve.wait_ge(s["fproj_mm"], 1)
                    link(dve.tensor_scalar(res[:, :], ps[:, 3, 0:T], V("bo0"), m[:, 5:6], ALU.add, ALU.mult))
                    dve.tensor_tensor(x[:, :], x[:, :], res[:, :], ALU.add).then_inc(s["ln_src"], 1)

                    layer_norm(3, h[:, :], m[:, 7:8], m[:, 6:7])
                    dve.wait_ge(s["qkv_mm"], 2)
                    for i, bias in enumerate(("bq1", "bk1")):
                        ins = dve.tensor_scalar(phe[:, i, :], ps[:, 2, i * T:(i + 1) * T], V(bias), 0.0, ALU.add, ALU.min)
                    ins.then_inc(s["phi_min"], 1)
                    for i, bias in enumerate(("bq1", "bk1")):
                        ins = dve.tensor_scalar(phi[:, i, :], ps[:, 2, i * T:(i + 1) * T], V(bias), 0.0, ALU.add, ALU.max)
                    link(ins)
                    dve.tensor_tensor(vaug[:, :, :, 0:HD],
                                      ps[:, 3, 0:T].rearrange("p (t h d) -> p t h d", t=NT, h=H0),
                                      row[:, None, NH:NH + P].rearrange("p o (h d) -> p o h d", h=H0)
                                      .broadcast_to([P, NT, H0, HD]), ALU.add).then_inc(s["v_ready"], 1)
                    dve.wait_ge(s["phi_exp"], 1)
                    dve.tensor_tensor(phi[:, :, :], phi[:, :, :], phe[:, :, :], ALU.add).then_inc(s["phi_ready"], 1)
                    dve.wait_ge(s["phi_ready"], 1)
                    split(1, phi[:, :, :])
                    dve.wait_ge(s["state_mm"], 1)
                    dve.tensor_tensor(state[:, :], ps[:, 3, 0:H0 * (HD + 1)], diag[:, :], ALU.mult)\
                        .then_inc(s["state_sb"], 1)
                    for k in range(H0 // 4):
                        dve.wait_ge(s["lin_mm"], 1 if k == 0 else 2 * k)
                        dve.tensor_tensor(masked[:, k % 2, :, :, :].rearrange("p e t q -> p (e t) q"),
                                          ps[:, 4 + 2 * (k % 2):6 + 2 * (k % 2), :].rearrange("p a (c q) -> p (a c) q", q=P),
                                          tri[:, None, :].broadcast_to([P, 8, P]), ALU.mult).then_inc(s["lin_masked"], 1)
                    dve.wait_ge(s["lin_mm"], 8)
                    dve.wait_ge(s["inter_sb"], 1)
                    narrow_out(1)
                    dve.wait_ge(s["proj_mm"], 2)
                    link(dve.tensor_scalar(res[:, :], ps[:, 3, 0:T], V("bo1"), m[:, 8:9], ALU.add, ALU.mult))
                    dve.tensor_tensor(x[:, :], x[:, :], res[:, :], ALU.add).then_inc(s["ln_src"], 1)

                    layer_norm(4, y[:, :], m[:, 10:11], m[:, 9:10])

                    def shift_tokens(signal):
                        dve.tensor_copy(ysh[0:64, :], y[0:64, :])
                        dve.memset(ysh[64:128, 0:1], 0.0)
                        dve.tensor_copy(ysh[64:128, 1:T], y[64:128, 0:T - 1]).then_inc(s[signal], 1)

                    for l in range(DEPTH):
                        shift_tokens("y_ready")
                        for t in range(NT):
                            for i in range(2):
                                k = 4 * l + 2 * t + i + 1
                                dve.wait_ge(s["l_sq"], k)
                                dve.reduce_sum(ss[:, i, t, :], sq[:, i, t, :, :], AX.X)
                                link(dve.tensor_tensor(
                                    r1[:, i, t, :, :], qk[:, i, t, :, :],
                                    wave[:, l, 2 * i, t, None, :].broadcast_to([P, LH, LD]), ALU.mult))
                        dve.tensor_scalar(ss[:, :, :, :], ss[:, :, :, :], 1e-24, None, ALU.max).then_inc(s["l_ss"], 1)
                        dve.wait_ge(s["l_r2"], l + 1)
                        link(dve.tensor_tensor(r1[:, :, :, :, :], r1[:, :, :, :, :], r2[:, :, :, :, :], ALU.add))
                        dve.wait_ge(s["l_rn"], l + 1)
                        for i in range(2):
                            dve.tensor_tensor(r1[:, i, :, :, :], r1[:, i, :, :, :],
                                              rn[:, i, :, :, None].broadcast_to([P, NT, LH, LD]), ALU.mult)\
                                .then_inc(s["l_rot"], 1)
                        for e in range(LH):
                            dve.wait_ge(s["ls_mm"], LH * l + e + 1)
                            dve.tensor_reduce(lnm[:, e, 0:1], ps[:, 4 + e % 4, 0:P], AX.X, ALU.max, negate=True)
                            dve.tensor_reduce(lnm[:, e, 1:2], ps[:, 4 + e % 4, P:SW], AX.X, ALU.max, negate=True)\
                                .then_inc(s["l_max"], 1)
                        for e in range(LH):
                            dve.wait_ge(s["l_pT"], LH * l + e + 1)
                            dve.tensor_copy(lpT[:, e, :], ps[:, 2 + e % 2, 0:PW]).then_inc(s["l_pTsb"], 1)
                        link(dve.reciprocal(lr[:, :, :], ls[:, :, :]))
                        dve.wait_ge(s["lo_mm"], l + 1)
                        for t in range(NT):
                            ins = dve.tensor_tensor(lo[:, t, :].rearrange("p (h d) -> p h d", h=LH),
                                                    ps[:, 4 + t, :].rearrange("p (h d) -> p h d", h=LH),
                                                    lr[:, :, t:t + 1].broadcast_to([P, LH, LD]), ALU.mult)
                        ins.then_inc(s["lo_ready"], 1)
                        dve.wait_ge(s["lproj_mm"], l + 1)
                        link(dve.tensor_tensor(y[:, :], y[:, :], ps[:, 2, 0:T], ALU.add))
                        shift_tokens("ln_src")
                        layer_norm(5 + l, h[:, :], V("ln_g", l), V("ln_b", l))
                        for j in range(3):
                            dve.wait_ge(s["gelu_done"], 3 * l + j + 1)
                            dve.scalar_tensor_tensor(ug[0:HT[j], j, :], ps[0:HT[j], 3 + j, 0:T],
                                                     V(f"b1a{j}_", l)[0:HT[j], :], gel[0:HT[j], j, :],
                                                     ALU.add, ALU.mult).then_inc(s["ug_ready"], 1)
                        dve.wait_ge(s["down_mm"], l + 1)
                        link(dve.scalar_tensor_tensor(y[:, :], ps[:, 6, 0:T], V("b2_", l), y[:, :], ALU.add, ALU.add))
                    dve.scalar_tensor_tensor(x[:, :], y[:, :], m[:, 11:12], x[:, :], ALU.mult, ALU.add)\
                        .then_inc(s["x_done"], 1)

            nc.all_engine_barrier(sems_to_clear=loop_sems)


def layout(inputs):
    import numpy as np
    f = np.float32
    A = {k: np.asarray(v) for k, v in inputs.items()}
    a = {}
    a["z"] = A["L0_attn_z"].transpose(0, 2, 1)
    a["cT"] = np.stack([A["L0_c"].T, A["L1_c"].T], 1)
    a["wmod"] = np.stack([A["L0_wmod"], A["L1_wmod"]], 1)
    w = A["L0_attn_w_qkv"].reshape(P, H0, HD, 3)
    dh = lambda u: u.transpose(0, 2, 1).reshape(u.shape[0], P)
    a["w0qkv"] = np.concatenate([dh(w[..., 0]), dh(w[..., 1]), w[..., 2].reshape(P, P)], 1)
    a["w0proj"] = A["L0_attn_w_proj"]
    a["wr"] = A["L0_ffn_Wr"]
    pk = [A["L0_ffn_" + n].reshape(P, NH, DA).transpose(1, 0, 2) for n in ("Wq", "Wk", "Wv")]
    pb = [np.concatenate([A["L0_ffn_" + n].reshape(NH, DA, 1)] * 2, 1) for n in ("bq", "bk", "bv")]
    a["wpack"] = np.concatenate(pk + pb, 2)
    a["wo0"] = A["L0_ffn_Wo"]
    a["w1qkv"] = np.concatenate([dh(A["L1_attn_Wq"].T.reshape(P, H0, HD)), dh(A["L1_attn_Wk"].T.reshape(P, H0, HD)),
                                 A["L1_attn_Wv"].T], 1)
    a["w1o"] = A["L1_attn_Wo"].T
    a["wqkv"], a["wo"], a["w1"], a["w2"] = (A["L1_ffn_" + n] for n in ("wqkv", "wo", "w1", "w2"))
    pad = lambda u: np.concatenate([u, np.zeros(3 * P - HID, f)]).reshape(3, P)
    col = {"ln_scale": A["L0_attn_ln_scale"], "ln_bias": A["L0_attn_ln_bias"], "b_proj": A["L0_attn_b_proj"],
           "bo0": A["L0_ffn_bo"], "bo1": A["L1_attn_bo"],
           "bq1": A["L1_attn_bq"].reshape(H0, HD).T.reshape(P), "bk1": A["L1_attn_bk"].reshape(H0, HD).T.reshape(P)}
    for l in range(DEPTH):
        col[f"ln_g{l}"], col[f"ln_b{l}"], col[f"b2_{l}"] = A["L1_ffn_ln_g"][l], A["L1_ffn_ln_b"][l], A["L1_ffn_b2"][l]
        for j in range(3):
            col[f"b1a{j}_{l}"] = pad(A["L1_ffn_b1"][l][:HID])[j]
            col[f"b1g{j}_{l}"] = pad(A["L1_ffn_b1"][l][HID:])[j]
    a["vecs"] = np.stack([col[n] for n in VEC], 1)
    swap = lambda u: np.concatenate([u[LD // 2:], u[:LD // 2]])
    flat = [A["L0_ffn_br"], A["L1_attn_bv"]]
    for l in range(DEPTH):
        q, k = A["L1_ffn_q_scale"][l], A["L1_ffn_k_scale"][l]
        flat += [q, swap(q), k, swap(k)]
    a["rows"] = np.broadcast_to(np.concatenate(flat)[None], (P, ROWS))
    a["ident_in"] = np.eye(P, dtype=f)
    i = np.arange(P)
    a["tri_in"] = (i[None, :] >= i[:, None]).astype(f)
    a["diag_in"] = np.repeat((i[:, None] % H0 == np.arange(H0)[None, :]), HD + 1, 1).astype(f)
    a["sel_in"] = np.repeat(np.arange(2 * H0)[:, None] % H0 == np.arange(H0)[None, :], P, 1).astype(f)
    c = np.arange(P + WINDOW)
    t0 = (i[None, :] > i[:, None]) | (i[:, None] > i[None, :] + WINDOW)
    t1 = (c[None, :] > i[:, None] + WINDOW) | (c[None, :] < i[:, None])
    a["band_in"] = (np.concatenate([t0, t1], 1) * NEG).astype(f)
    half = np.arange(0, LD, 2, dtype=f)
    inv = (f(1) / f(10000) ** (half / f(LD))).astype(f)
    t = np.arange(T, dtype=f)
    fr = np.concatenate([t[:, None] * inv[None]] * 2, 1)
    base = (half + f(0.4 * LD)) / f(1.4 * LD)
    sc = np.concatenate([base[None] ** ((t - T // 2) / f(WINDOW // 2))[:, None]] * 2, 1)
    sg = np.where(np.arange(LD) < LD // 2, -1, 1).astype(f)[None]
    tabs = np.stack([np.cos(fr) * sc, np.sin(fr) * sg * sc, np.cos(fr) / sc, np.sin(fr) * sg / sc]).astype(f)
    a["rot_in"] = tabs.reshape(4, NT, P, LD).transpose(2, 0, 1, 3)
    return {k: np.ascontiguousarray(v, dtype=f) for k, v in a.items()}


_IN = ["z", "cT", "wmod", "w0qkv", "w0proj", "wr", "wpack", "wo0", "w1qkv", "w1o", "wqkv", "wo", "w1", "w2",
       "vecs", "rows", "ident_in", "tri_in", "diag_in", "sel_in", "band_in", "rot_in"]


def kernel(**inputs):
    import numpy as np
    import concourse.bacc as bacc
    from concourse.bass_utils import run_bass_kernel_spmd

    arrays = layout(inputs)
    nc = bacc.Bacc("TRN2", target_bir_lowering=False, num_devices=1)
    args = [nc.dram_tensor(n, arrays[n].shape, F32, kind="ExternalInput").ap() for n in _IN]
    out = nc.dram_tensor("out", (NB, P, T), F32, kind="ExternalOutput").ap()
    program(nc, *args, out)
    r = run_bass_kernel_spmd(nc, [arrays], core_ids=[0])
    return np.ascontiguousarray(r.results[0]["out"].transpose(0, 2, 1))
```

```python
from contextlib import ExitStack

import concourse.bass as bass
from concourse import mybir

F32 = mybir.dt.float32
BF16 = mybir.dt.bfloat16
U32 = mybir.dt.uint32
ACT = mybir.ActivationFunctionType
ALU = mybir.AluOpType
AX = mybir.AxisListType

P = 128
NB = 16
T = 256
NT = T // P
H0 = 16
HD = P // H0
TERMS = ((0, 0), (1, 1), (0, 1), (1, 0), (0, 2), (2, 0))
KS = HD * len(TERMS)
NH = 16
NA = 4
DA = 64
WC = 3 * DA + 3
DEPTH = 2
LH = 8
LD = 64
INNER = LH * LD
WINDOW = 64
HID = 341
HT = (128, 128, 85)
SW = P + P + WINDOW
PW = P + 2 * P
RING = 4
NEG = -3.0e38
LN_EPS = 1e-5
RSTD_SHIFT = 16

VEC = {n: i for i, n in enumerate(
    ["ln_scale", "ln_bias", "b_proj", "bo0", "bq1", "bk1", "bo1"]
    + [f"{n}{l}" for l in range(DEPTH) for n in
       ("ln_g", "ln_b", "b2_", "b1a0_", "b1a1_", "b1a2_", "b1g0_", "b1g1_", "b1g2_")])}
NV = len(VEC)
ROWS = 16 + P + DEPTH * 4 * LD


def norm_steps(u):
    return [f"ln{u}.{n}" for n in ("tok", "stat", "rstd", "norm", "feat", "out")]


STEPS = {
    "a": ["in"] + norm_steps(0) + norm_steps(1) + ["qkv", "part0", "part1r", "part1", "part2", "stack"]
    + [f"max{k}" for k in range(H0 + 2)] + ["nm", "nmT", "nmsb"] + [f"st{k}" for k in range(H0 + 3)]
    + ["att", "attT", "attTsb", "proj", "add"],
    "b": ["in"] + norm_steps(0) + ["hmean", "route", "lmax", "dexp", "top", "gexp", "g", "fqk", "fqk_sb", "fv", "fv_sb"]
    + [f"f{r}.{k}" for r in range(2) for k in range(6)] + ["fo", "fo_sb", "fo_T", "foT_sb", "fproj", "fadd"]
    + norm_steps(1) + ["qkv", "phi0", "phi1", "phi2", "kT", "part1r", "part1", "part2", "stack", "state", "inter"]
    + [f"lin{k}" for k in range(2 * H0 // 2 + 2)] + ["att", "attT", "attTsb", "proj", "add"],
    "c": ["in"] + norm_steps(0)
    + [f"{l}.{n}" for l in range(DEPTH) for n in
       [f"q{k}" for k in range(12)] + [f"x{k}" for k in range(6)] + [f"h{k}" for k in range(LH + 4)]
       + ["o0", "o1", "o2", "oT", "oTsb", "proj", "y"] + norm_steps(1 + l)
       + ["up0", "up1", "up2", "gelu", "ug", "down", "add"]] + ["done"],
}


def turns(active):
    order = [((i + 0.5) / len(STEPS[k]), k, step) for k in active for i, step in enumerate(STEPS[k])]
    return [(k, step) for _, k, step in sorted(order)]


def take_turns(active, streams):
    at = {k: next(streams[k], None) for k in active}
    for k, step in turns(active):
        while at[k] == step:
            at[k] = next(streams[k], None)
    assert not any(at.values()), at


def program(nc, z, cT, wmod, w0qkv, w0proj, wr, wpack, wo0, w1qkv, w1o, wqkv, wo, w1, w2,
            vecs, rows, ident_in, tri_in, diag_in, sel_in, band_in, rot_in, out):
    with ExitStack() as ctx:
        def sb(name, shape, dt=F32):
            return ctx.enter_context(nc.sbuf_tensor(name, shape, dt))

        def sem(name):
            return ctx.enter_context(nc.semaphore(name))

        c_sb = sb("c_sb", [P, 2, NB])
        w0qkv_sb = sb("w0qkv_sb", [P, 3 * P])
        w0proj_sb = sb("w0proj_sb", [P, P])
        wr_sb = sb("wr_sb", [P, NH])
        wo0_sb = sb("wo0_sb", [P, 2, P])
        w1qkv_sb = sb("w1qkv_sb", [P, 3 * P])
        w1o_sb = sb("w1o_sb", [P, P])
        wqkv_sb = sb("wqkv_sb", [P, DEPTH, 3 * INNER])
        wo_sb = sb("wo_sb", [P, DEPTH, 4, P])
        w1_sb = sb("w1_sb", [P, DEPTH, 2 * HID])
        w2_sb = sb("w2_sb", [P, DEPTH, 3, P])
        vec = sb("vec", [P, NV])
        row = sb("row", [P, ROWS])
        ident = sb("ident", [P, P])
        tri = sb("tri", [P, P])
        diag = sb("diag", [P, H0 * (HD + 1)])
        bandf = sb("bandf", [P, SW])
        rot = sb("rot", [P, 4, NT, LD])
        identb = sb("identb", [P, P], BF16)
        sel = sb("sel", [2 * H0, H0, P], BF16)
        band = sb("band", [P, SW], BF16)
        ones = sb("ones", [P, P])
        eps = sb("eps", [P, 1])
        shift = sb("shift", [P, 1])
        wave = sb("wave", [P, DEPTH, 4, NT, LD])
        silu = sb("silu", [P, 2, NB])
        stmp = sb("stmp", [P, 2, NB])
        mod = sb("mod", [P, 12, NB])
        sgn = sb("sgn", [P, NB])
        mag = sb("mag", [P, NB])

        def norm_buffers(k):
            return {"xn": sb(k + "_xn", [P, NT, P]), "stats": sb(k + "_stats", [P, NT, 6]), "mv": sb(k + "_mv", [P, NT, 2]),
                    "lnv": sb(k + "_lnv", [P, NT]), "rstd": sb(k + "_rstd", [P, NT])}

        norm = {k: norm_buffers(k) for k in "abc"}
        m = {k: sb(k + "_m", [P, 12]) for k in "abc"}
        x_in = sb("x_in", [P, T])
        x_ab = sb("x_ab", [P, T])
        x_b = sb("x_b", [P, T])
        x_bc = sb("x_bc", [P, T])
        x_c = sb("x_c", [P, T])
        ha = sb("ha", [P, T])
        zn = sb("zn", [P, T])
        hb = sb("hb", [P, T])
        hc = sb("hc", [P, T])
        res_a = sb("res_a", [P, T])
        res_b = sb("res_b", [P, T])

        def narrow_buffers(k):
            return {"part": sb(k + "_part", [P, 6, T], BF16),
                    "rem": sb(k + "_rem", [P, 2, T]), "vaug": sb(k + "_vaug", [P, NT, H0, HD + 1]),
                    "stack": sb(k + "_stack", [KS, H0, 2, T], BF16), "rsum": sb(k + "_rsum", [P, NT, H0]),
                    "att": sb(k + "_att", [P, NT, P]), "attT": sb(k + "_attT", [P, T])}

        narrow = {k: narrow_buffers(k) for k in "ab"}
        nmax = sb("nmax", [P, H0, NT])
        nmb = sb("nmb", [P, NT, 2, H0], BF16)
        nmT = sb("nmT", [2 * H0, T], BF16)
        pT = sb("pT", [P, 2, NT, T])

        phi = sb("phi", [P, 2, T])
        phe = sb("phe", [P, 2, T])
        den = sb("den", [P, NT, H0])
        knat = sb("knat", [P, P])
        inter = sb("inter", [P, H0 * (HD + 1)])
        state = sb("state", [P, H0 * (HD + 1)])
        hsum = sb("hsum", [P, 1])
        hmean = sb("hmean", [P, P])
        logit = sb("logit", [P, NH])
        lmax = sb("lmax", [P, 1])
        dist = sb("dist", [P, NH])
        dsum = sb("dsum", [P, 1])
        drec = sb("drec", [P, 1])
        top = sb("top", [P, 8])
        tidx = sb("tidx", [P, 8], U32)
        ntop = sb("ntop", [P, 1])
        ge = sb("ge", [P, NA + 1])
        gsum = sb("gsum", [P, 1])
        grec = sb("grec", [P, 1])
        g = sb("g", [P, NA])
        wsel = sb("wsel", [P, NA, WC])
        gp = sb("gp", [P, 2])
        gq = sb("gq", [P, 2])
        bp = sb("bp", [P, 2, 3])
        bvg = sb("bvg", [P, 2])
        fq = sb("fq", [P, 2, T])
        fk = sb("fk", [P, 2, T])
        fv = sb("fv", [P, NT, NA, DA])
        fnm = sb("fnm", [P, NA, NT])
        fs = sb("fs", [P, NA, NT])
        fr = sb("fr", [P, NA, NT])
        fp = sb("fp", [P, 2, NT, T])
        fpT = sb("fpT", [P, NA, NT, NT, P])
        fo = sb("fo", [P, NT, NA, DA])
        foT = sb("foT", [P, 2, T])

        y = sb("y", [P, T + 1])
        HALVES = ((slice(0, P // 2), slice(0, T)), (slice(P // 2, P), slice(1, T + 1)))
        qk = sb("qk", [P, 2, NT, LH, LD])
        sq = sb("sq", [P, 2, LH, LD])
        ss = sb("ss", [P, 2, NT, LH])
        lss = sb("lss", [P, 2, NT, LH])
        rn = sb("rn", [P, 2, NT, LH])
        r1 = sb("r1", [P, 2, NT, LH, LD])
        r2 = sb("r2", [P, 2, LH, LD])
        qkT = sb("qkT", [P, 2, 4, T])
        lv = sb("lv", [P, NT, INNER])
        lnm = sb("lnm", [P, LH, NT])
        ls = sb("ls", [P, LH, NT])
        lr = sb("lr", [P, LH, NT])
        lp = sb("lp", [P, RING, PW])
        lpT = sb("lpT", [P, LH, PW])

        ps = ctx.enter_context(nc.psum_tensor("ps", [P, 8, 512], F32))
        psb = ps[:, 0, :].bitcast(BF16)

        wmod_sb = qk[:, :, :, :, :].rearrange("p i t h d -> p (i t h d)")[:, 0:12 * P].rearrange("p (l n) -> p l n", l=2)
        self32 = lpT[0:2 * H0, :, :].rearrange("p h c -> p (h c)")[:, 0:H0 * P]

        masked = fpT[:, 0:2, :, :, :].rearrange("p k t c q -> p (k t c q)")\
            .rearrange("p (k e t q) -> p k e t q", k=2, e=2, t=NT)
        lo = r1[:, 0, :, :, :].rearrange("p t h d -> p t (h d)")
        loT = r1[:, 1, :, :, :].rearrange("p t h d -> p (t h d)").rearrange("p (j t) -> p j t", j=4)
        qk_flat = qk[:, :, :, :, :].rearrange("p i t h d -> p (i t h d)")
        gel = qk_flat[:, 0:3 * T].rearrange("p (j t) -> p j t", j=3)
        ug = qk_flat[:, 4 * T:7 * T].rearrange("p (j t) -> p j t", j=3)

        loaded = sem("loaded")
        pool_ready = sem("pool_ready")
        silu_e = sem("silu_e")
        silu_done = sem("silu_done")
        mod_mm = sem("mod_mm")
        set_chain = sem("set_chain")
        names = """dve_chain act_chain pool_chain
            a_x_in a_m a_ln_tok a_ln_stat a_ln_rstd a_ln_norm a_ln_feat a_ln_out
            a_qkv_mm a_part0 a_part1_r a_part1 a_part2 a_v a_stacked
            a_sc_mm a_sc_max a_nm a_nm_T a_nm_sb a_st_mm a_st_exp a_pv_mm
            a_att a_att_T a_attT_sb a_proj_mm a_done
            b_m b_ln_tok b_ln_stat b_ln_rstd b_ln_norm b_ln_feat b_ln_out
            b_hmean b_route_mm b_lmax b_dexp b_top b_gexp b_g b_wsel b_fqk_mm b_fqk b_fv_mm b_fv
            b_fs_mm b_fmax b_fexp b_fT b_fTsb b_fo_mm b_fo b_fo_T b_foT_sb b_fproj_mm b_mid
            b_qkv_mm b_phi_min b_phi_max b_phi_exp b_phi b_v b_kT b_knat b_part0 b_part1_r b_part1 b_part2 b_stacked
            b_state_mm b_state b_inter_mm b_inter b_lin_mm b_masked b_lpv_mm
            b_att b_att_T b_attT_sb b_proj_mm b_done
            c_m c_x c_ln_tok c_ln_stat c_ln_rstd c_ln_norm c_ln_feat c_ln_out c_y
            c_qkv_mm c_copied c_sq c_v c_ss c_sumsq c_t1 c_r2 c_rn c_rot c_T c_Tsb
            c_s_mm c_max c_exp c_pT c_pTsb c_o_mm c_o c_oT c_oTsb c_proj_mm
            c_up_mm c_gelu c_ug c_down_mm c_done c_out""".split()
        s = {n: sem(n) for n in names}
        loop_sems = range(s[names[0]].num, s[names[-1]].num + 1)
        assert [s[n].num for n in names] == list(loop_sems)

        LOADS = ((c_sb[:, :, :], cT), (wmod_sb, wmod), (w0qkv_sb[:, :], w0qkv), (w0proj_sb[:, :], w0proj),
                 (wr_sb[:, :], wr), (wo0_sb[:, :, :], wo0.rearrange("(j p) n -> p j n", p=P)),
                 (w1qkv_sb[:, :], w1qkv), (w1o_sb[:, :], w1o),
                 (wqkv_sb[:, :, :], wqkv.rearrange("l p n -> p l n")),
                 (wo_sb[:, 0, :, :], wo[0].rearrange("(j p) n -> p j n", p=P)),
                 (wo_sb[:, 1, :, :], wo[1].rearrange("(j p) n -> p j n", p=P)),
                 (w1_sb[:, :, :], w1.rearrange("l p n -> p l n")),
                 (w2_sb[:, :, 0, :], w2[:, 0:P, :].rearrange("l p n -> p l n")),
                 (w2_sb[:, :, 1, :], w2[:, P:2 * P, :].rearrange("l p n -> p l n")),
                 (w2_sb[0:HT[2], :, 2, :], w2[:, 2 * P:HID, :].rearrange("l p n -> p l n")),
                 (vec[:, :], vecs), (row[:, :], rows), (ident[:, :], ident_in), (tri[:, :], tri_in),
                 (diag[:, :], diag_in), (self32, sel_in), (bandf[:, :], band_in), (rot[:, :, :, :], rot_in))

        def V(name, l=""):
            i = VEC[f"{name}{l}"]
            return vec[:, i:i + 1]

        with nc.Block() as block:
            @block.sync
            def _(sp):
                for dst, src in LOADS:
                    sp.dma_start(dst, src).then_inc(loaded, 16)

            @block.gpsimd
            def _(pool):
                pool.memset(narrow["a"]["vaug"][:, :, :, :], 1.0).then_inc(pool_ready, 1)
                pool.memset(narrow["b"]["vaug"][:, :, :, :], 1.0).then_inc(pool_ready, 1)
                pool.memset(y[:, :], 0.0).then_inc(pool_ready, 1)
                pool.memset(lp[:, :, :], 0.0).then_inc(pool_ready, 1)
                pool.memset(ones[:, :], 1.0).then_inc(pool_ready, 1)
                pool.memset(eps[:, :], LN_EPS).then_inc(pool_ready, 1)
                pool.memset(shift[:, :], 0.5 * RSTD_SHIFT * 0.6931471805599453).then_inc(pool_ready, 1)

            @block.scalar
            def _(act):
                act.wait_ge(loaded, 16 * len(LOADS))
                act.activation(stmp[:, :, :], c_sb[:, :, :], ACT.Exp, scale=-1.0).then_inc(silu_e, 1)

            @block.tensor
            def _(pe):
                pe.wait_ge(silu_done, 1)
                for l in range(2):
                    for j in range(6):
                        mm = pe.matmul(ps[:, l, j * NB:(j + 1) * NB], wmod_sb[:, l, j * P:(j + 1) * P],
                                       silu[:, l, :], start=True, stop=True)
                mm.then_inc(mod_mm, 1)

            @block.vector
            def _(dve):
                n = [0]

                def link(ins):
                    n[0] += 1
                    ins.then_inc(set_chain, 1)
                    dve.wait_ge(set_chain, n[0])

                dve.wait_ge(loaded, 16 * len(LOADS))
                dve.tensor_copy(identb[:, :], ident[:, :])
                dve.tensor_copy(sel[:, :, :].rearrange("p a b -> p (a b)"), self32)
                dve.tensor_copy(band[:, :], bandf[:, :])
                dve.tensor_scalar(w0qkv_sb[:, 0:P], w0qkv_sb[:, 0:P], float(HD) ** -0.5, None, ALU.mult)
                for l in range(DEPTH):
                    for i in range(4):
                        at = NH + P + (l * 4 + i) * LD
                        ins = dve.tensor_tensor(wave[:, l, i, :, :], rot[:, i, :, :],
                                                row[:, None, at:at + LD].broadcast_to([P, NT, LD]), ALU.mult)
                link(ins)
                dve.tensor_scalar(wave[:, :, 0:2, :, :].rearrange("p l i t d -> p l (i t d)"),
                                  wave[:, :, 0:2, :, :].rearrange("p l i t d -> p l (i t d)"), 8.0, None, ALU.mult)
                dve.wait_ge(silu_e, 1)
                link(dve.tensor_scalar(stmp[:, :, :], stmp[:, :, :], 1.0, None, ALU.add))
                link(dve.reciprocal(stmp[:, :, :], stmp[:, :, :]))
                dve.tensor_tensor(silu[:, :, :], c_sb[:, :, :], stmp[:, :, :], ALU.mult).then_inc(silu_done, 1)
                dve.wait_ge(mod_mm, 1)
                for l in range(2):
                    for j in range(6):
                        src = ps[:, l, j * NB:(j + 1) * NB]
                        dst = mod[:, 6 * l + j, :]
                        if j % 3 == 0:
                            dve.tensor_copy(dst, src)
                        elif j % 3 == 1:
                            dve.tensor_scalar(dst, src, 1.0, None, ALU.add)
                        else:
                            link(dve.tensor_scalar(sgn[:, :], src, 0.0, 2.0, ALU.is_ge, ALU.mult))
                            link(dve.tensor_scalar(sgn[:, :], sgn[:, :], 1.0, None, ALU.subtract))
                            link(dve.tensor_tensor(mag[:, :], src, sgn[:, :], ALU.mult))
                            link(dve.scalar_tensor_tensor(dst, mag[:, :], 0.25, sgn[:, :], ALU.max, ALU.mult))
                dve.wait_ge(pool_ready, 7)

        BA, BB, BC = 0, 3, 5

        def turn(seq):
            active = list(seq)
            with nc.Block() as block:

                @block.sync
                def _(sp):
                    def stack_parts(k):
                        sp.wait_ge(s[k + "_part2"], 1)
                        for t, (i, j) in enumerate(TERMS):
                            sp.dma_start(narrow[k]["stack"][HD * t:HD * t + HD, :, :, :],
                                         narrow[k]["part"][:, i:3 + j + 1:3 + j - i, :]).then_inc(s[k + "_stacked"], 16)

                    def a():
                        yield "in"
                        sp.dma_start(x_in[:, :], z[bass.ds(seq["a"], 1)].rearrange("b p t -> p (b t)"))\
                            .then_inc(s["a_x_in"], 16)
                        yield "stack"
                        stack_parts("a")

                    def b():
                        yield "gexp"
                        sp.wait_ge(s["b_top"], 1)
                        for k in range(NA):
                            head = sp.value_load(tidx[0:1, k:k + 1], min_val=0, max_val=NH - 1)
                            sp.dma_start(wsel[:, k, :], wpack[bass.ds(head, 1)].rearrange("b p n -> p (b n)"))\
                                .then_inc(s["b_wsel"], 16)
                        yield "stack"
                        stack_parts("b")

                    def c():
                        yield "done"
                        sp.wait_ge(s["c_done"], 1)
                        sp.dma_start(out[bass.ds(seq["c"], 1)].rearrange("b p t -> p (b t)"), x_c[:, :])\
                            .then_inc(s["c_out"], 16)
                        sp.wait_ge(s["c_out"], 16)

                    take_turns(active, {"a": a(), "b": b(), "c": c()})

                @block.gpsimd
                def _(pool):
                    def part1(k):
                        pool.wait_ge(s[k + "_part1_r"], 1)
                        pool.tensor_copy(narrow[k]["part"][:, 1:5:3, :], narrow[k]["rem"][:, :, :])\
                            .then_inc(s[k + "_part1"], 1)

                    def a():
                        yield "part1"
                        part1("a")

                    def b():
                        yield "part1"
                        part1("b")

                    def c():
                        yield "in"
                        pool.tensor_copy(x_c[:, :], x_bc[:, :]).then_inc(s["c_x"], 1)
                        for l in range(DEPTH):
                            for n in range(6):
                                yield f"{l}.q{n + 2}"
                                if n >= 2 and n < 6:
                                    u = 4 * l + n - 2
                                    i, t = n % 2, (n - 2) // 2
                                    pool.wait_ge(s["c_t1"], u + 1)
                                    pool.wait_ge(s["c_r2"], u + 1)
                                    pool.tensor_tensor(r1[:, i, t, :, :], r1[:, i, t, :, :], r2[:, i, :, :], ALU.add)\
                                        .then_inc(s["c_rot"], 1)
                                if n < 4:
                                    u = 4 * l + n
                                    i, t = n % 2, n // 2
                                    pool.wait_ge(s["c_copied"], u + 1)
                                    if u >= 2:
                                        pool.wait_ge(s["c_rot"], u - 1)
                                    for a in range(2):
                                        d0, d1 = a * LD // 2, (1 - a) * LD // 2
                                        ins = pool.tensor_tensor(
                                            r2[:, i, :, d0:d0 + LD // 2], qk[:, i, t, :, d1:d1 + LD // 2],
                                            wave[:, l, 2 * i + 1, t, None, d0:d0 + LD // 2].broadcast_to([P, LH, LD // 2]),
                                            ALU.mult)
                                    ins.then_inc(s["c_r2"], 1)
                            for i in range(2):
                                yield f"{l}.q{10 + i}"
                                pool.wait_ge(s["c_sumsq"], l + 1)
                                pool.wait_ge(s["c_rot"], 4 * (l + 1))
                                pool.tensor_tensor(r1[:, i, :, :, :], r1[:, i, :, :, :],
                                                   rn[:, i, :, :, None].broadcast_to([P, NT, LH, LD]), ALU.mult)\
                                    .then_inc(s["c_rn"], 1)

                    take_turns(active, {"a": a(), "b": b(), "c": c()})

                @block.tensor
                def _(pe):
                    def layer_norm(k, u, bank, src, ready, n):
                        yield f"ln{u}.tok"
                        if ready:
                            pe.wait_ge(s[ready], n)
                        for t in range(NT):
                            mm = pe.transpose(ps[:, bank, t * P:(t + 1) * P], src[:, t * P:(t + 1) * P], ident[:, :])
                        mm.then_inc(s[k + "_ln_tok"], 1)
                        yield f"ln{u}.feat"
                        pe.wait_ge(s[k + "_ln_norm"], u + 1)
                        for t in range(NT):
                            mm = pe.transpose(ps[:, bank, 256 + t * P:256 + (t + 1) * P], norm[k]["xn"][:, t, :],
                                              ident[:, :])
                        mm.then_inc(s[k + "_ln_feat"], 1)

                    def narrow_qkv(k, u, w, src, qk_bank, v_bank):
                        yield "qkv"
                        pe.wait_ge(s[k + "_ln_out"], u + 1)
                        for i in range(2):
                            pe.matmul(ps[:, qk_bank, i * T:(i + 1) * T], w[:, i * P:(i + 1) * P], src[:, :],
                                      start=True, stop=True)
                        for t in range(NT):
                            mm = pe.matmul(ps[:, v_bank, t * P:(t + 1) * P], src[:, t * P:(t + 1) * P],
                                           w[:, 2 * P:3 * P], start=True, stop=True)
                        mm.then_inc(s[k + "_qkv_mm"], 1)

                    def project(k, w, bank0, bank1):
                        yield "attT"
                        pe.wait_ge(s[k + "_att"], 1)
                        for t in range(NT):
                            mm = pe.transpose(ps[:, bank0, t * P:(t + 1) * P], narrow[k]["att"][:, t, :], ident[:, :])
                        mm.then_inc(s[k + "_att_T"], 1)
                        yield "proj"
                        pe.wait_ge(s[k + "_attT_sb"], 1)
                        pe.matmul(ps[:, bank1, 0:T], w[:, :], narrow[k]["attT"][:, :], start=True, stop=True)\
                            .then_inc(s[k + "_proj_mm"], 1)

                    def a():
                        stack, vaug = narrow["a"]["stack"], narrow["a"]["vaug"]
                        yield from layer_norm("a", 0, BA, x_in, "a_x_in", 16)
                        yield from layer_norm("a", 1, BA, ha, "a_ln_out", 1)
                        yield from narrow_qkv("a", 1, w0qkv_sb, zn, BA + 1, BA)
                        for k in range(H0):
                            yield f"max{k}"
                            if k == 0:
                                pe.wait_ge(s["a_stacked"], 16 * len(TERMS))
                            if k >= 2:
                                pe.wait_ge(s["a_sc_max"], k - 1)
                            for t in range(NT):
                                mm = pe.matmul(ps[:, BA + 1 + k % 2, t * T:(t + 1) * T],
                                               stack[:, k, 0, t * P:(t + 1) * P], stack[:, k, 1, :],
                                               start=True, stop=True)
                            mm.then_inc(s["a_sc_mm"], 1)
                        yield "nmT"
                        pe.wait_ge(s["a_nm"], 1)
                        for t in range(NT):
                            mm = pe.transpose(psb[0:2 * H0, t * P:(t + 1) * P],
                                              nmb[:, t, :, :].rearrange("p a h -> p (a h)"), identb[:, :])
                        mm.then_inc(s["a_nm_T"], 1)
                        for k in range(H0 + 3):
                            yield f"st{k}"
                            if k >= 3:
                                e = k - 3
                                pe.wait_ge(s["a_st_exp"], e + 1)
                                for t in range(NT):
                                    at = (t * H0 + e) * (HD + 1)
                                    for c in range(NT):
                                        mm = pe.matmul(ps[:, BA, at:at + HD + 1], pT[:, e % 2, c, t * P:(t + 1) * P],
                                                       vaug[:, c, e, :], start=(c == 0), stop=(c == 1))
                                mm.then_inc(s["a_pv_mm"], 1)
                            if k < H0:
                                if k == 0:
                                    pe.wait_ge(s["a_nm_sb"], 1)
                                if k >= 2:
                                    pe.wait_ge(s["a_st_exp"], k - 1)
                                for c in range(NT):
                                    o = ps[:, BA + 1 + k % 2, c * T:(c + 1) * T]
                                    pe.matmul(o, stack[:, k, 1, c * P:(c + 1) * P], stack[:, k, 0, :],
                                              start=True, stop=False)
                                    mm = pe.matmul(o, sel[:, k, :], nmT[:, :], start=False, stop=True)
                                mm.then_inc(s["a_st_mm"], 1)
                        yield from project("a", w0proj_sb, BA + 1, BA + 2)

                    def b():
                        stack, vaug = narrow["b"]["stack"], narrow["b"]["vaug"]
                        yield from layer_norm("b", 0, BB, x_ab, None, 0)
                        yield "route"
                        pe.wait_ge(s["b_hmean"], 1)
                        pe.matmul(ps[:, BB + 1, 0:NH], hmean[:, :], wr_sb[:, :], start=True, stop=True)\
                            .then_inc(s["b_route_mm"], 1)
                        yield "fqk"
                        pe.wait_ge(s["b_wsel"], 16 * NA)
                        for j in range(2):
                            for i in range(2):
                                for e in range(2):
                                    mm = pe.matmul(ps[64 * e:64 * e + 64, BB + i, j * T:(j + 1) * T],
                                                   wsel[:, 2 * j + e, i * DA:(i + 1) * DA], hb[:, :],
                                                   start=True, stop=True)
                        mm.then_inc(s["b_fqk_mm"], 1)
                        yield "fv"
                        pe.wait_ge(s["b_fqk"], 1)
                        for t in range(NT):
                            mm = pe.matmul(ps[:, BB, t * NA * DA:(t + 1) * NA * DA], hb[:, t * P:(t + 1) * P],
                                           wsel[:, :, 2 * DA:3 * DA], start=True, stop=True)
                        mm.then_inc(s["b_fv_mm"], 1)

                        def scores(k):
                            r = slice(64 * (k % 2), 64 * (k % 2) + 64)
                            for t in range(NT):
                                mm = pe.matmul(ps[:, BB + (k + 1) % 2, t * T:(t + 1) * T], fq[r, k // 2, t * P:(t + 1) * P],
                                               fk[r, k // 2, :], start=True, stop=True)
                            mm.then_inc(s["b_fs_mm"], 1)

                        def turn_p(k):
                            pe.wait_ge(s["b_fexp"], k + 1)
                            for t in range(NT):
                                for c in range(NT):
                                    mm = pe.transpose(ps[:, BB + (k + 1) % 2, (t * NT + c) * P:(t * NT + c + 1) * P],
                                                      fp[:, k % 2, t, c * P:(c + 1) * P], ident[:, :])
                            mm.then_inc(s["b_fT"], 1)

                        for r in range(2):
                            yield f"f{r}.0"
                            if r == 1:
                                pe.wait_ge(s["b_fTsb"], 1)
                            scores(2 * r)
                            yield f"f{r}.1"
                            if r == 0:
                                pe.wait_ge(s["b_fv"], 1)
                            else:
                                pe.wait_ge(s["b_fTsb"], 2)
                            scores(2 * r + 1)
                            yield f"f{r}.3"
                            turn_p(2 * r)
                            yield f"f{r}.4"
                            turn_p(2 * r + 1)
                        yield "fo"
                        pe.wait_ge(s["b_fTsb"], NA)
                        for k in range(NA):
                            for t in range(NT):
                                for c in range(NT):
                                    mm = pe.matmul(ps[:, BB + 1, (t * NA + k) * DA:(t * NA + k + 1) * DA],
                                                   fpT[:, k, t, c, :], fv[:, c, k, :], start=(c == 0), stop=(c == 1))
                        mm.then_inc(s["b_fo_mm"], 1)
                        yield "fo_T"
                        pe.wait_ge(s["b_fo"], 1)
                        for j in range(2):
                            for t in range(NT):
                                mm = pe.transpose(ps[:, BB, j * T + t * P:j * T + (t + 1) * P],
                                                  fo[:, t, 2 * j:2 * j + 2, :].rearrange("p a d -> p (a d)"), ident[:, :])
                        mm.then_inc(s["b_fo_T"], 1)
                        yield "fproj"
                        pe.wait_ge(s["b_foT_sb"], 1)
                        for j in range(2):
                            mm = pe.matmul(ps[:, BB + 1, 0:T], wo0_sb[:, j, :], foT[:, j, :], start=(j == 0), stop=(j == 1))
                        mm.then_inc(s["b_fproj_mm"], 1)

                        yield from layer_norm("b", 1, BB, x_b, "b_mid", 1)
                        yield from narrow_qkv("b", 1, w1qkv_sb, hb, BB + 1, BB)
                        yield "kT"
                        pe.wait_ge(s["b_phi"], 1)
                        pe.wait_ge(s["b_v"], 1)
                        pe.transpose(ps[:, BB, T:T + P], phi[:, 1, 0:P], ident[:, :]).then_inc(s["b_kT"], 1)
                        yield "state"
                        pe.wait_ge(s["b_knat"], 1)
                        pe.matmul(ps[:, BB + 1, 0:H0 * (HD + 1)], knat[:, :], vaug[:, 0, :, :].rearrange("p h d -> p (h d)"),
                                  start=True, stop=True).then_inc(s["b_state_mm"], 1)
                        yield "inter"
                        pe.wait_ge(s["b_state"], 1)
                        pe.matmul(ps[:, BB + 1, T:T + H0 * (HD + 1)], phi[:, 0, P:T], state[:, :], start=True, stop=True)\
                            .then_inc(s["b_inter_mm"], 1)
                        for n in range(H0 // 2 + 1):
                            yield f"lin{2 * n}"
                            if n < H0 // 2:
                                if n == 0:
                                    pe.wait_ge(s["b_stacked"], 16 * len(TERMS))
                                    pe.wait_ge(s["b_inter"], 1)
                                else:
                                    pe.wait_ge(s["b_masked"], n)
                                for e in range(2):
                                    for t in range(NT):
                                        mm = pe.matmul(ps[:, BB + 1, e * T + t * P:e * T + (t + 1) * P],
                                                       stack[:, 2 * n + e, 1, t * P:(t + 1) * P],
                                                       stack[:, 2 * n + e, 0, t * P:(t + 1) * P], start=True, stop=True)
                                mm.then_inc(s["b_lin_mm"], 1)
                            if n >= 1:
                                pe.wait_ge(s["b_masked"], n)
                                for e in range(2):
                                    for t in range(NT):
                                        at = (t * H0 + 2 * (n - 1) + e) * (HD + 1)
                                        mm = pe.matmul(ps[:, BB, at:at + HD + 1], masked[:, (n - 1) % 2, e, t, :],
                                                       vaug[:, t, 2 * (n - 1) + e, :], start=True, stop=True)
                                mm.then_inc(s["b_lpv_mm"], 1)
                        yield from project("b", w1o_sb, BB + 1, BB)

                    def c():
                        yield from layer_norm("c", 0, BC, x_bc, None, 0)
                        for l in range(DEPTH):
                            for n in range(6):
                                yield f"{l}.q{n}"
                                t, i = n // 3, n % 3
                                if n == 0:
                                    pe.wait_ge(s["c_y"], 2 * l + 1)
                                if n >= 3 and i < 2:
                                    pe.wait_ge(s["c_sq"], 4 * l + i + 1)
                                elif n >= 3:
                                    pe.wait_ge(s["c_v"], 2 * l + 1)
                                pe.matmul(ps[:, BC + i, :], y[:, t * P:(t + 1) * P],
                                          wqkv_sb[:, l, i * INNER:(i + 1) * INNER], start=True, stop=True)\
                                    .then_inc(s["c_qkv_mm"], 1)
                            for n in range(4):
                                yield f"{l}.x{n}"
                                i, half = n // 2, n % 2
                                pe.wait_ge(s["c_rn"], 2 * l + i + 1)
                                if n == 0:
                                    pe.wait_ge(s["c_v"], 2 * (l + 1))
                                    pe.wait_ge(s["c_sq"], 4 * (l + 1))
                                if n == 3:
                                    pe.wait_ge(s["c_Tsb"], 4 * l + 1)
                                for j in range(2):
                                    for t in range(NT):
                                        e = (2 * half + j) * 2
                                        mm = pe.transpose(ps[:, BC + n % 3, j * T + t * P:j * T + (t + 1) * P],
                                                          r1[:, i, t, e:e + 2, :].rearrange("p a d -> p (a d)"),
                                                          ident[:, :])
                                mm.then_inc(s["c_T"], 1)
                            for k in range(LH + 4):
                                yield f"{l}.h{k}"
                                if 3 <= k < LH + 3:
                                    e = k - 3
                                    pe.wait_ge(s["c_exp"], LH * l + e + 1)
                                    if e == 0:
                                        pe.wait_ge(s["c_Tsb"], 4 * (l + 1))
                                    else:
                                        pe.wait_ge(s["c_pTsb"], LH * l + e)
                                    for c in range(3):
                                        mm = pe.transpose(ps[:, BC + 2, c * P:(c + 1) * P],
                                                          lp[:, e % RING, c * P:(c + 1) * P], ident[:, :])
                                    mm.then_inc(s["c_pT"], 1)
                                if k < LH:
                                    e = k
                                    if e == 0:
                                        pe.wait_ge(s["c_Tsb"], 4 * (l + 1))
                                    if e >= 2:
                                        pe.wait_ge(s["c_exp"], LH * l + e - 1)
                                    o = ps[:, BC + e % 2, 0:SW]
                                    r = slice(64 * (e % 2), 64 * (e % 2) + 64)
                                    pe.matmul(o[:, 0:P], identb[:, :], band[:, 0:P], start=True, stop=False)
                                    pe.matmul(o[:, 0:P], qkT[r, 0, e // 2, 0:P], qkT[r, 1, e // 2, 0:P],
                                              start=False, stop=True)
                                    pe.matmul(o[:, P:SW], identb[:, :], band[:, P:SW], start=True, stop=False)
                                    pe.matmul(o[:, P:SW], qkT[r, 0, e // 2, P:T], qkT[r, 1, e // 2, P - WINDOW:T],
                                              start=False, stop=True).then_inc(s["c_s_mm"], 1)
                            yield f"{l}.o0"
                            pe.wait_ge(s["c_exp"], LH * (l + 1))
                            pe.wait_ge(s["c_pTsb"], LH * (l + 1))
                            for e in range(LH):
                                d = slice(e * LD, (e + 1) * LD)
                                mm = pe.matmul(ps[:, BC, d], lpT[:, e, 0:P], lv[:, 0, d], start=True, stop=True)
                            mm.then_inc(s["c_o_mm"], 1)
                            yield f"{l}.o1"
                            for e in range(LH):
                                d = slice(e * LD, (e + 1) * LD)
                                pe.matmul(ps[:, BC + 1, d], lpT[:, e, P:2 * P], lv[:, 0, d], start=True, stop=False)
                                mm = pe.matmul(ps[:, BC + 1, d], lpT[:, e, 2 * P:3 * P], lv[:, 1, d],
                                               start=False, stop=True)
                            mm.then_inc(s["c_o_mm"], 1)
                            yield f"{l}.oT"
                            pe.wait_ge(s["c_o"], 2 * (l + 1))
                            for j in range(4):
                                for t in range(NT):
                                    mm = pe.transpose(ps[:, BC + (2, 0)[j // 2], (j % 2) * T + t * P:(j % 2) * T + (t + 1) * P],
                                                      lo[:, t, j * P:(j + 1) * P], ident[:, :])
                                if j % 2:
                                    mm.then_inc(s["c_oT"], 1)
                            yield f"{l}.proj"
                            pe.wait_ge(s["c_oTsb"], 2 * (l + 1))
                            for j in range(4):
                                mm = pe.matmul(ps[:, BC + 1, 0:T], wo_sb[:, l, j, :], loT[:, j, :],
                                               start=(j == 0), stop=(j == 3))
                            mm.then_inc(s["c_proj_mm"], 1)

                            for label in layer_norm("c", 1 + l, BC, y, "c_y", 2 * l + 2):
                                yield f"{l}.{label}"
                            for j in range(3):
                                yield f"{l}.up{j}"
                                if j == 0:
                                    pe.wait_ge(s["c_ln_out"], 1 + l)
                                for i in range(2):
                                    at = i * HID + j * P
                                    mm = pe.matmul(ps[0:HT[j], BC + (2, 1, 0)[j], i * T:(i + 1) * T],
                                                   w1_sb[:, l, at:at + HT[j]], hc[:, :], start=True, stop=True)
                                mm.then_inc(s["c_up_mm"], 1)
                            yield f"{l}.down"
                            pe.wait_ge(s["c_ug"], 3 * (l + 1))
                            for j in range(3):
                                mm = pe.matmul(ps[:, BC + 1, 0:T], w2_sb[0:HT[j], l, j, :], ug[0:HT[j], j, :],
                                               start=(j == 0), stop=(j == 2))
                            mm.then_inc(s["c_down_mm"], 1)

                    take_turns(active, {"a": a(), "b": b(), "c": c()})

                @block.scalar
                def _(act):
                    n_link = [0]

                    def link(ins):
                        n_link[0] += 1
                        ins.then_inc(s["act_chain"], 1)
                        act.wait_ge(s["act_chain"], n_link[0])

                    def layer_norm(k, u):
                        yield f"ln{u}.rstd"
                        b = norm[k]
                        act.wait_ge(s[k + "_ln_stat"], u + 1)
                        link(act.activation(b["lnv"][:, :], b["mv"][:, :, 1], ACT.Ln, bias=eps[:, :]))
                        act.activation(b["rstd"][:, :], b["lnv"][:, :], ACT.Exp, scale=-0.5).then_inc(s[k + "_ln_rstd"], 1)

                    def project(k, bank):
                        yield "attTsb"
                        act.wait_ge(s[k + "_att_T"], 1)
                        act.activation(narrow[k]["attT"][:, :], ps[:, bank, 0:T], ACT.Copy).then_inc(s[k + "_attT_sb"], 1)

                    def a():
                        yield from layer_norm("a", 0)
                        yield from layer_norm("a", 1)
                        yield "part0"
                        act.wait_ge(s["a_qkv_mm"], 1)
                        act.activation(narrow["a"]["part"][:, 0:4:3, :], ps[:, BA + 1, :].rearrange("p (i t) -> p i t", i=2),
                                       ACT.Copy).then_inc(s["a_part0"], 1)
                        yield "nmsb"
                        act.wait_ge(s["a_nm_T"], 1)
                        act.activation(nmT[:, :], psb[0:2 * H0, 0:T], ACT.Copy).then_inc(s["a_nm_sb"], 1)
                        for k in range(H0):
                            yield f"st{k + 1}"
                            act.wait_ge(s["a_st_mm"], k + 1)
                            if k >= 2:
                                act.wait_ge(s["a_pv_mm"], k - 1)
                            act.activation(pT[:, k % 2, :, :].rearrange("p c t -> p (c t)"), ps[:, BA + 1 + k % 2, :],
                                           ACT.Exp).then_inc(s["a_st_exp"], 1)
                        yield from project("a", BA + 1)

                    def b():
                        yield from layer_norm("b", 0)
                        yield "dexp"
                        act.wait_ge(s["b_lmax"], 1)
                        act.activation(dist[:, :], logit[:, :], ACT.Exp, bias=lmax[:, :]).then_inc(s["b_dexp"], 1)
                        yield "gexp"
                        act.wait_ge(s["b_top"], 2)
                        act.activation(ge[:, 0:NA], top[:, 0:NA], ACT.Exp, bias=ntop[:, :])
                        act.activation(ge[:, NA:NA + 1], ntop[:, :], ACT.Exp).then_inc(s["b_gexp"], 1)
                        yield "fv_sb"
                        act.wait_ge(s["b_fv_mm"], 1)
                        act.activation(fv[:, :, :, :].rearrange("p t k d -> p (t k d)"), ps[:, BB, :], ACT.Copy)\
                            .then_inc(s["b_fv"], 1)
                        for k in range(NA):
                            yield f"f{k // 2}.{2 + k % 2}"
                            act.wait_ge(s["b_fmax"], k + 1)
                            if k >= 2:
                                act.wait_ge(s["b_fT"], k - 1)
                            for t in range(NT):
                                ins = act.activation(fp[:, k % 2, t, :], ps[:, BB + (k + 1) % 2, t * T:(t + 1) * T], ACT.Exp,
                                                     bias=fnm[:, k, t:t + 1], accum_out=fs[:, k, t:t + 1])
                            ins.then_inc(s["b_fexp"], 1)
                        yield "foT_sb"
                        act.wait_ge(s["b_fo_T"], 1)
                        for j in range(2):
                            ins = act.activation(foT[:, j, :], ps[:, BB, j * T:(j + 1) * T], ACT.Identity,
                                                 bias=bvg[:, j:j + 1])
                        ins.then_inc(s["b_foT_sb"], 1)

                        yield from layer_norm("b", 1)
                        yield "phi1"
                        act.wait_ge(s["b_phi_min"], 1)
                        act.activation(phe[:, :, :], phe[:, :, :], ACT.Exp).then_inc(s["b_phi_exp"], 1)
                        yield "kT"
                        act.wait_ge(s["b_phi"], 1)
                        act.activation(narrow["b"]["part"][:, 0:4:3, :], phi[:, :, :], ACT.Copy).then_inc(s["b_part0"], 1)
                        yield "part1r"
                        act.wait_ge(s["b_kT"], 1)
                        act.activation(knat[:, :], ps[:, BB, T:T + P], ACT.Copy).then_inc(s["b_knat"], 1)
                        yield "lin0"
                        act.wait_ge(s["b_inter_mm"], 1)
                        act.activation(inter[:, :], ps[:, BB + 1, T:T + H0 * (HD + 1)], ACT.Copy).then_inc(s["b_inter"], 1)
                        yield from project("b", BB + 1)

                    def c():
                        yield from layer_norm("c", 0)
                        for l in range(DEPTH):
                            for n in range(6):
                                yield f"{l}.q{n + 1}"
                                t, i = n // 3, n % 3
                                act.wait_ge(s["c_qkv_mm"], 6 * l + n + 1)
                                src = ps[:, BC + i, :]
                                if i == 2:
                                    act.activation(lv[:, t, :], src, ACT.Copy).then_inc(s["c_v"], 1)
                                    continue
                                u = 4 * l + 2 * t + i
                                act.activation(qk[:, i, t, :, :].rearrange("p h d -> p (h d)"), src, ACT.Copy)\
                                    .then_inc(s["c_copied"], 1)
                                if u >= 2:
                                    act.wait_ge(s["c_ss"], u - 1 + l)
                                act.activation(sq[:, i, :, :].rearrange("p h d -> p (h d)"), src, ACT.Square)\
                                    .then_inc(s["c_sq"], 1)
                            yield f"{l}.q8"
                            act.wait_ge(s["c_ss"], 5 * (l + 1))
                            link(act.activation(lss[:, :, :, :], ss[:, :, :, :], ACT.Ln, scale=float(2 ** RSTD_SHIFT)))
                            act.activation(rn[:, :, :, :], lss[:, :, :, :], ACT.Exp, scale=-0.5, bias=shift[:, :])\
                                .then_inc(s["c_sumsq"], 1)
                            for k in range(4):
                                yield f"{l}.x{k + 1}"
                                act.wait_ge(s["c_T"], 4 * l + k + 1)
                                act.activation(qkT[:, k // 2, 2 * (k % 2):2 * (k % 2) + 2, :].rearrange("p j t -> p (j t)"),
                                               ps[:, BC + k % 3, :], ACT.Copy).then_inc(s["c_Tsb"], 1)
                            for k in range(2, LH + 4):
                                yield f"{l}.h{k}"
                                if k < LH + 2:
                                    e = k - 2
                                    act.wait_ge(s["c_max"], LH * l + e + 1)
                                    if e >= RING:
                                        act.wait_ge(s["c_pT"], LH * l + e - RING + 1)
                                    act.activation(lp[:, e % RING, 0:P], ps[:, BC + e % 2, 0:P], ACT.Exp,
                                                   bias=lnm[:, e, 0:1], accum_out=ls[:, e, 0:1])
                                    act.activation(lp[:, e % RING, P + P - WINDOW:PW], ps[:, BC + e % 2, P:SW], ACT.Exp,
                                                   bias=lnm[:, e, 1:2], accum_out=ls[:, e, 1:2]).then_inc(s["c_exp"], 1)
                                if k >= 4 and (k - 4) % 2:
                                    e = k - 4
                                    act.wait_ge(s["c_pT"], LH * l + e + 1)
                                    act.activation(lpT[:, e, :], ps[:, BC + 2, 0:PW], ACT.Copy).then_inc(s["c_pTsb"], 1)
                            yield f"{l}.oTsb"
                            for j in range(2):
                                act.wait_ge(s["c_oT"], 2 * l + j + 1)
                                act.activation(loT[:, 2 * j:2 * j + 2, :].rearrange("p j t -> p (j t)"),
                                               ps[:, BC + (2, 0)[j], :], ACT.Copy).then_inc(s["c_oTsb"], 1)
                            for label in layer_norm("c", 1 + l):
                                yield f"{l}.{label}"
                            yield f"{l}.gelu"
                            act.preload_act_table_set("gelu_and_others")
                            for j in range(3):
                                act.wait_ge(s["c_up_mm"], 3 * l + j + 1)
                                act.activation(gel[0:HT[j], j, :], ps[0:HT[j], BC + (2, 1, 0)[j], T:2 * T], ACT.Gelu,
                                               bias=V(f"b1g{j}_", l)[0:HT[j], :]).then_inc(s["c_gelu"], 1)
                            act.preload_act_table_set("natural_log_exp_and_others")

                    act.preload_act_table_set("natural_log_exp_and_others")
                    take_turns(active, {"a": a(), "b": b(), "c": c()})

                @block.vector
                def _(dve):
                    n_link = [0]

                    def link(ins):
                        n_link[0] += 1
                        ins.then_inc(s["dve_chain"], 1)
                        dve.wait_ge(s["dve_chain"], n_link[0])

                    def layer_norm(k, u, bank, dst, scale, bias):
                        b = norm[k]
                        yield f"ln{u}.stat"
                        dve.wait_ge(s[k + "_ln_tok"], u + 1)
                        for t in range(NT):
                            ins = dve.bn_stats(b["stats"][:, t, :], ps[:, bank, t * P:(t + 1) * P])
                        link(ins)
                        for t in range(NT):
                            ins = dve.bn_aggr(b["mv"][:, t, :], b["stats"][:, t, :])
                        ins.then_inc(s[k + "_ln_stat"], 1)
                        yield f"ln{u}.norm"
                        dve.wait_ge(s[k + "_ln_rstd"], u + 1)
                        for t in range(NT):
                            ins = dve.tensor_scalar(b["xn"][:, t, :], ps[:, bank, t * P:(t + 1) * P], b["mv"][:, t, 0:1],
                                                    b["rstd"][:, t:t + 1], ALU.subtract, ALU.mult)
                        ins.then_inc(s[k + "_ln_norm"], 1)
                        yield f"ln{u}.out"
                        dve.wait_ge(s[k + "_ln_feat"], u + 1)
                        if dst is None:
                            for r, ty in HALVES:
                                ins = dve.tensor_scalar(y[r, ty], ps[r, bank, 256:512], scale[r, :], bias[r, :],
                                                        ALU.mult, ALU.add)
                            ins.then_inc(s["c_y"], 1)
                        else:
                            dve.tensor_scalar(dst, ps[:, bank, 256:512], scale, bias, ALU.mult, ALU.add)\
                                .then_inc(s[k + "_ln_out"], 1)

                    def modulation(k):
                        yield "in"
                        dve.tensor_copy(m[k][:, :], mod[:, :, bass.ds(seq[k], 1)].rearrange("p a b -> p (a b)"))\
                            .then_inc(s[k + "_m"], 1)
                        dve.wait_ge(s[k + "_m"], 1)

                    def part1r(k, src):
                        dve.wait_ge(s[k + "_part0"], 1)
                        dve.tensor_tensor(narrow[k]["rem"][:, :, :], src, narrow[k]["part"][:, 0:4:3, :], ALU.subtract)\
                            .then_inc(s[k + "_part1_r"], 1)

                    def part2(k):
                        dve.wait_ge(s[k + "_part1"], 1)
                        dve.tensor_tensor(narrow[k]["part"][:, 2:6:3, :], narrow[k]["rem"][:, :, :],
                                          narrow[k]["part"][:, 1:5:3, :], ALU.subtract).then_inc(s[k + "_part2"], 1)

                    def heads_out(k, bank):
                        o = ps[:, bank, 0:NT * H0 * (HD + 1)].rearrange("p (t h d) -> p t h d", t=NT, h=H0)
                        rsum, att = narrow[k]["rsum"], narrow[k]["att"]
                        if k == "a":
                            link(dve.reciprocal(rsum[:, :, :], o[:, :, :, HD]))
                        else:
                            later = ps[:, bank, H0 * (HD + 1):2 * H0 * (HD + 1)]
                            link(dve.tensor_tensor(later, later, inter[:, :], ALU.add))
                            link(dve.tensor_scalar(den[:, :, :], o[:, :, :, HD], 1e-6, None, ALU.add))
                            link(dve.reciprocal(rsum[:, :, :], den[:, :, :]))
                        dve.tensor_tensor(att[:, :, :].rearrange("p t (h d) -> p t h d", h=H0), o[:, :, :, 0:HD],
                                          rsum[:, :, :, None].broadcast_to([P, NT, H0, HD]), ALU.mult)\
                            .then_inc(s[k + "_att"], 1)

                    def a():
                        yield from modulation("a")
                        yield from layer_norm("a", 0, BA, ha[:, :], m["a"][:, 1:2], m["a"][:, 0:1])
                        yield from layer_norm("a", 1, BA, zn[:, :], V("ln_scale"), V("ln_bias"))
                        yield "part1r"
                        dve.wait_ge(s["a_qkv_mm"], 1)
                        part1r("a", ps[:, BA + 1, :].rearrange("p (i t) -> p i t", i=2))
                        dve.tensor_copy(narrow["a"]["vaug"][:, :, :, 0:HD],
                                        ps[:, BA, 0:T].rearrange("p (t h d) -> p t h d", t=NT, h=H0))\
                            .then_inc(s["a_v"], 1)
                        yield "part2"
                        part2("a")
                        for k in range(H0):
                            yield f"max{k + 1}"
                            dve.wait_ge(s["a_sc_mm"], k + 1)
                            dve.tensor_reduce(nmax[:, k, :], ps[:, BA + 1 + k % 2, :].rearrange("p (t j) -> p t j", t=NT),
                                              AX.X, ALU.max, negate=True).then_inc(s["a_sc_max"], 1)
                        yield "nm"
                        dve.wait_ge(s["a_sc_max"], H0)
                        neg = nmax[:, :, :].rearrange("p h t -> p t h")
                        link(dve.tensor_copy(nmb[:, :, 0, :], neg))
                        dve.tensor_tensor(nmb[:, :, 1, :], neg, nmb[:, :, 0, :], ALU.subtract).then_inc(s["a_nm"], 1)
                        yield "att"
                        dve.wait_ge(s["a_pv_mm"], H0)
                        heads_out("a", BA)
                        yield "add"
                        dve.wait_ge(s["a_proj_mm"], 1)
                        link(dve.scalar_tensor_tensor(res_a[:, :], ps[:, BA + 2, 0:T], V("b_proj"), ha[:, :],
                                                      ALU.add, ALU.add))
                        if "b" in active:
                            dve.wait_ge(s["b_mid"], 1)
                        dve.scalar_tensor_tensor(x_ab[:, :], res_a[:, :], m["a"][:, 2:3], x_in[:, :], ALU.mult, ALU.add)\
                            .then_inc(s["a_done"], 1)

                    def b():
                        yield from modulation("b")
                        yield from layer_norm("b", 0, BB, hb[:, :], m["b"][:, 4:5], m["b"][:, 3:4])
                        yield "hmean"
                        dve.wait_ge(s["b_ln_out"], 1)
                        link(dve.reduce_sum(hsum[:, :], hb[:, :], AX.X))
                        dve.tensor_scalar(hmean[:, :], ones[:, :], hsum[:, :], 1.0 / T, ALU.mult, ALU.mult)\
                            .then_inc(s["b_hmean"], 1)
                        yield "lmax"
                        dve.wait_ge(s["b_route_mm"], 1)
                        link(dve.tensor_tensor(logit[:, :], ps[:, BB + 1, 0:NH], row[:, 0:NH], ALU.add))
                        dve.tensor_reduce(lmax[:, :], logit[:, :], AX.X, ALU.max, negate=True).then_inc(s["b_lmax"], 1)
                        yield "top"
                        dve.wait_ge(s["b_dexp"], 1)
                        link(dve.reduce_sum(dsum[:, :], dist[:, :], AX.X))
                        link(dve.reciprocal(drec[:, :], dsum[:, :]))
                        link(dve.tensor_scalar(dist[:, :], dist[:, :], drec[:, :], None, ALU.mult))
                        link(dve.max(top[:, :], dist[:, :]))
                        dve.max_index(tidx[:, :], top[:, :], dist[:, :]).then_inc(s["b_top"], 1)
                        dve.tensor_scalar(ntop[:, :], top[:, 0:1], -1.0, None, ALU.mult).then_inc(s["b_top"], 1)
                        yield "g"
                        dve.wait_ge(s["b_gexp"], 1)
                        link(dve.reduce_sum(gsum[:, :], ge[:, 0:NA], AX.X))
                        link(dve.scalar_tensor_tensor(gsum[:, :], ge[:, NA:NA + 1], float(NH - NA), gsum[:, :],
                                                      ALU.mult, ALU.add))
                        link(dve.reciprocal(grec[:, :], gsum[:, :]))
                        dve.tensor_scalar(g[:, :], ge[:, 0:NA], grec[:, :], None, ALU.mult).then_inc(s["b_g"], 1)
                        yield "fqk"
                        dve.wait_ge(s["b_g"], 1)
                        dve.wait_ge(s["b_wsel"], 16 * NA)
                        for k in range(NA):
                            r = slice(64 * (k % 2), 64 * (k % 2) + 64)
                            dve.tensor_copy(gp[r, k // 2:k // 2 + 1], g[r, k:k + 1])
                            ins = dve.tensor_copy(bp[r, k // 2, :], wsel[r, k, 3 * DA:WC])
                        link(ins)
                        dve.tensor_scalar(gq[:, :], gp[:, :], float(DA) ** -0.5, None, ALU.mult)
                        link(dve.tensor_tensor(bvg[:, :], bp[:, :, 2], gp[:, :], ALU.mult))
                        yield "fqk_sb"
                        dve.wait_ge(s["b_fqk_mm"], 1)
                        for j in range(2):
                            dve.tensor_scalar(fq[:, j, :], ps[:, BB, j * T:(j + 1) * T], bp[:, j, 0:1], gq[:, j:j + 1],
                                              ALU.add, ALU.mult)
                        for j in range(2):
                            ins = dve.tensor_scalar(fk[:, j, :], ps[:, BB + 1, j * T:(j + 1) * T], bp[:, j, 1:2],
                                                    gp[:, j:j + 1], ALU.add, ALU.mult)
                        ins.then_inc(s["b_fqk"], 1)

                        def f_max(k):
                            dve.wait_ge(s["b_fs_mm"], k + 1)
                            dve.tensor_reduce(fnm[:, k, :], ps[:, BB + (k + 1) % 2, :].rearrange("p (t j) -> p t j", t=NT),
                                              AX.X, ALU.max, negate=True).then_inc(s["b_fmax"], 1)

                        def f_Tsb(k):
                            dve.wait_ge(s["b_fT"], k + 1)
                            dve.tensor_copy(fpT[:, k, :, :, :].rearrange("p t c q -> p (t c q)"), ps[:, BB + (k + 1) % 2, :])\
                                .then_inc(s["b_fTsb"], 1)

                        for r in range(2):
                            yield f"f{r}.1"
                            f_max(2 * r)
                            yield f"f{r}.2"
                            f_max(2 * r + 1)
                            yield f"f{r}.4"
                            f_Tsb(2 * r)
                            yield f"f{r}.5"
                            f_Tsb(2 * r + 1)
                        yield "fo"
                        dve.wait_ge(s["b_fexp"], NA)
                        link(dve.reciprocal(fr[:, :, :], fs[:, :, :]))
                        link(dve.tensor_tensor(fr[:, :, :], fr[:, :, :], g[:, :, None].broadcast_to([P, NA, NT]), ALU.mult))
                        yield "fo_sb"
                        dve.wait_ge(s["b_fo_mm"], 1)
                        dve.tensor_tensor(fo[:, :, :, :], ps[:, BB + 1, :].rearrange("p (t k d) -> p t k d", t=NT, k=NA),
                                          fr[:, :, :, None].rearrange("p k t o -> p t k o").broadcast_to([P, NT, NA, DA]),
                                          ALU.mult).then_inc(s["b_fo"], 1)
                        yield "fadd"
                        dve.wait_ge(s["b_fproj_mm"], 1)
                        link(dve.tensor_scalar(res_b[:, :], ps[:, BB + 1, 0:T], V("bo0"), m["b"][:, 5:6], ALU.add, ALU.mult))
                        dve.tensor_tensor(x_b[:, :], x_ab[:, :], res_b[:, :], ALU.add).then_inc(s["b_mid"], 1)

                        yield from layer_norm("b", 1, BB, hb[:, :], m["b"][:, 7:8], m["b"][:, 6:7])
                        yield "phi0"
                        dve.wait_ge(s["b_qkv_mm"], 1)
                        for i, bias in enumerate(("bq1", "bk1")):
                            ins = dve.tensor_scalar(phe[:, i, :], ps[:, BB + 1, i * T:(i + 1) * T], V(bias), 0.0,
                                                    ALU.add, ALU.min)
                        ins.then_inc(s["b_phi_min"], 1)
                        yield "phi1"
                        for i, bias in enumerate(("bq1", "bk1")):
                            ins = dve.tensor_scalar(phi[:, i, :], ps[:, BB + 1, i * T:(i + 1) * T], V(bias), 0.0,
                                                    ALU.add, ALU.max)
                        ins.then_inc(s["b_phi_max"], 1)
                        dve.tensor_tensor(narrow["b"]["vaug"][:, :, :, 0:HD],
                                          ps[:, BB, 0:T].rearrange("p (t h d) -> p t h d", t=NT, h=H0),
                                          row[:, None, NH:NH + P].rearrange("p o (h d) -> p o h d", h=H0)
                                          .broadcast_to([P, NT, H0, HD]), ALU.add).then_inc(s["b_v"], 1)
                        dve.wait_ge(s["b_phi_max"], 1)
                        yield "phi2"
                        dve.wait_ge(s["b_phi_exp"], 1)
                        dve.tensor_tensor(phi[:, :, :], phi[:, :, :], phe[:, :, :], ALU.add).then_inc(s["b_phi"], 1)
                        yield "part1r"
                        dve.wait_ge(s["b_phi"], 1)
                        part1r("b", phi[:, :, :])
                        yield "part2"
                        part2("b")
                        yield "state"
                        dve.wait_ge(s["b_state_mm"], 1)
                        dve.tensor_tensor(state[:, :], ps[:, BB + 1, 0:H0 * (HD + 1)], diag[:, :], ALU.mult)\
                            .then_inc(s["b_state"], 1)
                        for k in range(H0 // 2):
                            yield f"lin{2 * k + 1}"
                            dve.wait_ge(s["b_lin_mm"], k + 1)
                            if k >= 2:
                                dve.wait_ge(s["b_lpv_mm"], k - 1)
                            dve.tensor_tensor(masked[:, k % 2, :, :, :].rearrange("p e t q -> p (e t) q"),
                                              ps[:, BB + 1, :].rearrange("p (c q) -> p c q", q=P),
                                              tri[:, None, :].broadcast_to([P, 4, P]), ALU.mult).then_inc(s["b_masked"], 1)
                        yield "att"
                        dve.wait_ge(s["b_lpv_mm"], H0 // 2)
                        dve.wait_ge(s["b_inter"], 1)
                        heads_out("b", BB)
                        yield "add"
                        dve.wait_ge(s["b_proj_mm"], 1)
                        link(dve.tensor_scalar(res_b[:, :], ps[:, BB, 0:T], V("bo1"), m["b"][:, 8:9], ALU.add, ALU.mult))
                        if "c" in active:
                            dve.wait_ge(s["c_x"], 1)
                        dve.tensor_tensor(x_bc[:, :], x_b[:, :], res_b[:, :], ALU.add).then_inc(s["b_done"], 1)

                    def c():
                        yield from modulation("c")
                        yield from layer_norm("c", 0, BC, None, m["c"][:, 10:11], m["c"][:, 9:10])
                        for l in range(DEPTH):
                            for n, (t, i) in enumerate((t, i) for t in range(NT) for i in range(2)):
                                yield f"{l}.q{(2, 3, 5, 6)[n]}"
                                u = 4 * l + n
                                dve.wait_ge(s["c_sq"], u + 1)
                                dve.tensor_tensor(r1[:, i, t, :, :], qk[:, i, t, :, :],
                                                  wave[:, l, 2 * i, t, None, :].broadcast_to([P, LH, LD]), ALU.mult)\
                                    .then_inc(s["c_t1"], 1)
                                dve.reduce_sum(ss[:, i, t, :], sq[:, i, :, :], AX.X).then_inc(s["c_ss"], 1)
                            yield f"{l}.q7"
                            dve.wait_ge(s["c_ss"], 5 * l + 4)
                            dve.tensor_scalar(ss[:, :, :, :], ss[:, :, :, :], 1e-24, None, ALU.max).then_inc(s["c_ss"], 1)
                            for k in range(1, LH + 4):
                                yield f"{l}.h{k}"
                                if k < LH + 1:
                                    e = k - 1
                                    dve.wait_ge(s["c_s_mm"], LH * l + e + 1)
                                    dve.tensor_reduce(lnm[:, e, 0:1], ps[:, BC + e % 2, 0:P], AX.X, ALU.max, negate=True)
                                    dve.tensor_reduce(lnm[:, e, 1:2], ps[:, BC + e % 2, P:SW], AX.X, ALU.max, negate=True)\
                                        .then_inc(s["c_max"], 1)
                                if k >= 4 and (k - 4) % 2 == 0:
                                    e = k - 4
                                    dve.wait_ge(s["c_pT"], LH * l + e + 1)
                                    dve.tensor_copy(lpT[:, e, :], ps[:, BC + 2, 0:PW]).then_inc(s["c_pTsb"], 1)
                            yield f"{l}.o0"
                            dve.wait_ge(s["c_exp"], LH * (l + 1))
                            link(dve.reciprocal(lr[:, :, :], ls[:, :, :]))
                            for t in range(NT):
                                yield f"{l}.o{t + 1}"
                                dve.wait_ge(s["c_o_mm"], 2 * l + t + 1)
                                dve.tensor_tensor(lo[:, t, :].rearrange("p (h d) -> p h d", h=LH),
                                                  ps[:, BC + t, :].rearrange("p (h d) -> p h d", h=LH),
                                                  lr[:, :, t:t + 1].broadcast_to([P, LH, LD]), ALU.mult)\
                                    .then_inc(s["c_o"], 1)
                            yield f"{l}.y"
                            dve.wait_ge(s["c_proj_mm"], l + 1)
                            dve.wait_ge(s["c_y"], 2 * l + 1)
                            for r, ty in HALVES:
                                ins = dve.tensor_tensor(y[r, ty], y[r, ty], ps[r, BC + 1, 0:T], ALU.add)
                            ins.then_inc(s["c_y"], 1)
                            for label in layer_norm("c", 1 + l, BC, hc[:, :], V("ln_g", l), V("ln_b", l)):
                                yield f"{l}.{label}"
                            yield f"{l}.ug"
                            for j in range(3):
                                dve.wait_ge(s["c_gelu"], 3 * l + j + 1)
                                dve.scalar_tensor_tensor(ug[0:HT[j], j, :], ps[0:HT[j], BC + (2, 1, 0)[j], 0:T],
                                                         V(f"b1a{j}_", l)[0:HT[j], :], gel[0:HT[j], j, :],
                                                         ALU.add, ALU.mult).then_inc(s["c_ug"], 1)
                            yield f"{l}.add"
                            dve.wait_ge(s["c_down_mm"], l + 1)
                            dve.wait_ge(s["c_y"], 2 * l + 2)
                            for r, ty in HALVES:
                                ins = dve.scalar_tensor_tensor(y[r, ty], ps[r, BC + 1, 0:T], V("b2_", l)[r, :], y[r, ty],
                                                               ALU.add, ALU.add)
                            ins.then_inc(s["c_y"], 1)
                        yield "done"
                        dve.wait_ge(s["c_y"], 2 * DEPTH + 1)
                        dve.wait_ge(s["c_x"], 1)
                        for r, ty in HALVES:
                            ins = dve.scalar_tensor_tensor(x_c[r, :], y[r, ty], m["c"][r, 11:12], x_c[r, :],
                                                           ALU.mult, ALU.add)
                        ins.then_inc(s["c_done"], 1)

                    take_turns(active, {"a": a(), "b": b(), "c": c()})

            nc.all_engine_barrier(sems_to_clear=loop_sems)

        turn({"a": 0})
        turn({"a": 1, "b": 0})
        with nc.Fori(2, NB) as b:
            turn({"a": b, "b": b - 1, "c": b - 2})
        turn({"b": NB - 1, "c": NB - 2})
        turn({"c": NB - 1})


def layout(inputs):
    import numpy as np
    f = np.float32
    A = {k: np.asarray(v) for k, v in inputs.items()}
    a = {}
    a["z"] = A["L0_attn_z"].transpose(0, 2, 1)
    a["cT"] = np.stack([A["L0_c"].T, A["L1_c"].T], 1)
    a["wmod"] = np.stack([A["L0_wmod"], A["L1_wmod"]], 1)
    w = A["L0_attn_w_qkv"].reshape(P, H0, HD, 3)
    dh = lambda u: u.transpose(0, 2, 1).reshape(u.shape[0], P)
    a["w0qkv"] = np.concatenate([dh(w[..., 0]), dh(w[..., 1]), w[..., 2].reshape(P, P)], 1)
    a["w0proj"] = A["L0_attn_w_proj"]
    a["wr"] = A["L0_ffn_Wr"]
    pk = [A["L0_ffn_" + n].reshape(P, NH, DA).transpose(1, 0, 2) for n in ("Wq", "Wk", "Wv")]
    pb = [np.concatenate([A["L0_ffn_" + n].reshape(NH, DA, 1)] * 2, 1) for n in ("bq", "bk", "bv")]
    a["wpack"] = np.concatenate(pk + pb, 2)
    a["wo0"] = A["L0_ffn_Wo"]
    a["w1qkv"] = np.concatenate([dh(A["L1_attn_Wq"].T.reshape(P, H0, HD)), dh(A["L1_attn_Wk"].T.reshape(P, H0, HD)),
                                 A["L1_attn_Wv"].T], 1)
    a["w1o"] = A["L1_attn_Wo"].T
    a["wqkv"], a["wo"], a["w1"], a["w2"] = (A["L1_ffn_" + n] for n in ("wqkv", "wo", "w1", "w2"))
    pad = lambda u: np.concatenate([u, np.zeros(3 * P - HID, f)]).reshape(3, P)
    col = {"ln_scale": A["L0_attn_ln_scale"], "ln_bias": A["L0_attn_ln_bias"], "b_proj": A["L0_attn_b_proj"],
           "bo0": A["L0_ffn_bo"], "bo1": A["L1_attn_bo"],
           "bq1": A["L1_attn_bq"].reshape(H0, HD).T.reshape(P), "bk1": A["L1_attn_bk"].reshape(H0, HD).T.reshape(P)}
    for l in range(DEPTH):
        col[f"ln_g{l}"], col[f"ln_b{l}"], col[f"b2_{l}"] = A["L1_ffn_ln_g"][l], A["L1_ffn_ln_b"][l], A["L1_ffn_b2"][l]
        for j in range(3):
            col[f"b1a{j}_{l}"] = pad(A["L1_ffn_b1"][l][:HID])[j]
            col[f"b1g{j}_{l}"] = pad(A["L1_ffn_b1"][l][HID:])[j]
    a["vecs"] = np.stack([col[n] for n in VEC], 1)
    swap = lambda u: np.concatenate([u[LD // 2:], u[:LD // 2]])
    flat = [A["L0_ffn_br"], A["L1_attn_bv"]]
    for l in range(DEPTH):
        q, k = A["L1_ffn_q_scale"][l], A["L1_ffn_k_scale"][l]
        flat += [q, swap(q), k, swap(k)]
    a["rows"] = np.broadcast_to(np.concatenate(flat)[None], (P, ROWS))
    a["ident_in"] = np.eye(P, dtype=f)
    i = np.arange(P)
    a["tri_in"] = (i[None, :] >= i[:, None]).astype(f)
    a["diag_in"] = np.repeat((i[:, None] % H0 == np.arange(H0)[None, :]), HD + 1, 1).astype(f)
    a["sel_in"] = np.repeat(np.arange(2 * H0)[:, None] % H0 == np.arange(H0)[None, :], P, 1).astype(f)
    c = np.arange(P + WINDOW)
    t0 = (i[None, :] > i[:, None]) | (i[:, None] > i[None, :] + WINDOW)
    t1 = (c[None, :] > i[:, None] + WINDOW) | (c[None, :] < i[:, None])
    a["band_in"] = (np.concatenate([t0, t1], 1) * NEG).astype(f)
    half = np.arange(0, LD, 2, dtype=f)
    inv = (f(1) / f(10000) ** (half / f(LD))).astype(f)
    t = np.arange(T, dtype=f)
    fr = np.concatenate([t[:, None] * inv[None]] * 2, 1)
    base = (half + f(0.4 * LD)) / f(1.4 * LD)
    sc = np.concatenate([base[None] ** ((t - T // 2) / f(WINDOW // 2))[:, None]] * 2, 1)
    sg = np.where(np.arange(LD) < LD // 2, -1, 1).astype(f)[None]
    tabs = np.stack([np.cos(fr) * sc, np.sin(fr) * sg * sc, np.cos(fr) / sc, np.sin(fr) * sg / sc]).astype(f)
    a["rot_in"] = tabs.reshape(4, NT, P, LD).transpose(2, 0, 1, 3)
    return {k: np.ascontiguousarray(v, dtype=f) for k, v in a.items()}


_IN = ["z", "cT", "wmod", "w0qkv", "w0proj", "wr", "wpack", "wo0", "w1qkv", "w1o", "wqkv", "wo", "w1", "w2",
       "vecs", "rows", "ident_in", "tri_in", "diag_in", "sel_in", "band_in", "rot_in"]


def kernel(**inputs):
    import numpy as np
    import concourse.bacc as bacc
    from concourse.bass_utils import run_bass_kernel_spmd

    arrays = layout(inputs)
    nc = bacc.Bacc("TRN2", target_bir_lowering=False, num_devices=1)
    args = [nc.dram_tensor(n, arrays[n].shape, F32, kind="ExternalInput").ap() for n in _IN]
    out = nc.dram_tensor("out", (NB, P, T), F32, kind="ExternalOutput").ap()
    program(nc, *args, out)
    r = run_bass_kernel_spmd(nc, [arrays], core_ids=[0])
    return np.ascontiguousarray(r.results[0]["out"].transpose(0, 2, 1))
```

```python
from contextlib import ExitStack

import concourse.bass as bass
from concourse import mybir

F32 = mybir.dt.float32
BF16 = mybir.dt.bfloat16
U32 = mybir.dt.uint32
ACT = mybir.ActivationFunctionType
ALU = mybir.AluOpType
AX = mybir.AxisListType

P = 128
NB = 16
T = 256
NT = T // P
H0 = 16
HD = P // H0
TERMS = ((0, 0), (1, 1), (0, 1), (1, 0), (0, 2), (2, 0))
KS = HD * len(TERMS)
NH = 16
NA = 4
DA = 64
WC = 3 * DA + 3
DEPTH = 2
LH = 8
LD = 64
INNER = LH * LD
WINDOW = 64
HID = 341
HT = (128, 128, 85)
SW = P + P + WINDOW
PW = P + 2 * P
GR = 32
RING = 4
NEG = -3.0e38
LN_EPS = 1e-5
RSTD_SHIFT = 16

VEC = {n: i for i, n in enumerate(
    ["ln_scale", "ln_bias", "b_proj", "bo0", "bq1", "bk1", "bo1"]
    + [f"{n}{l}" for l in range(DEPTH) for n in
       ("ln_g", "ln_b", "b2_", "b1a0_", "b1a1_", "b1a2_", "b1g0_", "b1g1_", "b1g2_")])}
NV = len(VEC)
ROWS = 16 + P + DEPTH * 4 * LD


def norm_steps(u):
    return [f"ln{u}.{n}" for n in ("tok", "stat", "rstd", "norm", "feat", "out")]


STEPS = {
    "a": ["in"] + norm_steps(0) + norm_steps(1) + ["qkv", "part0", "part1r", "part1", "part2", "stack"]
    + [f"max{k}" for k in range(H0 + 2)] + ["nm", "nmT", "nmsb", "nmst"] + [f"st{k}" for k in range(H0 + 3)]
    + ["att", "attR", "attn", "proj", "add"],
    "b": ["in"] + norm_steps(0) + ["hmean", "route", "lmax", "dexp", "top", "gexp", "g", "fqk", "fqk_sb", "fv", "fv_sb"]
    + [f"f{r}.{k}" for r in range(2) for k in range(6)] + ["fo", "foT_sb", "fproj", "fadd"]
    + norm_steps(1) + ["qkv", "phi0", "phi1", "phi2", "kT", "part1r", "part1", "part2", "stack", "state"]
    + [f"lin{k}" for k in range(2 * H0 // 2 + 2)] + ["att", "attR", "attn", "proj", "add"] + norm_steps(2),
    "c": ["in"]
    + [f"{l}.{n}" for l in range(DEPTH) for n in
       [f"q{k}" for k in range(12)] + [f"x{k}" for k in range(6)] + [f"h{k}" for k in range(LH + 4)]
       + ["o", "oTsb", "proj", "y"] + norm_steps(l)
       + ["up0", "up1", "up2", "gelu", "ug", "down", "add"]] + ["done"],
}


PLACE = {
    "a": [
        0, 887, 1020, 1324, 1450, 1555, 1633, 1713, 1791, 1908, 1986, 2083, 2154, 2229, 2547, 2623, 2712,
        2913, 2942, 3501, 3592, 3759, 3927, 4025, 4137, 4225, 4337, 4425, 4537, 4682, 4892, 5058, 5269,
        5434, 5645, 5730, 5730, 5793, 5838, 5887, 5922, 6164, 6207, 6275, 6337, 6388, 6470, 6506, 6566,
        6602, 6663, 6698, 6751, 7133, 7434, 7612, 7913, 8091, 8242, 8515, 8662, 8662, 9597, 10565, 10597],
    "b": [
        0, 0, 54, 178, 267, 378, 433, 519, 641, 699, 772, 817, 981, 1044, 1461, 1546, 1755, 1936, 1936,
        2143, 2289, 2517, 2679, 2935, 2935, 3088, 3088, 3277, 3487, 3676, 3735, 3779, 3859, 4342, 4715,
        4912, 5208, 5419, 5684, 5765, 5811, 6010, 6067, 6149, 6169, 6283, 6383, 6589, 6670, 6670, 6727,
        6812, 6862, 6940, 7040, 7040, 7217, 7217, 7395, 7395, 7594, 7594, 7896, 7896, 8197, 8197, 8531,
        8531, 8623, 8623, 8809, 8837, 8945, 9566, 9781, 10274, 10627, 11067, 11396],
    "c": [
        0, 0, 0, 143, 215, 286, 358, 462, 691, 728, 728, 918, 918, 918, 1218, 1336, 1454, 1554, 1554, 1646,
        1707, 1774, 1834, 2025, 2178, 2356, 2558, 2759, 2960, 3039, 3144, 3210, 3210, 3274, 3519, 3648,
        3710, 3849, 3950, 4075, 4168, 4265, 4522, 4692, 4692, 4692, 4993, 4993, 5236, 5511, 5511, 5892,
        6096, 6242, 6455, 6560, 6563, 6563, 6571, 6571, 6571, 6593, 6601, 6609, 6663, 6663, 6726, 6790,
        6870, 6940, 7102, 7281, 7335, 7348, 7362, 7375, 7454, 7682, 7815, 7815, 7982, 7982, 8487, 8546,
        8635, 8698, 8777, 8836, 8897, 9167, 9843, 9843, 9843, 10704, 10704, 11598],
}


def turns(active):
    order = [(at, k, i) for k in active for i, at in enumerate(PLACE[k])]
    return [(k, STEPS[k][i]) for _, k, i in sorted(order)]


def take_turns(active, streams):
    at = {k: next(streams[k], None) for k in active}
    for k, step in turns(active):
        while at[k] == step:
            at[k] = next(streams[k], None)
    assert not any(at.values()), at


def program(nc, z, cT, wmod, w0qkv, w0proj, wr, wpack, wo0, w1qkv, w1o, wqkv, wo, w1, w2,
            vecs, rows, ident_in, tri_in, diag_in, sumrow_in, band_in, rot_in, out):
    with ExitStack() as ctx:
        def sb(name, shape, dt=F32):
            return ctx.enter_context(nc.sbuf_tensor(name, shape, dt))

        def sem(name):
            return ctx.enter_context(nc.semaphore(name))

        c_sb = sb("c_sb", [P, 2, NB])
        w0qkv_sb = sb("w0qkv_sb", [P, 3 * P])
        w0proj_sb = sb("w0proj_sb", [P, H0 // 4, P])
        wr_sb = sb("wr_sb", [P, NH])
        wo0_sb = sb("wo0_sb", [P, 2, P])
        w1qkv_sb = sb("w1qkv_sb", [P, 3 * P])
        w1o_sb = sb("w1o_sb", [P, H0 // 4, P])
        wqkv_sb = sb("wqkv_sb", [P, DEPTH, 3 * INNER])
        wo_sb = sb("wo_sb", [P, DEPTH, 4, P])
        w1_sb = sb("w1_sb", [P, DEPTH, 2 * HID])
        w2_sb = sb("w2_sb", [P, DEPTH, 3, P])
        vec = sb("vec", [P, NV])
        row = sb("row", [P, ROWS])
        ident = sb("ident", [P, P])
        tri = sb("tri", [P, P])
        diag = sb("diag", [P, H0 * GR])
        identb = sb("identb", [P, P], BF16)
        sumrow = sb("sumrow", [P, P])
        band = sb("band", [P, SW], BF16)
        ones = sb("ones", [P, P])
        eps = sb("eps", [P, 1])
        sum_eps = {k: sb("sum_eps_" + k, [P, 1]) for k in "ab"}
        shift = sb("shift", [P, 1])
        wave = sb("wave", [P, DEPTH, 4, NT, LD])
        silu = sb("silu", [P, 2, NB])
        stmp = sb("stmp", [P, 2, NB])
        mod = sb("mod", [P, 12, NB])
        sgn = sb("sgn", [P, NB])
        mag = sb("mag", [P, NB])

        def norm_buffers(k):
            return {"xn": sb(k + "_xn", [P, NT, P]), "stats": sb(k + "_stats", [P, NT, 6]), "mv": sb(k + "_mv", [P, NT, 2]),
                    "lnv": sb(k + "_lnv", [P, NT]), "rstd": sb(k + "_rstd", [P, NT])}

        norm = {k: norm_buffers(k) for k in "abc"}
        m = {k: sb(k + "_m", [P, 12]) for k in "abc"}
        x_in = sb("x_in", [P, T])
        x_ab = sb("x_ab", [P, T])
        x_b = sb("x_b", [P, T])
        x_bc = sb("x_bc", [P, T])
        x_c = sb("x_c", [P, T])
        ha = sb("ha", [P, T])
        zn = sb("zn", [P, T])
        hb = sb("hb", [P, T])
        hc = sb("hc", [P, T])
        res_a = sb("res_a", [P, T])
        res_b = sb("res_b", [P, T])

        def narrow_buffers(k):
            return {"part": sb(k + "_part", [P, 6, T], BF16),
                    "vaug": sb(k + "_vaug", [P, NT, H0, GR]),
                    "stack": sb(k + "_stack", [KS + 2 * (k == "a"), H0, 2, T], BF16),
                    "att": sb(k + "_att", [P, H0 // 4, T])}

        narrow = {k: narrow_buffers(k) for k in "ab"}
        for buffers in narrow.values():
            buffers["rem"] = buffers["att"][:, 0:2, :]
        nmax = sb("nmax", [P, H0, NT])
        nmb = sb("nmb", [P, NT, 2, H0], BF16)
        nmT = sb("nmT", [2 * H0, T], BF16)
        pT = sb("pT", [P, 2, NT, T])

        phi = sb("phi", [P, 2, T])
        phe = sb("phe", [P, 2, T])
        knat = sb("knat", [P, P])
        state = sb("state", [P, H0, GR])
        hsum = sb("hsum", [P, 1])
        hmean = sb("hmean", [P, P])
        logit = sb("logit", [P, NH])
        lmax = sb("lmax", [P, 1])
        dist = sb("dist", [P, NH])
        dsum = sb("dsum", [P, 1])
        drec = sb("drec", [P, 1])
        top = sb("top", [P, 8])
        tidx = sb("tidx", [P, 8], U32)
        ntop = sb("ntop", [P, 1])
        ge = sb("ge", [P, NA + 1])
        gsum = sb("gsum", [P, 1])
        grec = sb("grec", [P, 1])
        g = sb("g", [P, NA])
        wsel = sb("wsel", [P, NA, WC])
        gp = sb("gp", [P, 2])
        gq = sb("gq", [P, 2])
        bp = sb("bp", [P, 2, 3])
        bvg = sb("bvg", [P, 2])
        fq = sb("fq", [P, 2, T])
        fk = sb("fk", [P, 2, T])
        fv = sb("fv", [P, NT, NA, DA])
        fnm = sb("fnm", [P, NA, NT])
        fs = sb("fs", [P, NA, NT])
        fr = sb("fr", [P, NA, NT])
        fp = sb("fp", [P, 2, NT, T])
        fpT = sb("fpT", [P, NA, NT, NT, P])
        foT = sb("foT", [P, 2, T])

        y = sb("y", [P, T + 1])
        y_bc = sb("y_bc", [P, T + 1])
        HALVES = ((slice(0, P // 2), slice(0, T)), (slice(P // 2, P), slice(1, T + 1)))
        qk = sb("qk", [P, 2, NT, LH, LD])
        sq = sb("sq", [P, 2, LH, LD])
        ss = sb("ss", [P, 2, NT, LH])
        lss = sb("lss", [P, 2, NT, LH])
        rn = sb("rn", [P, 2, NT, LH])
        r1 = sb("r1", [P, 2, NT, LH, LD])
        r2 = sb("r2", [P, 2, LH, LD])
        qkT = sb("qkT", [P, 2, 4, T])
        lv = sb("lv", [P, NT, INNER])
        lnm = sb("lnm", [P, LH, NT])
        ls = sb("ls", [P, LH, NT])
        lr = sb("lr", [P, LH, NT])
        lp = sb("lp", [P, RING, PW])
        lpT = sb("lpT", [P, LH, PW])

        ps = ctx.enter_context(nc.psum_tensor("ps", [P, 8, 512], F32))
        psb = ps[:, 0, :].bitcast(BF16)

        wmod_sb = qk[:, :, :, :, :].rearrange("p i t h d -> p (i t h d)")[:, 0:12 * P].rearrange("p (l n) -> p l n", l=2)

        masked = fpT[:, 0:2, :, :, :].rearrange("p k t c q -> p (k t c q)")\
            .rearrange("p (k e t q) -> p k e t q", k=2, e=2, t=NT)
        narrow["a"]["recip"] = pT[:, :, :, :].rearrange("p e c t -> p e (c t)")
        narrow["b"]["recip"] = masked[:, :, :, :, :].rearrange("p k e t q -> p k (e t q)")
        loT = r1[:, 1, :, :, :].rearrange("p t h d -> p (t h d)").rearrange("p (j t) -> p j t", j=4)
        qk_flat = qk[:, :, :, :, :].rearrange("p i t h d -> p (i t h d)")
        gel = qk_flat[:, 0:3 * T].rearrange("p (j t) -> p j t", j=3)
        ug = qk_flat[:, 4 * T:7 * T].rearrange("p (j t) -> p j t", j=3)

        lpT_flat = lpT[:, :, :].rearrange("p h c -> p (h c)")
        rot = lpT_flat[:, 0:4 * NT * LD].rearrange("p (i t d) -> p i t d", i=4, t=NT)
        bandf = lpT_flat[:, 4 * NT * LD:4 * NT * LD + SW]

        loaded = sem("loaded")
        pool_ready = sem("pool_ready")
        silu_e = sem("silu_e")
        silu_done = sem("silu_done")
        mod_mm = sem("mod_mm")
        set_chain = sem("set_chain")
        last_stored = sem("last_stored")
        names = """dve_chain act_chain
            a_x_in a_m a_ln_tok a_ln_stat a_ln_rstd a_ln_norm a_ln_feat a_ln_out
            a_qkv_mm a_part0 a_part1_r a_part1 a_part2 a_v a_stacked
            a_sc_mm a_sc_max a_nm a_nm_T a_nm_sb a_nm_st a_st_mm a_st_exp a_pv_mm
            a_att a_att_R a_att_rec a_att_n a_proj_mm a_done
            b_m b_ln_tok b_ln_stat b_ln_rstd b_ln_norm b_ln_feat b_ln_out
            b_hmean b_route_mm b_lmax b_dexp b_top b_gexp b_g b_wsel b_fqk_mm b_fqk b_fv_mm b_fv
            b_fs_mm b_fmax b_fexp b_fnorm b_fT b_fTsb b_fo_mm b_foT_sb b_fproj_mm b_mid
            b_qkv_mm b_phi_min b_phi_max b_phi_exp b_phi b_v b_kT b_knat b_part0 b_part1_r b_part1 b_part2 b_stacked
            b_state_mm b_state b_lin_mm b_masked b_lpv_mm
            b_att b_att_R b_att_rec b_att_n b_proj_mm b_done
            c_m c_x c_ln_tok c_ln_stat c_ln_rstd c_ln_norm c_ln_feat c_ln_out c_y
            c_qkv_mm c_copied c_sq c_v c_ss c_sumsq c_t1 c_r2 c_rot_q c_rot_k c_rn_q c_rn_k c_T c_Tsb
            c_s_mm c_max c_exp c_norm c_pT c_pTsb c_o_mm c_oTsb c_proj_mm
            c_up_mm c_gelu c_ug c_down_mm c_done c_out""".split()
        s = {n: sem(n) for n in names}
        loop_sems = range(s[names[0]].num, s[names[-1]].num + 1)
        assert [s[n].num for n in names] == list(loop_sems)

        LOADS = ((c_sb[:, :, :], cT), (wmod_sb, wmod), (w0qkv_sb[:, :], w0qkv), (w0proj_sb[:, :, :], w0proj),
                 (wr_sb[:, :], wr), (wo0_sb[:, :, :], wo0.rearrange("(j p) n -> p j n", p=P)),
                 (w1qkv_sb[:, :], w1qkv), (w1o_sb[:, :, :], w1o),
                 (wqkv_sb[:, :, :], wqkv.rearrange("l p n -> p l n")),
                 (wo_sb[:, 0, :, :], wo[0].rearrange("(j p) n -> p j n", p=P)),
                 (wo_sb[:, 1, :, :], wo[1].rearrange("(j p) n -> p j n", p=P)),
                 (w1_sb[:, :, :], w1.rearrange("l p n -> p l n")),
                 (w2_sb[:, :, 0, :], w2[:, 0:P, :].rearrange("l p n -> p l n")),
                 (w2_sb[:, :, 1, :], w2[:, P:2 * P, :].rearrange("l p n -> p l n")),
                 (w2_sb[0:HT[2], :, 2, :], w2[:, 2 * P:HID, :].rearrange("l p n -> p l n")),
                 (vec[:, :], vecs), (row[:, :], rows), (ident[:, :], ident_in), (tri[:, :], tri_in),
                 (diag[:, :], diag_in), (sumrow[:, :], sumrow_in), (bandf[:, :], band_in), (rot[:, :, :, :], rot_in))

        def V(name, l=""):
            i = VEC[f"{name}{l}"]
            return vec[:, i:i + 1]

        with nc.Block() as block:
            @block.sync
            def _(sp):
                for dst, src in LOADS[0::2]:
                    sp.dma_start(dst, src).then_inc(loaded, 16)

            @block.gpsimd
            def _(pool):
                for k in "ab":
                    pool.memset(narrow[k]["vaug"][:, :, :, :], 0.0).then_inc(pool_ready, 1)
                pool.wait_ge(pool_ready, 2)
                for k in "ab":
                    pool.memset(narrow[k]["vaug"][:, :, :, HD:HD + 1], 1.0).then_inc(pool_ready, 1)
                pool.memset(narrow["a"]["stack"][:, :, :, :], 1.0).then_inc(pool_ready, 1)
                pool.memset(sum_eps["a"][:, :], 0.0).then_inc(pool_ready, 1)
                pool.memset(sum_eps["b"][:, :], 1e-6).then_inc(pool_ready, 1)
                pool.memset(y[:, :], 0.0).then_inc(pool_ready, 1)
                pool.memset(y_bc[:, :], 0.0).then_inc(pool_ready, 1)
                pool.memset(lp[:, :, :], 0.0).then_inc(pool_ready, 1)
                pool.memset(ones[:, :], 1.0).then_inc(pool_ready, 1)
                pool.memset(eps[:, :], LN_EPS).then_inc(pool_ready, 1)
                pool.memset(shift[:, :], 0.5 * RSTD_SHIFT * 0.6931471805599453).then_inc(pool_ready, 1)

            @block.scalar
            def _(act):
                for dst, src in LOADS[1::2]:
                    act.dma_start(dst, src).then_inc(loaded, 16)
                act.wait_ge(loaded, 16 * len(LOADS))
                act.activation(stmp[:, :, :], c_sb[:, :, :], ACT.Exp, scale=-1.0).then_inc(silu_e, 1)

            @block.tensor
            def _(pe):
                pe.wait_ge(silu_done, 1)
                for l in range(2):
                    for j in range(6):
                        mm = pe.matmul(ps[:, l, j * NB:(j + 1) * NB], wmod_sb[:, l, j * P:(j + 1) * P],
                                       silu[:, l, :], start=True, stop=True)
                mm.then_inc(mod_mm, 1)

            @block.vector
            def _(dve):
                n = [0]

                def link(ins):
                    n[0] += 1
                    ins.then_inc(set_chain, 1)
                    dve.wait_ge(set_chain, n[0])

                dve.wait_ge(loaded, 16 * len(LOADS))
                dve.tensor_copy(identb[:, :], ident[:, :])
                dve.tensor_copy(band[:, :], bandf[:, :])
                dve.tensor_scalar(w0qkv_sb[:, 0:P], w0qkv_sb[:, 0:P], float(HD) ** -0.5, None, ALU.mult)
                for l in range(DEPTH):
                    for i in range(4):
                        at = NH + P + (l * 4 + i) * LD
                        ins = dve.tensor_tensor(wave[:, l, i, :, :], rot[:, i, :, :],
                                                row[:, None, at:at + LD].broadcast_to([P, NT, LD]), ALU.mult)
                link(ins)
                dve.tensor_scalar(wave[:, :, 0:2, :, :].rearrange("p l i t d -> p l (i t d)"),
                                  wave[:, :, 0:2, :, :].rearrange("p l i t d -> p l (i t d)"), 8.0, None, ALU.mult)
                dve.wait_ge(silu_e, 1)
                link(dve.tensor_scalar(stmp[:, :, :], stmp[:, :, :], 1.0, None, ALU.add))
                link(dve.reciprocal(stmp[:, :, :], stmp[:, :, :]))
                dve.tensor_tensor(silu[:, :, :], c_sb[:, :, :], stmp[:, :, :], ALU.mult).then_inc(silu_done, 1)
                dve.wait_ge(mod_mm, 1)
                for l in range(2):
                    for j in range(6):
                        src = ps[:, l, j * NB:(j + 1) * NB]
                        dst = mod[:, 6 * l + j, :]
                        if j % 3 == 0:
                            dve.tensor_copy(dst, src)
                        elif j % 3 == 1:
                            dve.tensor_scalar(dst, src, 1.0, None, ALU.add)
                        else:
                            link(dve.tensor_scalar(sgn[:, :], src, 0.0, 2.0, ALU.is_ge, ALU.mult))
                            link(dve.tensor_scalar(sgn[:, :], sgn[:, :], 1.0, None, ALU.subtract))
                            link(dve.tensor_tensor(mag[:, :], src, sgn[:, :], ALU.mult))
                            link(dve.scalar_tensor_tensor(dst, mag[:, :], 0.25, sgn[:, :], ALU.max, ALU.mult))
                dve.wait_ge(pool_ready, 13)

        BA, BB, BC = 0, 3, 5
        LN_BANK = {"a": BA, "b": BB}

        def store(sp, n, stored):
            sp.dma_start(out[bass.ds(n, 1)].rearrange("b p t -> p (b t)"), x_c[:, :]).then_inc(stored, 16)

        def turn(seq):
            active = [k for k in seq if k in STEPS]
            with nc.Block() as block:

                @block.sync
                def _(sp):
                    def stack_parts(k):
                        sp.wait_ge(s[k + "_part2"], 1)
                        for t, (i, j) in enumerate(TERMS):
                            sp.dma_start(narrow[k]["stack"][HD * t:HD * t + HD, :, :, :],
                                         narrow[k]["part"][:, i:3 + j + 1:3 + j - i, :]).then_inc(s[k + "_stacked"], 16)

                    def a():
                        yield "in"
                        sp.dma_start(x_in[:, :], z[bass.ds(seq["a"], 1)].rearrange("b p t -> p (b t)"))\
                            .then_inc(s["a_x_in"], 16)
                        yield "stack"
                        stack_parts("a")
                        yield "nmst"
                        sp.wait_ge(s["a_nm_sb"], 1)
                        sp.dma_start(narrow["a"]["stack"][KS:KS + 2, :, 0, :], nmT[:, :]).then_inc(s["a_nm_st"], 16)

                    def b():
                        yield "gexp"
                        sp.wait_ge(s["b_top"], 1)
                        for k in range(NA):
                            head = sp.value_load(tidx[0:1, k:k + 1], min_val=0, max_val=NH - 1)
                            sp.dma_start(wsel[:, k, :], wpack[bass.ds(head, 1)].rearrange("b p n -> p (b n)"))\
                                .then_inc(s["b_wsel"], 16)
                        yield "stack"
                        stack_parts("b")

                    if "out" in seq:
                        store(sp, seq["out"], s["c_out"])
                    take_turns(active, {"a": a(), "b": b(), "c": iter(())})
                    if "out" in seq:
                        sp.wait_ge(s["c_out"], 16)

                @block.gpsimd
                def _(pool):
                    def part1(k):
                        pool.wait_ge(s[k + "_part1_r"], 1)
                        pool.tensor_copy(narrow[k]["part"][:, 1:5:3, :], narrow[k]["rem"][:, :, :])\
                            .then_inc(s[k + "_part1"], 1)

                    def a():
                        yield "part1"
                        part1("a")

                    def b():
                        yield "part1"
                        part1("b")

                    def c():
                        yield "0.q1"
                        if "out" in seq:
                            pool.wait_ge(s["c_out"], 16)
                        pool.tensor_copy(x_c[:, :], x_bc[:, :]).then_inc(s["c_x"], 1)
                        for l in range(DEPTH):
                            for n in range(6):
                                yield f"{l}.q{n + 2}"
                                if n in (2, 4):
                                    t = (n - 2) // 2
                                    pool.wait_ge(s["c_t1"], 4 * l + n - 1)
                                    pool.wait_ge(s["c_r2"], 4 * l + n - 1)
                                    pool.tensor_tensor(r1[:, 0, t, :, :], r1[:, 0, t, :, :], r2[:, 0, :, :], ALU.add)\
                                        .then_inc(s["c_rot_q"], 1)
                                if n < 4:
                                    u = 4 * l + n
                                    i, t = n % 2, n // 2
                                    pool.wait_ge(s["c_copied"], u + 1)
                                    if u >= 2:
                                        pool.wait_ge(s[("c_rot_q", "c_rot_k")[i]], u // 2)
                                    for a in range(2):
                                        d0, d1 = a * LD // 2, (1 - a) * LD // 2
                                        ins = pool.tensor_tensor(
                                            r2[:, i, :, d0:d0 + LD // 2], qk[:, i, t, :, d1:d1 + LD // 2],
                                            wave[:, l, 2 * i + 1, t, None, d0:d0 + LD // 2].broadcast_to([P, LH, LD // 2]),
                                            ALU.mult)
                                    ins.then_inc(s["c_r2"], 1)
                            yield f"{l}.q10"
                            pool.wait_ge(s["c_sumsq"], l + 1)
                            pool.wait_ge(s["c_rot_q"], 2 * (l + 1))
                            pool.tensor_tensor(r1[:, 0, :, :, :], r1[:, 0, :, :, :],
                                               rn[:, 0, :, :, None].broadcast_to([P, NT, LH, LD]), ALU.mult)\
                                .then_inc(s["c_rn_q"], 1)

                    take_turns(active, {"a": a(), "b": b(), "c": c()})

                @block.tensor
                def _(pe):
                    def layer_norm(k, u, bank, src, ready, n):
                        yield f"ln{u}.tok"
                        if ready:
                            pe.wait_ge(s[ready], n)
                        for t in range(NT):
                            mm = pe.transpose(ps[:, bank, t * P:(t + 1) * P], src[:, t * P:(t + 1) * P], ident[:, :])
                        mm.then_inc(s[k + "_ln_tok"], 1)
                        yield f"ln{u}.feat"
                        pe.wait_ge(s[k + "_ln_norm"], u + 1)
                        for t in range(NT):
                            mm = pe.transpose(ps[:, bank, 256 + t * P:256 + (t + 1) * P], norm[k]["xn"][:, t, :],
                                              ident[:, :])
                        mm.then_inc(s[k + "_ln_feat"], 1)

                    def narrow_qkv(k, u, w, src, qk_bank, v_bank):
                        yield "qkv"
                        pe.wait_ge(s[k + "_ln_out"], u + 1)
                        for i in range(2):
                            pe.matmul(ps[:, qk_bank, i * T:(i + 1) * T], w[:, i * P:(i + 1) * P], src[:, :],
                                      start=True, stop=True)
                        for t in range(NT):
                            mm = pe.matmul(ps[:, v_bank, t * P:(t + 1) * P], src[:, t * P:(t + 1) * P],
                                           w[:, 2 * P:3 * P], start=True, stop=True)
                        mm.then_inc(s[k + "_qkv_mm"], 1)

                    def project(k, w, banks, bank):
                        att = narrow[k]["att"]
                        yield "attR"
                        for n in range(2):
                            pe.wait_ge(s[k + "_att"], n + 1)
                            for j in range(2 * n, 2 * n + 2):
                                mm = pe.matmul(ps[:, banks[n], (j % 2) * T:(j % 2 + 1) * T], sumrow[:, :], att[:, j, :],
                                               start=True, stop=True)
                            mm.then_inc(s[k + "_att_R"], 1)
                        yield "proj"
                        for j in range(4):
                            if j % 2 == 0:
                                pe.wait_ge(s[k + "_att_n"], j // 2 + 1)
                            mm = pe.matmul(ps[:, bank, 0:T], w[:, j, :], att[:, j, :], start=(j == 0), stop=(j == 3))
                        mm.then_inc(s[k + "_proj_mm"], 1)

                    def head_rows(h):
                        return slice(GR * (h % 4), GR * (h % 4) + GR), (h // 4) % 2 * T

                    def a():
                        stack, vaug = narrow["a"]["stack"], narrow["a"]["vaug"]
                        yield from layer_norm("a", 0, BA, x_in, "a_x_in", 16)
                        yield from layer_norm("a", 1, BA, ha, "a_ln_out", 1)
                        yield from narrow_qkv("a", 1, w0qkv_sb, zn, BA + 1, BA)
                        for k in range(H0):
                            yield f"max{k}"
                            if k == 0:
                                pe.wait_ge(s["a_stacked"], 16 * len(TERMS))
                            if k >= 2:
                                pe.wait_ge(s["a_sc_max"], k - 1)
                            for t in range(NT):
                                mm = pe.matmul(ps[:, BA + 1 + k % 2, t * T:(t + 1) * T],
                                               stack[0:KS, k, 0, t * P:(t + 1) * P], stack[0:KS, k, 1, :],
                                               start=True, stop=True)
                            mm.then_inc(s["a_sc_mm"], 1)
                        yield "nmT"
                        pe.wait_ge(s["a_nm"], 1)
                        for t in range(NT):
                            mm = pe.transpose(psb[0:2 * H0, t * P:(t + 1) * P],
                                              nmb[:, t, :, :].rearrange("p a h -> p (a h)"), identb[:, :])
                        mm.then_inc(s["a_nm_T"], 1)
                        for k in range(H0 + 3):
                            yield f"st{k}"
                            if k >= 3:
                                e = k - 3
                                pe.wait_ge(s["a_st_exp"], e + 1)
                                if e == H0 // 2:
                                    pe.wait_ge(s["a_att"], 1)
                                r, at = head_rows(e)
                                for c in range(NT):
                                    mm = pe.matmul(ps[r, BA, at:at + T], vaug[:, c, e, :],
                                                   pT[:, e % 2, c, :], start=(c == 0), stop=(c == 1))
                                mm.then_inc(s["a_pv_mm"], 1)
                            if k < H0:
                                if k == 0:
                                    pe.wait_ge(s["a_nm_st"], 16)
                                if k >= 2:
                                    pe.wait_ge(s["a_st_exp"], k - 1)
                                for c in range(NT):
                                    o = ps[:, BA + 1 + k % 2, c * T:(c + 1) * T]
                                    mm = pe.matmul(o, stack[:, k, 1, c * P:(c + 1) * P], stack[:, k, 0, :],
                                                   start=True, stop=True)
                                mm.then_inc(s["a_st_mm"], 1)
                        yield from project("a", w0proj_sb, (BA + 1, BA + 2), BA)

                    def b():
                        stack, vaug = narrow["b"]["stack"], narrow["b"]["vaug"]
                        yield from layer_norm("b", 0, BB, x_ab, None, 0)
                        yield "route"
                        pe.wait_ge(s["b_hmean"], 1)
                        pe.matmul(ps[:, BB + 1, 0:NH], hmean[:, :], wr_sb[:, :], start=True, stop=True)\
                            .then_inc(s["b_route_mm"], 1)
                        yield "fqk"
                        pe.wait_ge(s["b_wsel"], 16 * NA)
                        for j in range(2):
                            for i in range(2):
                                for e in range(2):
                                    mm = pe.matmul(ps[64 * e:64 * e + 64, BB + i, j * T:(j + 1) * T],
                                                   wsel[:, 2 * j + e, i * DA:(i + 1) * DA], hb[:, :],
                                                   start=True, stop=True)
                        mm.then_inc(s["b_fqk_mm"], 1)
                        yield "fv"
                        pe.wait_ge(s["b_fqk"], 1)
                        for t in range(NT):
                            mm = pe.matmul(ps[:, BB, t * NA * DA:(t + 1) * NA * DA], hb[:, t * P:(t + 1) * P],
                                           wsel[:, :, 2 * DA:3 * DA], start=True, stop=True)
                        mm.then_inc(s["b_fv_mm"], 1)

                        def scores(k):
                            r = slice(64 * (k % 2), 64 * (k % 2) + 64)
                            for t in range(NT):
                                mm = pe.matmul(ps[:, BB + (k + 1) % 2, t * T:(t + 1) * T], fq[r, k // 2, t * P:(t + 1) * P],
                                               fk[r, k // 2, :], start=True, stop=True)
                            mm.then_inc(s["b_fs_mm"], 1)

                        def turn_p(k):
                            pe.wait_ge(s["b_fnorm"], k + 1)
                            for t in range(NT):
                                for c in range(NT):
                                    mm = pe.transpose(ps[:, BB + (k + 1) % 2, (c * NT + t) * P:(c * NT + t + 1) * P],
                                                      fp[:, k % 2, t, c * P:(c + 1) * P], ident[:, :])
                            mm.then_inc(s["b_fT"], 1)

                        for r in range(2):
                            yield f"f{r}.0"
                            if r == 1:
                                pe.wait_ge(s["b_fTsb"], 1)
                            scores(2 * r)
                            yield f"f{r}.1"
                            if r == 0:
                                pe.wait_ge(s["b_fv"], 1)
                            else:
                                pe.wait_ge(s["b_fTsb"], 2)
                            scores(2 * r + 1)
                            yield f"f{r}.3"
                            turn_p(2 * r)
                            yield f"f{r}.4"
                            turn_p(2 * r + 1)
                        yield "fo"
                        pe.wait_ge(s["b_fTsb"], NA)
                        for k in range(NA):
                            r = slice(DA * (k % 2), DA * (k % 2) + DA)
                            for c in range(NT):
                                mm = pe.matmul(ps[r, BB, (k // 2) * T:(k // 2 + 1) * T], fv[:, c, k, :],
                                               fpT[:, k, c, :, :].rearrange("p t q -> p (t q)"),
                                               start=(c == 0), stop=(c == 1))
                        mm.then_inc(s["b_fo_mm"], 1)
                        yield "fproj"
                        pe.wait_ge(s["b_foT_sb"], 1)
                        for j in range(2):
                            mm = pe.matmul(ps[:, BB + 1, 0:T], wo0_sb[:, j, :], foT[:, j, :], start=(j == 0), stop=(j == 1))
                        mm.then_inc(s["b_fproj_mm"], 1)

                        yield from layer_norm("b", 1, BB, x_b, "b_mid", 1)
                        yield from narrow_qkv("b", 1, w1qkv_sb, hb, BB + 1, BB)
                        yield "kT"
                        pe.wait_ge(s["b_phi"], 1)
                        pe.wait_ge(s["b_v"], 1)
                        pe.transpose(ps[:, BB, T:T + P], phi[:, 1, 0:P], ident[:, :]).then_inc(s["b_kT"], 1)
                        yield "state"
                        pe.wait_ge(s["b_knat"], 1)
                        pe.matmul(ps[:, BB + 1, :], knat[:, :], vaug[:, 0, :, :].rearrange("p h d -> p (h d)"),
                                  start=True, stop=True).then_inc(s["b_state_mm"], 1)
                        for n in range(H0 // 2 + 1):
                            yield f"lin{2 * n}"
                            if n < H0 // 2:
                                if n == 0:
                                    pe.wait_ge(s["b_stacked"], 16 * len(TERMS))
                                    pe.wait_ge(s["b_state"], 1)
                                else:
                                    pe.wait_ge(s["b_masked"], n)
                                for e in range(2):
                                    for t in range(NT):
                                        mm = pe.matmul(ps[:, BB + 1, e * T + t * P:e * T + (t + 1) * P],
                                                       stack[:, 2 * n + e, 1, t * P:(t + 1) * P],
                                                       stack[:, 2 * n + e, 0, t * P:(t + 1) * P], start=True, stop=True)
                                mm.then_inc(s["b_lin_mm"], 1)
                            if n >= 1:
                                pe.wait_ge(s["b_masked"], n)
                                if n - 1 == H0 // 4:
                                    pe.wait_ge(s["b_att"], 1)
                                for e in range(2):
                                    h = 2 * (n - 1) + e
                                    r, at = head_rows(h)
                                    pe.matmul(ps[r, BB, at:at + P], vaug[:, 0, h, :], masked[:, (n - 1) % 2, e, 0, :],
                                              start=True, stop=True)
                                    pe.matmul(ps[r, BB, at + P:at + T], vaug[:, 1, h, :],
                                              masked[:, (n - 1) % 2, e, 1, :], start=True, stop=False)
                                    mm = pe.matmul(ps[r, BB, at + P:at + T], state[:, h, :], phi[:, 0, P:T],
                                                   start=False, stop=True)
                                mm.then_inc(s["b_lpv_mm"], 1)
                        yield from project("b", w1o_sb, (BB + 1, BB), BB + 1)
                        yield from layer_norm("b", 2, BB, x_bc, "b_done", 1)

                    def c():
                        for l in range(DEPTH):
                            def values(half):
                                if half == 0:
                                    pe.wait_ge(s["c_exp"], LH * (l + 1))
                                pe.wait_ge(s["c_pTsb"], LH * l + 4 * (half + 1))
                                for e in range(4 * half, 4 * half + 4):
                                    d = slice(e * LD, (e + 1) * LD)
                                    r, at = slice(LD * (e % 2), LD * (e % 2) + LD), (e // 2) % 2 * T
                                    pe.matmul(ps[r, BC + half, at:at + P], lv[:, 0, d], lpT[:, e, 0:P],
                                              start=True, stop=True)
                                    pe.matmul(ps[r, BC + half, at + P:at + T], lv[:, 0, d], lpT[:, e, P:2 * P],
                                              start=True, stop=False)
                                    mm = pe.matmul(ps[r, BC + half, at + P:at + T], lv[:, 1, d],
                                                   lpT[:, e, 2 * P:3 * P], start=False, stop=True)
                                mm.then_inc(s["c_o_mm"], 1)

                            for n in range(6):
                                yield f"{l}.q{n}"
                                t, i = n // 3, n % 3
                                if n == 0 and l > 0:
                                    pe.wait_ge(s["c_y"], 2 * l)
                                if n >= 3 and i < 2:
                                    pe.wait_ge(s["c_sq"], 4 * l + i + 1)
                                elif n >= 3:
                                    pe.wait_ge(s["c_v"], 2 * l + 1)
                                pe.matmul(ps[:, BC + i, :], (y if l else y_bc)[:, t * P:(t + 1) * P],
                                          wqkv_sb[:, l, i * INNER:(i + 1) * INNER], start=True, stop=True)\
                                    .then_inc(s["c_qkv_mm"], 1)
                            for n in range(4):
                                yield f"{l}.x{n}"
                                i, half = 1 - n // 2, n % 2
                                pe.wait_ge(s[("c_rn_q", "c_rn_k")[i]], l + 1)
                                if n == 0:
                                    pe.wait_ge(s["c_v"], 2 * (l + 1))
                                    pe.wait_ge(s["c_sq"], 4 * (l + 1))
                                if n == 3:
                                    pe.wait_ge(s["c_Tsb"], 4 * l + 1)
                                for j in range(2):
                                    for t in range(NT):
                                        e = (2 * half + j) * 2
                                        mm = pe.transpose(ps[:, BC + n % 3, j * T + t * P:j * T + (t + 1) * P],
                                                          r1[:, i, t, e:e + 2, :].rearrange("p a d -> p (a d)"),
                                                          ident[:, :])
                                mm.then_inc(s["c_T"], 1)
                            for k in range(LH + 4):
                                yield f"{l}.h{k}"
                                if k == LH + 2:
                                    values(0)
                                if k >= 4:
                                    e = k - 4
                                    pe.wait_ge(s["c_norm"], LH * l + e + 1)
                                    if e == 0:
                                        pe.wait_ge(s["c_Tsb"], 4 * (l + 1))
                                    else:
                                        pe.wait_ge(s["c_pTsb"], LH * l + e)
                                    for c in range(3):
                                        mm = pe.transpose(ps[:, BC + 2, c * P:(c + 1) * P],
                                                          lp[:, e % RING, c * P:(c + 1) * P], ident[:, :])
                                    mm.then_inc(s["c_pT"], 1)
                                if k < LH:
                                    e = k
                                    if e == 0:
                                        pe.wait_ge(s["c_Tsb"], 4 * (l + 1))
                                    if e >= 2:
                                        pe.wait_ge(s["c_exp"], LH * l + e - 1)
                                    o = ps[:, BC + e % 2, 0:SW]
                                    r = slice(64 * (e % 2), 64 * (e % 2) + 64)
                                    pe.matmul(o[:, 0:P], identb[:, :], band[:, 0:P], start=True, stop=False)
                                    pe.matmul(o[:, 0:P], qkT[r, 0, e // 2, 0:P], qkT[r, 1, e // 2, 0:P],
                                              start=False, stop=True)
                                    pe.matmul(o[:, P:SW], identb[:, :], band[:, P:SW], start=True, stop=False)
                                    pe.matmul(o[:, P:SW], qkT[r, 0, e // 2, P:T], qkT[r, 1, e // 2, P - WINDOW:T],
                                              start=False, stop=True).then_inc(s["c_s_mm"], 1)
                            yield f"{l}.o"
                            values(1)
                            yield f"{l}.proj"
                            pe.wait_ge(s["c_oTsb"], 2 * (l + 1))
                            for j in range(4):
                                mm = pe.matmul(ps[:, BC + 2, 0:T], wo_sb[:, l, j, :], loT[:, j, :],
                                               start=(j == 0), stop=(j == 3))
                            mm.then_inc(s["c_proj_mm"], 1)

                            for label in layer_norm("c", l, BC, y, "c_y", 2 * l + 1):
                                yield f"{l}.{label}"
                            for j in range(3):
                                yield f"{l}.up{j}"
                                if j == 0:
                                    pe.wait_ge(s["c_ln_out"], 1 + l)
                                for i in range(2):
                                    at = i * HID + j * P
                                    mm = pe.matmul(ps[0:HT[j], BC + (2, 1, 0)[j], i * T:(i + 1) * T],
                                                   w1_sb[:, l, at:at + HT[j]], hc[:, :], start=True, stop=True)
                                mm.then_inc(s["c_up_mm"], 1)
                            yield f"{l}.down"
                            pe.wait_ge(s["c_ug"], 3 * (l + 1))
                            for j in range(3):
                                mm = pe.matmul(ps[:, BC + 1, 0:T], w2_sb[0:HT[j], l, j, :], ug[0:HT[j], j, :],
                                               start=(j == 0), stop=(j == 2))
                            mm.then_inc(s["c_down_mm"], 1)

                    take_turns(active, {"a": a(), "b": b(), "c": c()})

                @block.scalar
                def _(act):
                    n_link = [0]

                    def link(ins):
                        n_link[0] += 1
                        ins.then_inc(s["act_chain"], 1)
                        act.wait_ge(s["act_chain"], n_link[0])

                    def layer_norm(k, u, dst=None, scale=None, bias=None):
                        yield f"ln{u}.rstd"
                        b = norm[k]
                        act.wait_ge(s[k + "_ln_stat"], u + 1)
                        link(act.activation(b["lnv"][:, :], b["mv"][:, :, 1], ACT.Ln, bias=eps[:, :]))
                        act.activation(b["rstd"][:, :], b["lnv"][:, :], ACT.Exp, scale=-0.5).then_inc(s[k + "_ln_rstd"], 1)
                        if dst is not None:
                            yield f"ln{u}.out"
                            act.wait_ge(s[k + "_ln_feat"], u + 1)
                            act.activation(dst, ps[:, LN_BANK[k], 256:512], ACT.Identity, scale=scale, bias=bias)\
                                .then_inc(s[k + "_ln_out"], 1)

                    def heads_out(k, half, bank):
                        if k == "a":
                            act.wait_ge(s["a_pv_mm"], (half + 1) * H0 // 2)
                        else:
                            act.wait_ge(s["b_lpv_mm"], (half + 1) * H0 // 4)
                        act.activation(narrow[k]["att"][:, 2 * half:2 * half + 2, :].rearrange("p j t -> p (j t)"),
                                       ps[:, bank, :], ACT.Copy).then_inc(s[k + "_att"], 1)

                    def reciprocals(k, banks):
                        for n in range(2):
                            act.wait_ge(s[k + "_att_R"], n + 1)
                            r = narrow[k]["recip"][:, n, :]
                            link(act.activation(r, ps[:, banks[n], :], ACT.Ln, bias=sum_eps[k][:, :]))
                            act.activation(r, r, ACT.Exp, scale=-1.0).then_inc(s[k + "_att_rec"], 1)

                    def a():
                        yield "ln0.stat"
                        act.wait_ge(s["a_m"], 1)
                        yield from layer_norm("a", 0, ha[:, :], m["a"][:, 1:2], m["a"][:, 0:1])
                        yield from layer_norm("a", 1, zn[:, :], V("ln_scale"), V("ln_bias"))
                        yield "part0"
                        act.wait_ge(s["a_qkv_mm"], 1)
                        act.activation(narrow["a"]["part"][:, 0:4:3, :], ps[:, BA + 1, :].rearrange("p (i t) -> p i t", i=2),
                                       ACT.Copy).then_inc(s["a_part0"], 1)
                        yield "nmsb"
                        act.wait_ge(s["a_nm_T"], 1)
                        act.activation(nmT[:, :], psb[0:2 * H0, 0:T], ACT.Copy).then_inc(s["a_nm_sb"], 1)
                        for k in range(H0):
                            yield f"st{k + 1}"
                            if k == H0 // 2 + 2:
                                heads_out("a", 0, BA)
                            act.wait_ge(s["a_st_mm"], k + 1)
                            if k >= 2:
                                act.wait_ge(s["a_pv_mm"], k - 1)
                            act.activation(pT[:, k % 2, :, :].rearrange("p c t -> p (c t)"), ps[:, BA + 1 + k % 2, :],
                                           ACT.Exp).then_inc(s["a_st_exp"], 1)
                        yield "att"
                        heads_out("a", 1, BA)
                        yield "attn"
                        reciprocals("a", (BA + 1, BA + 2))

                    def b():
                        yield "ln0.stat"
                        act.wait_ge(s["b_m"], 1)
                        yield from layer_norm("b", 0, hb[:, :], m["b"][:, 4:5], m["b"][:, 3:4])
                        yield "dexp"
                        act.wait_ge(s["b_lmax"], 1)
                        act.activation(dist[:, :], logit[:, :], ACT.Exp, bias=lmax[:, :]).then_inc(s["b_dexp"], 1)
                        yield "gexp"
                        act.wait_ge(s["b_top"], 2)
                        act.activation(ge[:, 0:NA], top[:, 0:NA], ACT.Exp, bias=ntop[:, :])
                        act.activation(ge[:, NA:NA + 1], ntop[:, :], ACT.Exp).then_inc(s["b_gexp"], 1)
                        yield "fv_sb"
                        act.wait_ge(s["b_fv_mm"], 1)
                        act.activation(fv[:, :, :, :].rearrange("p t k d -> p (t k d)"), ps[:, BB, :], ACT.Copy)\
                            .then_inc(s["b_fv"], 1)
                        def turned(k):
                            act.wait_ge(s["b_fT"], k + 1)
                            act.activation(fpT[:, k, :, :, :].rearrange("p t c q -> p (t c q)"), ps[:, BB + (k + 1) % 2, :],
                                           ACT.Copy).then_inc(s["b_fTsb"], 1)

                        for k in range(NA):
                            if k == 2:
                                yield "f0.4"
                                turned(0)
                                yield "f0.5"
                                turned(1)
                            yield f"f{k // 2}.{2 + k % 2}"
                            act.wait_ge(s["b_fmax"], k + 1)
                            if k >= 2:
                                act.wait_ge(s["b_fT"], k - 1)
                            for t in range(NT):
                                ins = act.activation(fp[:, k % 2, t, :], ps[:, BB + (k + 1) % 2, t * T:(t + 1) * T], ACT.Exp,
                                                     bias=fnm[:, k, t:t + 1], accum_out=fs[:, k, t:t + 1])
                            ins.then_inc(s["b_fexp"], 1)
                        yield "f1.4"
                        turned(2)
                        yield "f1.5"
                        turned(3)
                        yield "foT_sb"
                        act.wait_ge(s["b_fo_mm"], 1)
                        for j in range(2):
                            ins = act.activation(foT[:, j, :], ps[:, BB, j * T:(j + 1) * T], ACT.Identity,
                                                 bias=bvg[:, j:j + 1])
                        ins.then_inc(s["b_foT_sb"], 1)

                        yield from layer_norm("b", 1, hb[:, :], m["b"][:, 7:8], m["b"][:, 6:7])
                        yield "phi1"
                        act.wait_ge(s["b_phi_min"], 1)
                        act.activation(phe[:, :, :], phe[:, :, :], ACT.Exp).then_inc(s["b_phi_exp"], 1)
                        yield "kT"
                        act.wait_ge(s["b_phi"], 1)
                        act.activation(narrow["b"]["part"][:, 0:4:3, :], phi[:, :, :], ACT.Copy).then_inc(s["b_part0"], 1)
                        yield "part1r"
                        act.wait_ge(s["b_kT"], 1)
                        act.activation(knat[:, :], ps[:, BB, T:T + P], ACT.Copy).then_inc(s["b_knat"], 1)
                        yield f"lin{H0 // 2 + 1}"
                        heads_out("b", 0, BB)
                        yield "att"
                        heads_out("b", 1, BB)
                        yield "attn"
                        reciprocals("b", (BB + 1, BB))
                        yield from layer_norm("b", 2)

                    def c():
                        for l in range(DEPTH):
                            for n in range(6):
                                yield f"{l}.q{n + 1}"
                                t, i = n // 3, n % 3
                                act.wait_ge(s["c_qkv_mm"], 6 * l + n + 1)
                                src = ps[:, BC + i, :]
                                if i == 2:
                                    act.activation(lv[:, t, :], src, ACT.Copy).then_inc(s["c_v"], 1)
                                    continue
                                u = 4 * l + 2 * t + i
                                act.activation(qk[:, i, t, :, :].rearrange("p h d -> p (h d)"), src, ACT.Copy)\
                                    .then_inc(s["c_copied"], 1)
                                if u >= 2:
                                    act.wait_ge(s["c_ss"], u - 1 + l)
                                act.activation(sq[:, i, :, :].rearrange("p h d -> p (h d)"), src, ACT.Square)\
                                    .then_inc(s["c_sq"], 1)
                            yield f"{l}.q8"
                            act.wait_ge(s["c_ss"], 5 * (l + 1))
                            link(act.activation(lss[:, :, :, :], ss[:, :, :, :], ACT.Ln, scale=float(2 ** RSTD_SHIFT)))
                            act.activation(rn[:, :, :, :], lss[:, :, :, :], ACT.Exp, scale=-0.5, bias=shift[:, :])\
                                .then_inc(s["c_sumsq"], 1)
                            for k in range(4):
                                yield f"{l}.x{k + 1}"
                                act.wait_ge(s["c_T"], 4 * l + k + 1)
                                act.activation(qkT[:, 1 - k // 2, 2 * (k % 2):2 * (k % 2) + 2, :].rearrange("p j t -> p (j t)"),
                                               ps[:, BC + k % 3, :], ACT.Copy).then_inc(s["c_Tsb"], 1)
                            for k in range(2, LH + 4):
                                yield f"{l}.h{k}"
                                if k < LH + 2:
                                    e = k - 2
                                    act.wait_ge(s["c_max"], LH * l + e + 1)
                                    if e >= RING:
                                        act.wait_ge(s["c_pT"], LH * l + e - RING + 1)
                                    act.activation(lp[:, e % RING, 0:P], ps[:, BC + e % 2, 0:P], ACT.Exp,
                                                   bias=lnm[:, e, 0:1], accum_out=ls[:, e, 0:1])
                                    act.activation(lp[:, e % RING, P + P - WINDOW:PW], ps[:, BC + e % 2, P:SW], ACT.Exp,
                                                   bias=lnm[:, e, 1:2], accum_out=ls[:, e, 1:2]).then_inc(s["c_exp"], 1)
                                if k >= 4:
                                    e = k - 4
                                    act.wait_ge(s["c_pT"], LH * l + e + 1)
                                    act.activation(lpT[:, e, :], ps[:, BC + 2, 0:PW], ACT.Copy).then_inc(s["c_pTsb"], 1)
                            yield f"{l}.oTsb"
                            for j in range(2):
                                act.wait_ge(s["c_o_mm"], 2 * l + j + 1)
                                act.activation(loT[:, 2 * j:2 * j + 2, :].rearrange("p j t -> p (j t)"),
                                               ps[:, BC + j, :], ACT.Copy).then_inc(s["c_oTsb"], 1)
                            for label in layer_norm("c", l):
                                yield f"{l}.{label}"
                            yield f"{l}.gelu"
                            act.preload_act_table_set("gelu_and_others")
                            for j in range(3):
                                act.wait_ge(s["c_up_mm"], 3 * l + j + 1)
                                act.activation(gel[0:HT[j], j, :], ps[0:HT[j], BC + (2, 1, 0)[j], T:2 * T], ACT.Gelu,
                                               bias=V(f"b1g{j}_", l)[0:HT[j], :]).then_inc(s["c_gelu"], 1)
                            act.preload_act_table_set("natural_log_exp_and_others")

                    act.preload_act_table_set("natural_log_exp_and_others")
                    take_turns(active, {"a": a(), "b": b(), "c": c()})

                @block.vector
                def _(dve):
                    n_link = [0]

                    def link(ins):
                        n_link[0] += 1
                        ins.then_inc(s["dve_chain"], 1)
                        dve.wait_ge(s["dve_chain"], n_link[0])

                    def layer_norm(k, u, bank, dst=None, scale=None, bias=None):
                        b = norm[k]
                        yield f"ln{u}.stat"
                        dve.wait_ge(s[k + "_ln_tok"], u + 1)
                        for t in range(NT):
                            ins = dve.bn_stats(b["stats"][:, t, :], ps[:, bank, t * P:(t + 1) * P])
                        link(ins)
                        for t in range(NT):
                            ins = dve.bn_aggr(b["mv"][:, t, :], b["stats"][:, t, :])
                        ins.then_inc(s[k + "_ln_stat"], 1)
                        yield f"ln{u}.norm"
                        dve.wait_ge(s[k + "_ln_rstd"], u + 1)
                        for t in range(NT):
                            ins = dve.tensor_scalar(b["xn"][:, t, :], ps[:, bank, t * P:(t + 1) * P], b["mv"][:, t, 0:1],
                                                    b["rstd"][:, t:t + 1], ALU.subtract, ALU.mult)
                        ins.then_inc(s[k + "_ln_norm"], 1)
                        if scale is None:
                            return
                        yield f"ln{u}.out"
                        dve.wait_ge(s[k + "_ln_feat"], u + 1)
                        if dst is None:
                            if "c" in active:
                                dve.wait_ge(s["c_y"], 1)
                            for r, ty in HALVES:
                                ins = dve.tensor_scalar(y_bc[r, ty], ps[r, bank, 256:512], scale[r, :], bias[r, :],
                                                        ALU.mult, ALU.add)
                            ins.then_inc(s["b_ln_out"], 1)
                        else:
                            dve.tensor_scalar(dst, ps[:, bank, 256:512], scale, bias, ALU.mult, ALU.add)\
                                .then_inc(s[k + "_ln_out"], 1)

                    def modulation(k):
                        yield "in"
                        dve.tensor_copy(m[k][:, :], mod[:, :, bass.ds(seq[k], 1)].rearrange("p a b -> p (a b)"))\
                            .then_inc(s[k + "_m"], 1)
                        dve.wait_ge(s[k + "_m"], 1)

                    def part1r(k, src):
                        dve.wait_ge(s[k + "_part0"], 1)
                        dve.tensor_tensor(narrow[k]["rem"][:, :, :], src, narrow[k]["part"][:, 0:4:3, :], ALU.subtract)\
                            .then_inc(s[k + "_part1_r"], 1)

                    def part2(k):
                        dve.wait_ge(s[k + "_part1"], 1)
                        dve.tensor_tensor(narrow[k]["part"][:, 2:6:3, :], narrow[k]["rem"][:, :, :],
                                          narrow[k]["part"][:, 1:5:3, :], ALU.subtract).then_inc(s[k + "_part2"], 1)

                    def normalise(k):
                        for n in range(2):
                            dve.wait_ge(s[k + "_att_rec"], n + 1)
                            half = narrow[k]["att"][:, 2 * n:2 * n + 2, :].rearrange("p j t -> p (j t)")
                            dve.tensor_tensor(half, half, narrow[k]["recip"][:, n, :], ALU.mult)\
                                .then_inc(s[k + "_att_n"], 1)

                    def a():
                        yield from modulation("a")
                        yield from layer_norm("a", 0, BA)
                        yield from layer_norm("a", 1, BA)
                        yield "part1r"
                        dve.wait_ge(s["a_qkv_mm"], 1)
                        part1r("a", ps[:, BA + 1, :].rearrange("p (i t) -> p i t", i=2))
                        dve.tensor_copy(narrow["a"]["vaug"][:, :, :, 0:HD],
                                        ps[:, BA, 0:T].rearrange("p (t h d) -> p t h d", t=NT, h=H0))\
                            .then_inc(s["a_v"], 1)
                        yield "part2"
                        part2("a")
                        for k in range(H0):
                            yield f"max{k + 1}"
                            dve.wait_ge(s["a_sc_mm"], k + 1)
                            dve.tensor_reduce(nmax[:, k, :], ps[:, BA + 1 + k % 2, :].rearrange("p (t j) -> p t j", t=NT),
                                              AX.X, ALU.max, negate=True).then_inc(s["a_sc_max"], 1)
                        yield "nm"
                        dve.wait_ge(s["a_sc_max"], H0)
                        neg = nmax[:, :, :].rearrange("p h t -> p t h")
                        link(dve.tensor_copy(nmb[:, :, 0, :], neg))
                        dve.tensor_tensor(nmb[:, :, 1, :], neg, nmb[:, :, 0, :], ALU.subtract).then_inc(s["a_nm"], 1)
                        yield "attn"
                        normalise("a")
                        yield "add"
                        dve.wait_ge(s["a_proj_mm"], 1)
                        link(dve.scalar_tensor_tensor(res_a[:, :], ps[:, BA, 0:T], V("b_proj"), ha[:, :],
                                                      ALU.add, ALU.add))
                        if "b" in active:
                            dve.wait_ge(s["b_mid"], 1)
                        dve.scalar_tensor_tensor(x_ab[:, :], res_a[:, :], m["a"][:, 2:3], x_in[:, :], ALU.mult, ALU.add)\
                            .then_inc(s["a_done"], 1)

                    def b():
                        yield from modulation("b")
                        yield from layer_norm("b", 0, BB)
                        yield "hmean"
                        dve.wait_ge(s["b_ln_out"], 1)
                        link(dve.reduce_sum(hsum[:, :], hb[:, :], AX.X))
                        dve.tensor_scalar(hmean[:, :], ones[:, :], hsum[:, :], 1.0 / T, ALU.mult, ALU.mult)\
                            .then_inc(s["b_hmean"], 1)
                        yield "lmax"
                        dve.wait_ge(s["b_route_mm"], 1)
                        link(dve.tensor_tensor(logit[:, :], ps[:, BB + 1, 0:NH], row[:, 0:NH], ALU.add))
                        dve.tensor_reduce(lmax[:, :], logit[:, :], AX.X, ALU.max, negate=True).then_inc(s["b_lmax"], 1)
                        yield "top"
                        dve.wait_ge(s["b_dexp"], 1)
                        link(dve.reduce_sum(dsum[:, :], dist[:, :], AX.X))
                        link(dve.reciprocal(drec[:, :], dsum[:, :]))
                        link(dve.tensor_scalar(dist[:, :], dist[:, :], drec[:, :], None, ALU.mult))
                        link(dve.max(top[:, :], dist[:, :]))
                        dve.max_index(tidx[:, :], top[:, :], dist[:, :]).then_inc(s["b_top"], 1)
                        dve.tensor_scalar(ntop[:, :], top[:, 0:1], -1.0, None, ALU.mult).then_inc(s["b_top"], 1)
                        yield "g"
                        dve.wait_ge(s["b_gexp"], 1)
                        link(dve.reduce_sum(gsum[:, :], ge[:, 0:NA], AX.X))
                        link(dve.scalar_tensor_tensor(gsum[:, :], ge[:, NA:NA + 1], float(NH - NA), gsum[:, :],
                                                      ALU.mult, ALU.add))
                        link(dve.reciprocal(grec[:, :], gsum[:, :]))
                        dve.tensor_scalar(g[:, :], ge[:, 0:NA], grec[:, :], None, ALU.mult).then_inc(s["b_g"], 1)
                        yield "fqk"
                        dve.wait_ge(s["b_g"], 1)
                        dve.wait_ge(s["b_wsel"], 16 * NA)
                        for k in range(NA):
                            r = slice(64 * (k % 2), 64 * (k % 2) + 64)
                            dve.tensor_copy(gp[r, k // 2:k // 2 + 1], g[r, k:k + 1])
                            ins = dve.tensor_copy(bp[r, k // 2, :], wsel[r, k, 3 * DA:WC])
                        link(ins)
                        dve.tensor_scalar(gq[:, :], gp[:, :], float(DA) ** -0.5, None, ALU.mult)
                        link(dve.tensor_tensor(bvg[:, :], bp[:, :, 2], gp[:, :], ALU.mult))
                        yield "fqk_sb"
                        dve.wait_ge(s["b_fqk_mm"], 1)
                        for j in range(2):
                            dve.tensor_scalar(fq[:, j, :], ps[:, BB, j * T:(j + 1) * T], bp[:, j, 0:1], gq[:, j:j + 1],
                                              ALU.add, ALU.mult)
                        for j in range(2):
                            ins = dve.tensor_scalar(fk[:, j, :], ps[:, BB + 1, j * T:(j + 1) * T], bp[:, j, 1:2],
                                                    gp[:, j:j + 1], ALU.add, ALU.mult)
                        ins.then_inc(s["b_fqk"], 1)

                        def f_max(k):
                            dve.wait_ge(s["b_fs_mm"], k + 1)
                            dve.tensor_reduce(fnm[:, k, :], ps[:, BB + (k + 1) % 2, :].rearrange("p (t j) -> p t j", t=NT),
                                              AX.X, ALU.max, negate=True).then_inc(s["b_fmax"], 1)

                        def f_norm(k):
                            dve.wait_ge(s["b_fexp"], k + 1)
                            link(dve.reciprocal(fr[:, k, :], fs[:, k, :]))
                            for t in range(NT):
                                ins = dve.tensor_scalar(fp[:, k % 2, t, :], fp[:, k % 2, t, :], fr[:, k, t:t + 1],
                                                        g[:, k:k + 1], ALU.mult, ALU.mult)
                            ins.then_inc(s["b_fnorm"], 1)

                        for r in range(2):
                            yield f"f{r}.1"
                            f_max(2 * r)
                            yield f"f{r}.2"
                            f_max(2 * r + 1)
                            yield f"f{r}.3"
                            f_norm(2 * r)
                            yield f"f{r}.4"
                            f_norm(2 * r + 1)
                        yield "fadd"
                        dve.wait_ge(s["b_fproj_mm"], 1)
                        link(dve.tensor_scalar(res_b[:, :], ps[:, BB + 1, 0:T], V("bo0"), m["b"][:, 5:6], ALU.add, ALU.mult))
                        dve.tensor_tensor(x_b[:, :], x_ab[:, :], res_b[:, :], ALU.add).then_inc(s["b_mid"], 1)

                        yield from layer_norm("b", 1, BB)
                        yield "phi0"
                        dve.wait_ge(s["b_qkv_mm"], 1)
                        for i, bias in enumerate(("bq1", "bk1")):
                            ins = dve.tensor_scalar(phe[:, i, :], ps[:, BB + 1, i * T:(i + 1) * T], V(bias), 0.0,
                                                    ALU.add, ALU.min)
                        ins.then_inc(s["b_phi_min"], 1)
                        yield "phi1"
                        for i, bias in enumerate(("bq1", "bk1")):
                            ins = dve.tensor_scalar(phi[:, i, :], ps[:, BB + 1, i * T:(i + 1) * T], V(bias), 0.0,
                                                    ALU.add, ALU.max)
                        ins.then_inc(s["b_phi_max"], 1)
                        dve.tensor_tensor(narrow["b"]["vaug"][:, :, :, 0:HD],
                                          ps[:, BB, 0:T].rearrange("p (t h d) -> p t h d", t=NT, h=H0),
                                          row[:, None, NH:NH + P].rearrange("p o (h d) -> p o h d", h=H0)
                                          .broadcast_to([P, NT, H0, HD]), ALU.add).then_inc(s["b_v"], 1)
                        dve.wait_ge(s["b_phi_max"], 1)
                        yield "phi2"
                        dve.wait_ge(s["b_phi_exp"], 1)
                        dve.tensor_tensor(phi[:, :, :], phi[:, :, :], phe[:, :, :], ALU.add).then_inc(s["b_phi"], 1)
                        yield "part1r"
                        dve.wait_ge(s["b_phi"], 1)
                        part1r("b", phi[:, :, :])
                        yield "part2"
                        part2("b")
                        yield "state"
                        dve.wait_ge(s["b_state_mm"], 1)
                        dve.tensor_tensor(state[:, :, :].rearrange("p h d -> p (h d)"), ps[:, BB + 1, :], diag[:, :], ALU.mult)\
                            .then_inc(s["b_state"], 1)
                        for k in range(H0 // 2):
                            yield f"lin{2 * k + 1}"
                            dve.wait_ge(s["b_lin_mm"], k + 1)
                            if k >= 2:
                                dve.wait_ge(s["b_lpv_mm"], k - 1)
                            dve.tensor_tensor(masked[:, k % 2, :, :, :].rearrange("p e t q -> p (e t) q"),
                                              ps[:, BB + 1, :].rearrange("p (c q) -> p c q", q=P),
                                              tri[:, None, :].broadcast_to([P, 4, P]), ALU.mult).then_inc(s["b_masked"], 1)
                        yield "attn"
                        normalise("b")
                        yield "add"
                        dve.wait_ge(s["b_proj_mm"], 1)
                        link(dve.tensor_scalar(res_b[:, :], ps[:, BB + 1, 0:T], V("bo1"), m["b"][:, 8:9], ALU.add, ALU.mult))
                        if "c" in active:
                            dve.wait_ge(s["c_x"], 1)
                        dve.tensor_tensor(x_bc[:, :], x_b[:, :], res_b[:, :], ALU.add).then_inc(s["b_done"], 1)
                        yield from layer_norm("b", 2, BB, None, m["b"][:, 10:11], m["b"][:, 9:10])

                    def c():
                        yield from modulation("c")
                        for l in range(DEPTH):
                            def add_k(t):
                                dve.wait_ge(s["c_t1"], 4 * l + 2 * t + 2)
                                dve.wait_ge(s["c_r2"], 4 * l + 2 * t + 2)
                                dve.tensor_tensor(r1[:, 1, t, :, :], r1[:, 1, t, :, :], r2[:, 1, :, :], ALU.add)\
                                    .then_inc(s["c_rot_k"], 1)

                            for n, (t, i) in enumerate((t, i) for t in range(NT) for i in range(2)):
                                yield f"{l}.q{(2, 3, 5, 6)[n]}"
                                u = 4 * l + n
                                dve.wait_ge(s["c_sq"], u + 1)
                                dve.tensor_tensor(r1[:, i, t, :, :], qk[:, i, t, :, :],
                                                  wave[:, l, 2 * i, t, None, :].broadcast_to([P, LH, LD]), ALU.mult)\
                                    .then_inc(s["c_t1"], 1)
                                dve.reduce_sum(ss[:, i, t, :], sq[:, i, :, :], AX.X).then_inc(s["c_ss"], 1)
                                if n == 2:
                                    add_k(0)
                            yield f"{l}.q7"
                            dve.wait_ge(s["c_ss"], 5 * l + 4)
                            dve.tensor_scalar(ss[:, :, :, :], ss[:, :, :, :], 1e-24, None, ALU.max).then_inc(s["c_ss"], 1)
                            yield f"{l}.q8"
                            add_k(1)
                            yield f"{l}.q10"
                            dve.wait_ge(s["c_sumsq"], l + 1)
                            dve.wait_ge(s["c_rot_k"], 2 * (l + 1))
                            dve.tensor_tensor(r1[:, 1, :, :, :], r1[:, 1, :, :, :],
                                              rn[:, 1, :, :, None].broadcast_to([P, NT, LH, LD]), ALU.mult)\
                                .then_inc(s["c_rn_k"], 1)
                            for k in range(1, LH + 3):
                                yield f"{l}.h{k}"
                                if k < LH + 1:
                                    e = k - 1
                                    dve.wait_ge(s["c_s_mm"], LH * l + e + 1)
                                    dve.tensor_reduce(lnm[:, e, 0:1], ps[:, BC + e % 2, 0:P], AX.X, ALU.max, negate=True)
                                    dve.tensor_reduce(lnm[:, e, 1:2], ps[:, BC + e % 2, P:SW], AX.X, ALU.max, negate=True)\
                                        .then_inc(s["c_max"], 1)
                                if 3 <= k < LH + 3:
                                    e = k - 3
                                    dve.wait_ge(s["c_exp"], LH * l + e + 1)
                                    link(dve.reciprocal(lr[:, e, :], ls[:, e, :]))
                                    p0, p1 = lp[:, e % RING, 0:P], lp[:, e % RING, P + P - WINDOW:PW]
                                    dve.tensor_scalar(p0, p0, lr[:, e, 0:1], None, ALU.mult)
                                    dve.tensor_scalar(p1, p1, lr[:, e, 1:2], None, ALU.mult).then_inc(s["c_norm"], 1)
                            yield f"{l}.y"
                            dve.wait_ge(s["c_proj_mm"], l + 1)
                            if l > 0:
                                dve.wait_ge(s["c_y"], 2 * l)
                            for r, ty in HALVES:
                                ins = dve.tensor_tensor(y[r, ty], (y if l else y_bc)[r, ty], ps[r, BC + 2, 0:T], ALU.add)
                            ins.then_inc(s["c_y"], 1)
                            for label in layer_norm("c", l, BC, hc[:, :], V("ln_g", l), V("ln_b", l)):
                                yield f"{l}.{label}"
                            yield f"{l}.ug"
                            for j in range(3):
                                dve.wait_ge(s["c_gelu"], 3 * l + j + 1)
                                dve.scalar_tensor_tensor(ug[0:HT[j], j, :], ps[0:HT[j], BC + (2, 1, 0)[j], 0:T],
                                                         V(f"b1a{j}_", l)[0:HT[j], :], gel[0:HT[j], j, :],
                                                         ALU.add, ALU.mult).then_inc(s["c_ug"], 1)
                            yield f"{l}.add"
                            dve.wait_ge(s["c_down_mm"], l + 1)
                            dve.wait_ge(s["c_y"], 2 * l + 1)
                            for r, ty in HALVES:
                                ins = dve.scalar_tensor_tensor(y[r, ty], ps[r, BC + 1, 0:T], V("b2_", l)[r, :], y[r, ty],
                                                               ALU.add, ALU.add)
                            ins.then_inc(s["c_y"], 1)
                        yield "done"
                        dve.wait_ge(s["c_y"], 2 * DEPTH)
                        dve.wait_ge(s["c_x"], 1)
                        for r, ty in HALVES:
                            ins = dve.scalar_tensor_tensor(x_c[r, :], y[r, ty], m["c"][r, 11:12], x_c[r, :],
                                                           ALU.mult, ALU.add)
                        ins.then_inc(s["c_done"], 1)

                    take_turns(active, {"a": a(), "b": b(), "c": c()})

            nc.all_engine_barrier(sems_to_clear=loop_sems)

        turn({"a": 0})
        turn({"a": 1, "b": 0})
        turn({"a": 2, "b": 1, "c": 0})
        with nc.Fori(3, NB) as n:
            turn({"a": n, "b": n - 1, "c": n - 2, "out": n - 3})
        turn({"b": NB - 1, "c": NB - 2, "out": NB - 3})
        turn({"c": NB - 1, "out": NB - 2})
        with nc.Block() as block:
            @block.sync
            def _(sp):
                store(sp, NB - 1, last_stored)
                sp.wait_ge(last_stored, 16)


def layout(inputs):
    import numpy as np
    f = np.float32
    A = {k: np.asarray(v) for k, v in inputs.items()}
    a = {}
    a["z"] = A["L0_attn_z"].transpose(0, 2, 1)
    a["cT"] = np.stack([A["L0_c"].T, A["L1_c"].T], 1)
    a["wmod"] = np.stack([A["L0_wmod"], A["L1_wmod"]], 1)
    w = A["L0_attn_w_qkv"].reshape(P, H0, HD, 3)
    dh = lambda u: u.transpose(0, 2, 1).reshape(u.shape[0], P)
    a["w0qkv"] = np.concatenate([dh(w[..., 0]), dh(w[..., 1]), w[..., 2].reshape(P, P)], 1)

    def by_groups(u):
        r = np.zeros((4, GR, H0 // 4, P), f)
        r[:, 0:HD] = u.reshape(H0 // 4, 4, HD, P).transpose(1, 2, 0, 3)
        return r.reshape(P, H0 // 4, P)

    a["w0proj"] = by_groups(A["L0_attn_w_proj"])
    a["wr"] = A["L0_ffn_Wr"]
    pk = [A["L0_ffn_" + n].reshape(P, NH, DA).transpose(1, 0, 2) for n in ("Wq", "Wk", "Wv")]
    pb = [np.concatenate([A["L0_ffn_" + n].reshape(NH, DA, 1)] * 2, 1) for n in ("bq", "bk", "bv")]
    a["wpack"] = np.concatenate(pk + pb, 2)
    a["wo0"] = A["L0_ffn_Wo"]
    a["w1qkv"] = np.concatenate([dh(A["L1_attn_Wq"].T.reshape(P, H0, HD)), dh(A["L1_attn_Wk"].T.reshape(P, H0, HD)),
                                 A["L1_attn_Wv"].T], 1)
    a["w1o"] = by_groups(A["L1_attn_Wo"].T)
    a["wqkv"], a["wo"], a["w1"], a["w2"] = (A["L1_ffn_" + n] for n in ("wqkv", "wo", "w1", "w2"))
    pad = lambda u: np.concatenate([u, np.zeros(3 * P - HID, f)]).reshape(3, P)
    col = {"ln_scale": A["L0_attn_ln_scale"], "ln_bias": A["L0_attn_ln_bias"], "b_proj": A["L0_attn_b_proj"],
           "bo0": A["L0_ffn_bo"], "bo1": A["L1_attn_bo"],
           "bq1": A["L1_attn_bq"].reshape(H0, HD).T.reshape(P), "bk1": A["L1_attn_bk"].reshape(H0, HD).T.reshape(P)}
    for l in range(DEPTH):
        col[f"ln_g{l}"], col[f"ln_b{l}"], col[f"b2_{l}"] = A["L1_ffn_ln_g"][l], A["L1_ffn_ln_b"][l], A["L1_ffn_b2"][l]
        for j in range(3):
            col[f"b1a{j}_{l}"] = pad(A["L1_ffn_b1"][l][:HID])[j]
            col[f"b1g{j}_{l}"] = pad(A["L1_ffn_b1"][l][HID:])[j]
    a["vecs"] = np.stack([col[n] for n in VEC], 1)
    swap = lambda u: np.concatenate([u[LD // 2:], u[:LD // 2]])
    flat = [A["L0_ffn_br"], A["L1_attn_bv"]]
    for l in range(DEPTH):
        q, k = A["L1_ffn_q_scale"][l], A["L1_ffn_k_scale"][l]
        flat += [q, swap(q), k, swap(k)]
    a["rows"] = np.broadcast_to(np.concatenate(flat)[None], (P, ROWS))
    a["ident_in"] = np.eye(P, dtype=f)
    i = np.arange(P)
    a["tri_in"] = (i[None, :] >= i[:, None]).astype(f)
    a["diag_in"] = np.repeat((i[:, None] % H0 == np.arange(H0)[None, :]), GR, 1).astype(f)
    a["sumrow_in"] = (i[:, None] == i[None, :] // GR * GR + HD).astype(f)
    c = np.arange(P + WINDOW)
    t0 = (i[None, :] > i[:, None]) | (i[:, None] > i[None, :] + WINDOW)
    t1 = (c[None, :] > i[:, None] + WINDOW) | (c[None, :] < i[:, None])
    a["band_in"] = (np.concatenate([t0, t1], 1) * NEG).astype(f)
    half = np.arange(0, LD, 2, dtype=f)
    inv = (f(1) / f(10000) ** (half / f(LD))).astype(f)
    t = np.arange(T, dtype=f)
    fr = np.concatenate([t[:, None] * inv[None]] * 2, 1)
    base = (half + f(0.4 * LD)) / f(1.4 * LD)
    sc = np.concatenate([base[None] ** ((t - T // 2) / f(WINDOW // 2))[:, None]] * 2, 1)
    sg = np.where(np.arange(LD) < LD // 2, -1, 1).astype(f)[None]
    tabs = np.stack([np.cos(fr) * sc, np.sin(fr) * sg * sc, np.cos(fr) / sc, np.sin(fr) * sg / sc]).astype(f)
    a["rot_in"] = tabs.reshape(4, NT, P, LD).transpose(2, 0, 1, 3)
    return {k: np.ascontiguousarray(v, dtype=f) for k, v in a.items()}


_IN = ["z", "cT", "wmod", "w0qkv", "w0proj", "wr", "wpack", "wo0", "w1qkv", "w1o", "wqkv", "wo", "w1", "w2",
       "vecs", "rows", "ident_in", "tri_in", "diag_in", "sumrow_in", "band_in", "rot_in"]


def kernel(**inputs):
    import numpy as np
    import concourse.bacc as bacc
    from concourse.bass_utils import run_bass_kernel_spmd

    arrays = layout(inputs)
    nc = bacc.Bacc("TRN2", target_bir_lowering=False, num_devices=1)
    args = [nc.dram_tensor(n, arrays[n].shape, F32, kind="ExternalInput").ap() for n in _IN]
    out = nc.dram_tensor("out", (NB, P, T), F32, kind="ExternalOutput").ap()
    program(nc, *args, out)
    r = run_bass_kernel_spmd(nc, [arrays], core_ids=[0])
    return np.ascontiguousarray(r.results[0]["out"].transpose(0, 2, 1))
```
